# Optimizing a Trainium2 kernel written in Bass

```python
import numpy as np
import jax
import jax.numpy as jnp

def _softmax(x, axis=-1):
    return jax.nn.softmax(x, axis=axis)

def _gelu(x):
    return jax.nn.gelu(x, approximate=True)

def _silu(x):
    return jax.nn.silu(x)

def _sigmoid(x):
    return jax.nn.sigmoid(x)

def _layernorm(x, axis=-1, eps=1e-05):
    m = jnp.mean(x, axis=axis, keepdims=True)
    v = jnp.var(x, axis=axis, keepdims=True)
    return (x - m) / jnp.sqrt(v + eps)

def _scatter_add(tgt, idx, src, axis=0):
    return tgt.at[idx].add(src)

def _segment_sum(src, seg, n):
    return jax.ops.segment_sum(src, seg, n)
kernel_name = 'mk_perceiver_d4_seqx_r4_a3782a'

def setup_inputs(seed: int=0):
    np.random.seed(seed)
    _w = jnp.asarray

    def _rec_inputs():
        import jax
        import jax.numpy as jnp
        _rk = jax.random.key(seed)
        x = 7.22e-05 + 1 * jax.random.normal(jax.random.fold_in(_rk, 1), (2, 256, 256), jnp.float32)
        _lenS = 256 - jax.random.randint(jax.random.fold_in(_rk, 7), (2,), 0, max(1, 256 // 4) + 1, jnp.int32)
        _lenS2 = 4096 - jax.random.randint(jax.random.fold_in(_rk, 8), (2,), 0, max(1, 4096 // 4) + 1, jnp.int32)
        _ctx_1024P = jax.random.normal(jax.random.fold_in(_rk, 11), (2, 16, 256), jnp.float32)
        _ctx_1024c = jax.random.dirichlet(jax.random.fold_in(_rk, 511), 0.3 * jnp.ones((16,), jnp.float32), (2, 4096))
        _ctx_1024t = jnp.einsum('bsk,bkd->bsd', _ctx_1024c, _ctx_1024P)
        _ctx_1024t = _ctx_1024t * jax.lax.rsqrt(jnp.mean(jnp.square(_ctx_1024t)) + 1e-12) * 0.953939
        ctx_1024 = 2.81802e-05 + 1.00001 * (_ctx_1024t + 0.3 * jax.random.normal(jax.random.fold_in(_rk, 611), (2, 4096, 256), jnp.float32))
        _validS = jnp.arange(256)[None, :] < _lenS[:, None]
        _validS2 = jnp.arange(4096)[None, :] < _lenS2[:, None]
        _causal = jnp.tril(jnp.ones((256, 256), dtype=bool))
        mask_BxS2_bk0 = jnp.logical_not(jnp.broadcast_to(_validS2[:, :], (2, 4096)))
        mask_BxS2_ik0 = jnp.where(jnp.broadcast_to(_validS2[:, :], (2, 4096)), 0, 1).astype(jnp.int32)
        return (x, ctx_1024, mask_BxS2_bk0, mask_BxS2_ik0)
    x, ctx_1024, mask_BxS2_bk0, mask_BxS2_ik0 = _rec_inputs()

    def _L0_xattn_setup():
        import jax, jax.numpy as jnp
        import numpy as np
        B, LQ, LKV = (8, 256, 512)
        QDIM, KDIM, HID = (256, 256, 256)
        key = jax.random.key(seed)
        ks = jax.random.split(key, 12)
        s = lambda d: 1.0 / np.sqrt(d)
        return {'query': jax.random.normal(ks[0], (B, LQ, QDIM), jnp.float32), 'key_value': jax.random.normal(ks[1], (B, LKV, KDIM), jnp.float32), 'key_mask': jax.random.randint(ks[2], (B, LKV), 0, 2).astype(bool), 'Wq': jax.random.uniform(ks[3], (QDIM, HID), jnp.float32, -s(QDIM), s(QDIM)), 'bq': jax.random.uniform(ks[4], (HID,), jnp.float32, -s(QDIM), s(QDIM)), 'Wk': jax.random.uniform(ks[5], (KDIM, HID), jnp.float32, -s(KDIM), s(KDIM)), 'bk': jax.random.uniform(ks[6], (HID,), jnp.float32, -s(KDIM), s(KDIM)), 'Wv': jax.random.uniform(ks[7], (KDIM, HID), jnp.float32, -s(KDIM), s(KDIM)), 'bv': jax.random.uniform(ks[8], (HID,), jnp.float32, -s(KDIM), s(KDIM)), 'Wo': jax.random.uniform(ks[9], (HID, QDIM), jnp.float32, -s(HID), s(HID)), 'bo': jax.random.uniform(ks[10], (QDIM,), jnp.float32, -s(HID), s(HID))}
    _L0_xattn_all = _L0_xattn_setup()
    _L0_xattn_in = {k: v for k, v in _L0_xattn_all.items() if k in ('Wq', 'bq', 'Wk', 'bk', 'Wv', 'bv', 'Wo', 'bo')}
    del _L0_xattn_all

    def _L0_attn_setup():
        import jax, jax.numpy as jnp
        import numpy as np
        DIM = 256
        HEADS = 16
        HIDDEN = 512
        EPS = 1e-06

        def _rmsnorm(x, scale):
            norm = jnp.linalg.norm(x, axis=-1, keepdims=True)
            return x * (scale * (x.shape[-1] ** 0.5 + EPS) / norm)
        key = jax.random.key(seed)
        ks = jax.random.split(key, 8)
        B, N, C = (4, 1024, DIM)
        s = 0.02
        return {'x': jax.random.normal(ks[0], (B, N, C), dtype=jnp.float32), 'scale1': jnp.ones((C,), jnp.float32), 'scale2': jnp.ones((C,), jnp.float32), 'gamma': jnp.ones((C,), jnp.float32), 'qkv_w': jax.random.normal(ks[1], (3 * C, C), jnp.float32) * s, 'proj_w': jax.random.normal(ks[2], (C, C), jnp.float32) * s, 'proj_b': jnp.zeros((C,), jnp.float32), 'conv1_w': jax.random.normal(ks[3], (HIDDEN, C), jnp.float32) * s, 'conv1_b': jnp.zeros((HIDDEN,), jnp.float32), 'conv2_w': jax.random.normal(ks[4], (C, HIDDEN), jnp.float32) * s, 'conv2_b': jnp.zeros((C,), jnp.float32)}
    _L0_attn_all = _L0_attn_setup()
    _L0_attn_in = {k: v for k, v in _L0_attn_all.items() if k in ('scale1', 'scale2', 'gamma', 'qkv_w', 'proj_w', 'proj_b', 'conv1_w', 'conv1_b', 'conv2_w', 'conv2_b')}
    del _L0_attn_all

    def _L0_ffn_setup():
        import jax, jax.numpy as jnp
        import numpy as np
        D_IN, D_HID = (256, 1024)

        def _ternary(key, shape):
            return jax.random.randint(key, shape, -1, 2).astype(jnp.float32)

        def _tlin(x, w, s):
            return jnp.einsum('bsi,oi->bso', x, w) * s
        key = jax.random.key(seed)
        ks = jax.random.split(key, 12)
        inv = lambda fan: 1.0 / np.sqrt(fan).astype(np.float32)
        return {'x': jax.random.normal(ks[0], (4, 512, D_IN), dtype=jnp.float32), 'w1_w': _ternary(ks[1], (D_HID, D_IN)), 'w1_s': jax.random.uniform(ks[2], (D_HID,), dtype=jnp.float32) * inv(D_IN), 'w2_w': _ternary(ks[3], (D_HID, D_IN)), 'w2_s': jax.random.uniform(ks[4], (D_HID,), dtype=jnp.float32) * inv(D_IN), 'h1_w': _ternary(ks[5], (D_HID, D_HID)), 'h1_s': jax.random.uniform(ks[6], (D_HID,), dtype=jnp.float32) * inv(D_HID), 'h2_w': _ternary(ks[7], (D_HID, D_HID)), 'h2_s': jax.random.uniform(ks[8], (D_HID,), dtype=jnp.float32) * inv(D_HID), 'w3_w': _ternary(ks[9], (D_IN, D_HID)), 'w3_s': jax.random.uniform(ks[10], (D_IN,), dtype=jnp.float32) * inv(D_HID)}
    _L0_ffn_all = _L0_ffn_setup()
    _L0_ffn_in = {k: v for k, v in _L0_ffn_all.items() if k in ('w1_w', 'w1_s', 'w2_w', 'w2_s', 'h1_w', 'h1_s', 'h2_w', 'h2_s', 'w3_w', 'w3_s')}
    del _L0_ffn_all

    def _L1_xattn_setup():
        import jax, jax.numpy as jnp
        import numpy as np
        D = 256
        key = jax.random.key(seed)
        ks = jax.random.split(key, 9)
        B, Nq, Nk = (8, 512, 512)
        s = 1.0 / np.sqrt(D)
        return {'query': jax.random.normal(ks[0], (B, Nq, D), jnp.float32), 'key': jax.random.normal(ks[1], (B, Nk, D), jnp.float32), 'value': jax.random.normal(ks[2], (B, Nk, D), jnp.float32), 'Wq': jax.random.uniform(ks[3], (D, D), jnp.float32, -s, s), 'bq': jax.random.uniform(ks[4], (D,), jnp.float32, -s, s), 'Wk': jax.random.uniform(ks[5], (D, D), jnp.float32, -s, s), 'bk': jax.random.uniform(ks[6], (D,), jnp.float32, -s, s), 'Wv': jax.random.uniform(ks[7], (D, D), jnp.float32, -s, s), 'bv': jax.random.uniform(ks[8], (D,), jnp.float32, -s, s)}
    _L1_xattn_all = _L1_xattn_setup()
    _L1_xattn_in = {k: v for k, v in _L1_xattn_all.items() if k in ('Wq', 'bq', 'Wk', 'bk', 'Wv', 'bv')}
    del _L1_xattn_all

    def _L1_attn_setup():
        import jax, jax.numpy as jnp
        import numpy as np
        B, S, C = (32, 256, 256)
        key = jax.random.key(seed)
        ks = jax.random.split(key, 4)
        scale = 1.0 / np.sqrt(C)
        x = jax.random.normal(ks[0], (B, S, C), dtype=jnp.float32)
        Wq = jax.random.normal(ks[1], (C, C), dtype=jnp.float32) * scale
        Wk = jax.random.normal(ks[2], (C, C), dtype=jnp.float32) * scale
        Wv = jax.random.normal(ks[3], (C, C), dtype=jnp.float32) * scale
        gamma = jnp.zeros((1,), dtype=jnp.float32)
        return {'x': x, 'Wq': Wq, 'Wk': Wk, 'Wv': Wv, 'gamma': gamma}
    _L1_attn_all = _L1_attn_setup()
    _L1_attn_in = {k: v for k, v in _L1_attn_all.items() if k in ('Wq', 'Wk', 'Wv', 'gamma')}
    del _L1_attn_all

    def _L1_ffn_setup():
        import jax, jax.numpy as jnp
        import numpy as np
        B, S, H, I, E = (2, 1024, 256, 128, 8)
        key = jax.random.key(seed)
        ks = jax.random.split(key, 5)
        scale_h = 1.0 / np.sqrt(H)
        scale_i = 1.0 / np.sqrt(I)
        return {'hidden_states': jax.random.normal(ks[0], (B, S, H), dtype=jnp.float32), 'gate_w': jax.random.normal(ks[1], (E, H), dtype=jnp.float32) * scale_h, 'w_gate': jax.random.normal(ks[2], (E, I, H), dtype=jnp.float32) * scale_h, 'w_up': jax.random.normal(ks[3], (E, I, H), dtype=jnp.float32) * scale_h, 'w_down': jax.random.normal(ks[4], (E, H, I), dtype=jnp.float32) * scale_i}
    _L1_ffn_all = _L1_ffn_setup()
    _L1_ffn_in = {k: v for k, v in _L1_ffn_all.items() if k in ('gate_w', 'w_gate', 'w_up', 'w_down')}
    del _L1_ffn_all

    def _L2_xattn_setup():
        import jax, jax.numpy as jnp
        import numpy as np
        B, SQ, SK, D, H = (4, 512, 512, 256, 16)
        SCALE = (D / H) ** 0.5
        key = jax.random.key(seed)
        ks = jax.random.split(key, 8)
        s = 1.0 / np.sqrt(D)
        return {'x1': jax.random.normal(ks[0], (B, SQ, D), dtype=jnp.float32), 'x2': jax.random.normal(ks[1], (B, SK, D), dtype=jnp.float32), 'Wq': jax.random.uniform(ks[2], (D, D), jnp.float32, -s, s), 'bq': jax.random.uniform(ks[3], (D,), jnp.float32, -s, s), 'Wk': jax.random.uniform(ks[4], (D, D), jnp.float32, -s, s), 'bk': jax.random.uniform(ks[5], (D,), jnp.float32, -s, s), 'Wv': jax.random.uniform(ks[6], (D, D), jnp.float32, -s, s), 'bv': jax.random.uniform(ks[7], (D,), jnp.float32, -s, s)}
    _L2_xattn_all = _L2_xattn_setup()
    _L2_xattn_in = {k: v for k, v in _L2_xattn_all.items() if k in ('Wq', 'bq', 'Wk', 'bk', 'Wv', 'bv')}
    del _L2_xattn_all

    def _L2_attn_setup():
        import jax, jax.numpy as jnp
        import numpy as np
        NUM_HEADS = 16
        key = jax.random.key(seed)
        k1, k2, k3, k4 = jax.random.split(key, 4)
        d_model = 256
        B, S = (4, 512)
        scale = 1.0 / np.sqrt(d_model)
        x = jax.random.normal(k1, (B, S, d_model), dtype=jnp.float32)
        W_k = jax.random.normal(k2, (d_model, d_model), dtype=jnp.float32) * scale
        W_v = jax.random.normal(k3, (d_model, d_model), dtype=jnp.float32) * scale
        W_o = jax.random.normal(k4, (d_model, d_model), dtype=jnp.float32) * scale
        return {'x': x, 'W_k': W_k, 'W_v': W_v, 'W_o': W_o}
    _L2_attn_all = _L2_attn_setup()
    _L2_attn_in = {k: v for k, v in _L2_attn_all.items() if k in ('W_k', 'W_v', 'W_o')}
    del _L2_attn_all

    def _L2_ffn_setup():
        import jax, jax.numpy as jnp
        import numpy as np
        BEST_K = 2

        def _expert(xf, w1, w3, w2):
            return jax.nn.silu(xf @ w1) * (xf @ w3) @ w2
        key = jax.random.key(seed)
        ks = jax.random.split(key, 9)
        E, S_sh, D, H = (8, 2, 256, 128)
        B, S = (2, 512)
        w = lambda k, shape: jax.random.normal(k, shape, dtype=jnp.float32) * 0.02
        return {'x': jax.random.normal(ks[0], (B, S, D), dtype=jnp.float32), 'router_w': w(ks[1], (D, E)), 'router_b': jnp.zeros((E,), dtype=jnp.float32), 'routed_w1': w(ks[2], (E, D, H)), 'routed_w3': w(ks[3], (E, D, H)), 'routed_w2': w(ks[4], (E, H, D)), 'shared_w1': w(ks[5], (S_sh, D, H)), 'shared_w3': w(ks[6], (S_sh, D, H)), 'shared_w2': w(ks[7], (S_sh, H, D))}
    _L2_ffn_all = _L2_ffn_setup()
    _L2_ffn_in = {k: v for k, v in _L2_ffn_all.items() if k in ('router_w', 'router_b', 'routed_w1', 'routed_w3', 'routed_w2', 'shared_w1', 'shared_w3', 'shared_w2')}
    del _L2_ffn_all

    def _L3_xattn_setup():
        import jax, jax.numpy as jnp
        import numpy as np
        B, LQ, LK, D = (4, 512, 512, 256)
        H = 16
        HD = D // H

        def _split_heads(x):
            b, l, _ = x.shape
            return x.reshape(b, l, H, HD).transpose(0, 2, 1, 3)
        key = jax.random.key(seed)
        ks = jax.random.split(key, 10)
        s = 0.02
        return {'hidden_states': jax.random.normal(ks[0], (B, LQ, D), jnp.float32), 'context': jax.random.normal(ks[1], (B, LK, D), jnp.float32), 'attention_mask': jax.random.randint(ks[2], (B, LK), 0, 2, jnp.int32), 'q_w': jax.random.normal(ks[3], (D, D), jnp.float32) * s, 'q_b': jnp.zeros((D,), jnp.float32), 'k_w': jax.random.normal(ks[4], (D, D), jnp.float32) * s, 'k_b': jnp.zeros((D,), jnp.float32), 'v_w': jax.random.normal(ks[5], (D, D), jnp.float32) * s, 'v_b': jnp.zeros((D,), jnp.float32)}
    _L3_xattn_all = _L3_xattn_setup()
    _L3_xattn_in = {k: v for k, v in _L3_xattn_all.items() if k in ('q_w', 'q_b', 'k_w', 'k_b', 'v_w', 'v_b')}
    del _L3_xattn_all

    def _L3_attn_setup():
        import jax, jax.numpy as jnp
        import numpy as np
        D_MODEL = 256
        NUM_HEADS = 4
        EXPAND_K = 1.0
        EXPAND_V = 2.0
        KEY_DIM = int(D_MODEL * EXPAND_K)
        VALUE_DIM = int(D_MODEL * EXPAND_V)
        HEAD_K = KEY_DIM // NUM_HEADS
        HEAD_V = VALUE_DIM // NUM_HEADS
        CHUNK = 64
        EPS = 1e-05
        ROPE_BASE = 10000.0

        def _apply_rotary(q, k):
            d = q.shape[-1]
            half = d // 2
            inv_freq = 1.0 / ROPE_BASE ** (jnp.arange(0, d, 2, dtype=jnp.float32) / d)
            t = jnp.arange(q.shape[1], dtype=jnp.float32)
            freqs = t[:, None] * inv_freq[None, :]
            cos = jnp.cos(freqs)[None, :, None, :]
            sin = jnp.sin(freqs)[None, :, None, :]

            def rot(x):
                x1, x2 = (x[..., :half], x[..., half:])
                return jnp.concatenate([x1 * cos - x2 * sin, x2 * cos + x1 * sin], axis=-1)
            return (rot(q), rot(k))

        def _chunk_retention(q, k, v, gamma):
            B, T, H, dk = q.shape
            dv = v.shape[-1]
            C = CHUNK
            N = T // C
            qc = q.reshape(B, N, C, H, dk).transpose(1, 0, 3, 2, 4)
            kc = k.reshape(B, N, C, H, dk).transpose(1, 0, 3, 2, 4)
            vc = v.reshape(B, N, C, H, dv).transpose(1, 0, 3, 2, 4)
            i = jnp.arange(C, dtype=jnp.float32)
            cross_dec = gamma[:, None] ** (i + 1.0)
            k_dec = gamma[:, None] ** (C - 1.0 - i)
            diff = i[:, None] - i[None, :]
            mask = jnp.where(diff >= 0, gamma[:, None, None] ** diff, 0.0)
            gC = gamma ** C

            def step(S, inp):
                qb, kb, vb = inp
                attn = jnp.einsum('bhid,bhjd->bhij', qb, kb) * mask
                o_intra = jnp.einsum('bhij,bhjv->bhiv', attn, vb)
                o_inter = jnp.einsum('bhid,bhdv->bhiv', qb * cross_dec[:, :, None], S)
                S_new = gC[:, None, None] * S + jnp.einsum('bhjd,bhjv->bhdv', kb * k_dec[:, :, None], vb)
                return (S_new, o_intra + o_inter)
            S0 = jnp.zeros((B, H, dk, dv), dtype=q.dtype)
            _, o = jax.lax.scan(step, S0, (qc, kc, vc))
            return o.transpose(1, 0, 3, 2, 4).reshape(B, T, H, dv)
        key = jax.random.key(seed)
        ks = jax.random.split(key, 7)
        B, T = (4, 512)
        s = 0.02
        return {'x': jax.random.normal(ks[0], (B, T, D_MODEL), dtype=jnp.float32), 'Wq': jax.random.normal(ks[1], (KEY_DIM, D_MODEL), dtype=jnp.float32) * s, 'Wk': jax.random.normal(ks[2], (KEY_DIM, D_MODEL), dtype=jnp.float32) * s, 'Wv': jax.random.normal(ks[3], (VALUE_DIM, D_MODEL), dtype=jnp.float32) * s, 'Wg': jax.random.normal(ks[4], (VALUE_DIM, D_MODEL), dtype=jnp.float32) * s, 'Wo': jax.random.normal(ks[5], (D_MODEL, VALUE_DIM), dtype=jnp.float32) * s, 'gnorm_w': jnp.ones((HEAD_V,), dtype=jnp.float32)}
    _L3_attn_all = _L3_attn_setup()
    _L3_attn_in = {k: v for k, v in _L3_attn_all.items() if k in ('Wq', 'Wk', 'Wv', 'Wg', 'Wo', 'gnorm_w')}
    del _L3_attn_all

    def _L3_ffn_setup():
        import jax, jax.numpy as jnp
        import numpy as np
        D_MODEL = 256
        N_HEADS = 16
        HEAD_DIM = D_MODEL // N_HEADS
        FFN_DIM = 1024
        N_EXPERTS = 8
        CAP_FRAC = 0.25
        MOE_TOKEN_DROPOUT = 0.2
        LN_EPS = 1e-05
        B, S = (4, 128)

        def _layer_norm(x, g, b):
            mu = x.mean(-1, keepdims=True)
            var = ((x - mu) ** 2).mean(-1, keepdims=True)
            return (x - mu) * jax.lax.rsqrt(var + LN_EPS) * g + b

        def _self_attention(x, wq, bq, wk, bk, wv, bv, wo, bo):
            b, s, d = x.shape
            q = ((x @ wq + bq) * HEAD_DIM ** (-0.5)).reshape(b, s, N_HEADS, HEAD_DIM)
            k = (x @ wk + bk).reshape(b, s, N_HEADS, HEAD_DIM)
            v = (x @ wv + bv).reshape(b, s, N_HEADS, HEAD_DIM)
            scores = jnp.einsum('bqhd,bkhd->bhqk', q, k)
            p = jax.nn.softmax(scores, axis=-1)
            o = jnp.einsum('bhqk,bkhd->bqhd', p, v).reshape(b, s, d)
            return o @ wo + bo

        def _moe_ffn(x, wr, w1, b1, w2, b2):
            T, D = x.shape
            C = int(np.ceil(CAP_FRAC * T))
            logits = x @ wr
            probs = jax.nn.softmax(logits, axis=-1)
            top1 = jnp.argmax(probs, axis=-1)
            m1 = jax.nn.one_hot(top1, N_EXPERTS, dtype=x.dtype)
            top2 = jnp.argmax(jnp.where(m1 > 0, -jnp.inf, logits), axis=-1)
            m2 = jax.nn.one_hot(top2, N_EXPERTS, dtype=x.dtype)
            loc1 = jnp.cumsum(m1, axis=0) - 1.0
            loc2 = jnp.cumsum(m2, axis=0) - 1.0 + m1.sum(0, keepdims=True)
            m1 = m1 * (loc1 < C)
            m2 = m2 * (loc2 < C)
            t1 = (probs * m1).sum(-1)
            t2 = (probs * m2).sum(-1)
            denom = jnp.maximum(t1 + t2, jnp.finfo(x.dtype).eps)
            t1, t2 = (t1 / denom, t2 / denom)
            tok = jnp.arange(T)
            s1 = loc1[tok, top1].astype(jnp.int32)
            s2 = loc2[tok, top2].astype(jnp.int32)
            v1 = m1[tok, top1] > 0
            v2 = m2[tok, top2] > 0
            s1 = jnp.where(v1, s1, C)
            s2 = jnp.where(v2, s2, C)
            buf = jnp.zeros((N_EXPERTS, C, D), x.dtype)
            buf = buf.at[top1, s1].set(x, mode='drop')
            buf = buf.at[top2, s2].set(x, mode='drop')
            h = jax.nn.relu(jnp.einsum('ecd,edf->ecf', buf, w1) + b1[:, None, :])
            y = (jnp.einsum('ecf,efd->ecd', h, w2) + b2[:, None, :]) * (1.0 - MOE_TOKEN_DROPOUT)
            y1 = y[top1, jnp.minimum(s1, C - 1)]
            y2 = y[top2, jnp.minimum(s2, C - 1)]
            g1 = t1 * v1
            g2 = t2 * v2
            return g1[:, None] * y1 + g2[:, None] * y2
        key = jax.random.key(seed)
        ks = jax.random.split(key, 20)

        def w(k, shape, scale=0.02):
            return jax.random.normal(k, shape, jnp.float32) * scale
        return {'x': jax.random.normal(ks[0], (B, S, D_MODEL), jnp.float32), 'wq': w(ks[1], (D_MODEL, D_MODEL)), 'bq': w(ks[2], (D_MODEL,)), 'wk': w(ks[3], (D_MODEL, D_MODEL)), 'bk': w(ks[4], (D_MODEL,)), 'wv': w(ks[5], (D_MODEL, D_MODEL)), 'bv': w(ks[6], (D_MODEL,)), 'wo': w(ks[7], (D_MODEL, D_MODEL)), 'bo': w(ks[8], (D_MODEL,)), 'ln1_g': 1.0 + w(ks[9], (D_MODEL,)), 'ln1_b': w(ks[10], (D_MODEL,)), 'ln2_g': 1.0 + w(ks[11], (D_MODEL,)), 'ln2_b': w(ks[12], (D_MODEL,)), 'wr': w(ks[13], (D_MODEL, N_EXPERTS)), 'w1': w(ks[14], (N_EXPERTS, D_MODEL, FFN_DIM)), 'b1': w(ks[15], (N_EXPERTS, FFN_DIM)), 'w2': w(ks[16], (N_EXPERTS, FFN_DIM, D_MODEL)), 'b2': w(ks[17], (N_EXPERTS, D_MODEL))}
    _L3_ffn_all = _L3_ffn_setup()
    _L3_ffn_in = {k: v for k, v in _L3_ffn_all.items() if k in ('wq', 'bq', 'wk', 'bk', 'wv', 'bv', 'wo', 'bo', 'ln1_g', 'ln1_b', 'ln2_g', 'ln2_b', 'wr', 'w1', 'b1', 'w2', 'b2')}
    del _L3_ffn_all
    return {'x': x, 'ctx_1024': ctx_1024, 'mask_BxS2_bk0': mask_BxS2_bk0, 'mask_BxS2_ik0': mask_BxS2_ik0, 'L0_xattn_Wq': _L0_xattn_in['Wq'], 'L0_xattn_bq': _L0_xattn_in['bq'], 'L0_xattn_Wk': _L0_xattn_in['Wk'], 'L0_xattn_bk': _L0_xattn_in['bk'], 'L0_xattn_Wv': _L0_xattn_in['Wv'], 'L0_xattn_bv': _L0_xattn_in['bv'], 'L0_xattn_Wo': _L0_xattn_in['Wo'], 'L0_xattn_bo': _L0_xattn_in['bo'], 'L0_attn_scale1': _L0_attn_in['scale1'], 'L0_attn_scale2': _L0_attn_in['scale2'], 'L0_attn_gamma': _L0_attn_in['gamma'], 'L0_attn_qkv_w': _L0_attn_in['qkv_w'], 'L0_attn_proj_w': _L0_attn_in['proj_w'], 'L0_attn_proj_b': _L0_attn_in['proj_b'], 'L0_attn_conv1_w': _L0_attn_in['conv1_w'], 'L0_attn_conv1_b': _L0_attn_in['conv1_b'], 'L0_attn_conv2_w': _L0_attn_in['conv2_w'], 'L0_attn_conv2_b': _L0_attn_in['conv2_b'], 'L0_ffn_w1_w': _L0_ffn_in['w1_w'], 'L0_ffn_w1_s': _L0_ffn_in['w1_s'], 'L0_ffn_w2_w': _L0_ffn_in['w2_w'], 'L0_ffn_w2_s': _L0_ffn_in['w2_s'], 'L0_ffn_h1_w': _L0_ffn_in['h1_w'], 'L0_ffn_h1_s': _L0_ffn_in['h1_s'], 'L0_ffn_h2_w': _L0_ffn_in['h2_w'], 'L0_ffn_h2_s': _L0_ffn_in['h2_s'], 'L0_ffn_w3_w': _L0_ffn_in['w3_w'], 'L0_ffn_w3_s': _L0_ffn_in['w3_s'], 'L1_xattn_Wq': _L1_xattn_in['Wq'], 'L1_xattn_bq': _L1_xattn_in['bq'], 'L1_xattn_Wk': _L1_xattn_in['Wk'], 'L1_xattn_bk': _L1_xattn_in['bk'], 'L1_xattn_Wv': _L1_xattn_in['Wv'], 'L1_xattn_bv': _L1_xattn_in['bv'], 'L1_attn_Wq': _L1_attn_in['Wq'], 'L1_attn_Wk': _L1_attn_in['Wk'], 'L1_attn_Wv': _L1_attn_in['Wv'], 'L1_attn_gamma': _L1_attn_in['gamma'], 'L1_ffn_gate_w': _L1_ffn_in['gate_w'], 'L1_ffn_w_gate': _L1_ffn_in['w_gate'], 'L1_ffn_w_up': _L1_ffn_in['w_up'], 'L1_ffn_w_down': _L1_ffn_in['w_down'], 'L2_xattn_Wq': _L2_xattn_in['Wq'], 'L2_xattn_bq': _L2_xattn_in['bq'], 'L2_xattn_Wk': _L2_xattn_in['Wk'], 'L2_xattn_bk': _L2_xattn_in['bk'], 'L2_xattn_Wv': _L2_xattn_in['Wv'], 'L2_xattn_bv': _L2_xattn_in['bv'], 'L2_attn_W_k': _L2_attn_in['W_k'], 'L2_attn_W_v': _L2_attn_in['W_v'], 'L2_attn_W_o': _L2_attn_in['W_o'], 'L2_ffn_router_w': _L2_ffn_in['router_w'], 'L2_ffn_router_b': _L2_ffn_in['router_b'], 'L2_ffn_routed_w1': _L2_ffn_in['routed_w1'], 'L2_ffn_routed_w3': _L2_ffn_in['routed_w3'], 'L2_ffn_routed_w2': _L2_ffn_in['routed_w2'], 'L2_ffn_shared_w1': _L2_ffn_in['shared_w1'], 'L2_ffn_shared_w3': _L2_ffn_in['shared_w3'], 'L2_ffn_shared_w2': _L2_ffn_in['shared_w2'], 'L3_xattn_q_w': _L3_xattn_in['q_w'], 'L3_xattn_q_b': _L3_xattn_in['q_b'], 'L3_xattn_k_w': _L3_xattn_in['k_w'], 'L3_xattn_k_b': _L3_xattn_in['k_b'], 'L3_xattn_v_w': _L3_xattn_in['v_w'], 'L3_xattn_v_b': _L3_xattn_in['v_b'], 'L3_attn_Wq': _L3_attn_in['Wq'], 'L3_attn_Wk': _L3_attn_in['Wk'], 'L3_attn_Wv': _L3_attn_in['Wv'], 'L3_attn_Wg': _L3_attn_in['Wg'], 'L3_attn_Wo': _L3_attn_in['Wo'], 'L3_attn_gnorm_w': _L3_attn_in['gnorm_w'], 'L3_ffn_wq': _L3_ffn_in['wq'], 'L3_ffn_bq': _L3_ffn_in['bq'], 'L3_ffn_wk': _L3_ffn_in['wk'], 'L3_ffn_bk': _L3_ffn_in['bk'], 'L3_ffn_wv': _L3_ffn_in['wv'], 'L3_ffn_bv': _L3_ffn_in['bv'], 'L3_ffn_wo': _L3_ffn_in['wo'], 'L3_ffn_bo': _L3_ffn_in['bo'], 'L3_ffn_ln1_g': _L3_ffn_in['ln1_g'], 'L3_ffn_ln1_b': _L3_ffn_in['ln1_b'], 'L3_ffn_ln2_g': _L3_ffn_in['ln2_g'], 'L3_ffn_ln2_b': _L3_ffn_in['ln2_b'], 'L3_ffn_wr': _L3_ffn_in['wr'], 'L3_ffn_w1': _L3_ffn_in['w1'], 'L3_ffn_b1': _L3_ffn_in['b1'], 'L3_ffn_w2': _L3_ffn_in['w2'], 'L3_ffn_b2': _L3_ffn_in['b2']}

def reference(x, ctx_1024, mask_BxS2_bk0, mask_BxS2_ik0, L0_xattn_Wq, L0_xattn_bq, L0_xattn_Wk, L0_xattn_bk, L0_xattn_Wv, L0_xattn_bv, L0_xattn_Wo, L0_xattn_bo, L0_attn_scale1, L0_attn_scale2, L0_attn_gamma, L0_attn_qkv_w, L0_attn_proj_w, L0_attn_proj_b, L0_attn_conv1_w, L0_attn_conv1_b, L0_attn_conv2_w, L0_attn_conv2_b, L0_ffn_w1_w, L0_ffn_w1_s, L0_ffn_w2_w, L0_ffn_w2_s, L0_ffn_h1_w, L0_ffn_h1_s, L0_ffn_h2_w, L0_ffn_h2_s, L0_ffn_w3_w, L0_ffn_w3_s, L1_xattn_Wq, L1_xattn_bq, L1_xattn_Wk, L1_xattn_bk, L1_xattn_Wv, L1_xattn_bv, L1_attn_Wq, L1_attn_Wk, L1_attn_Wv, L1_attn_gamma, L1_ffn_gate_w, L1_ffn_w_gate, L1_ffn_w_up, L1_ffn_w_down, L2_xattn_Wq, L2_xattn_bq, L2_xattn_Wk, L2_xattn_bk, L2_xattn_Wv, L2_xattn_bv, L2_attn_W_k, L2_attn_W_v, L2_attn_W_o, L2_ffn_router_w, L2_ffn_router_b, L2_ffn_routed_w1, L2_ffn_routed_w3, L2_ffn_routed_w2, L2_ffn_shared_w1, L2_ffn_shared_w3, L2_ffn_shared_w2, L3_xattn_q_w, L3_xattn_q_b, L3_xattn_k_w, L3_xattn_k_b, L3_xattn_v_w, L3_xattn_v_b, L3_attn_Wq, L3_attn_Wk, L3_attn_Wv, L3_attn_Wg, L3_attn_Wo, L3_attn_gnorm_w, L3_ffn_wq, L3_ffn_bq, L3_ffn_wk, L3_ffn_bk, L3_ffn_wv, L3_ffn_bv, L3_ffn_wo, L3_ffn_bo, L3_ffn_ln1_g, L3_ffn_ln1_b, L3_ffn_ln2_g, L3_ffn_ln2_b, L3_ffn_wr, L3_ffn_w1, L3_ffn_b1, L3_ffn_w2, L3_ffn_b2):
    import jax
    import jax.numpy as jnp

    def _L0_xattn_ref(query, key_value, key_mask, Wq, bq, Wk, bk, Wv, bv, Wo, bo):
        import jax, jax.numpy as jnp
        import numpy as np
        B, LQ, LKV = (8, 256, 512)
        QDIM, KDIM, HID = (256, 256, 256)
        Q = query @ Wq + bq
        K = key_value @ Wk + bk
        V = key_value @ Wv + bv
        hid = Q.shape[-1]
        scores = jnp.einsum('bqh,bkh->bqk', Q, K) / jnp.sqrt(jnp.float32(hid))
        scores = jnp.where(key_mask[:, None, :], scores, jnp.float32(-1000000000.0))
        attn = jax.nn.softmax(scores, axis=-1)
        context = jnp.einsum('bqk,bkh->bqh', attn, V)
        return context @ Wo + bo

    def _L0_attn_ref(x, scale1, scale2, gamma, qkv_w, proj_w, proj_b, conv1_w, conv1_b, conv2_w, conv2_b):
        import jax, jax.numpy as jnp
        import numpy as np
        DIM = 256
        HEADS = 16
        HIDDEN = 512
        EPS = 1e-06

        def _rmsnorm(x, scale):
            norm = jnp.linalg.norm(x, axis=-1, keepdims=True)
            return x * (scale * (x.shape[-1] ** 0.5 + EPS) / norm)
        B, N, C = x.shape
        h, d = (HEADS, C // HEADS)
        xn = _rmsnorm(x, scale1)
        qkv = jnp.einsum('bnc,fc->bnf', xn, qkv_w)
        qkv = qkv.reshape(B, N, 3, h, d).transpose(2, 0, 3, 1, 4)
        q, k, v = (qkv[0], qkv[1], qkv[2])
        phi = lambda t: jnp.exp(-0.5 * t * t)
        q, k = (phi(q), phi(k))
        kv = jnp.einsum('bhnd,bhne->bhde', k, v)
        z = 1.0 / (jnp.einsum('bhnd,bhd->bhn', q, k.sum(2)) + 1e-06)
        out = jnp.einsum('bhnd,bhde,bhn->bhne', q, kv, z)
        out = out.transpose(0, 2, 1, 3).reshape(B, N, C)
        attn = jnp.einsum('bnc,oc->bno', out, proj_w) + proj_b
        x = x + gamma * attn
        xn2 = _rmsnorm(x, scale2)
        hdd = jax.nn.gelu(jnp.einsum('bnc,hc->bnh', xn2, conv1_w) + conv1_b, approximate=False)
        mlp = jnp.einsum('bnh,ch->bnc', hdd, conv2_w) + conv2_b
        return x + gamma * mlp

    def _L0_ffn_ref(x, w1_w, w1_s, w2_w, w2_s, h1_w, h1_s, h2_w, h2_s, w3_w, w3_s):
        import jax, jax.numpy as jnp
        import numpy as np
        D_IN, D_HID = (256, 1024)

        def _ternary(key, shape):
            return jax.random.randint(key, shape, -1, 2).astype(jnp.float32)

        def _tlin(x, w, s):
            return jnp.einsum('bsi,oi->bso', x, w) * s
        h = jax.nn.silu(_tlin(x, w1_w, w1_s)) * _tlin(x, w2_w, w2_s)
        h = jax.nn.gelu(_tlin(h, h1_w, h1_s), approximate=False)
        h = jax.nn.gelu(_tlin(h, h2_w, h2_s), approximate=False)
        return _tlin(h, w3_w, w3_s)

    def _L1_xattn_ref(query, key, value, Wq, bq, Wk, bk, Wv, bv):
        import jax, jax.numpy as jnp
        import numpy as np
        D = 256
        q = jnp.einsum('bnd,ed->bne', query, Wq) + bq
        k = jnp.einsum('bnd,ed->bne', key, Wk) + bk
        v = jnp.einsum('bnd,ed->bne', value, Wv) + bv
        scores = jnp.einsum('bqd,bkd->bqk', q, k)
        attn = jax.nn.softmax(scores, axis=-1)
        return jnp.einsum('bqk,bkd->bqd', attn, v)

    def _L1_attn_ref(x, Wq, Wk, Wv, gamma):
        import jax, jax.numpy as jnp
        import numpy as np
        B, S, C = (32, 256, 256)
        f = jnp.einsum('bsc,dc->bsd', x, Wq)
        g = jnp.einsum('bsc,dc->bsd', x, Wk)
        h = jnp.einsum('bsc,dc->bsd', x, Wv)
        scores = jnp.einsum('bsd,btd->bst', f, g)
        beta = jax.nn.softmax(scores, axis=1)
        o = gamma[0] * jnp.einsum('bsc,bst->btc', h, beta) + x
        return o

    def _L1_ffn_ref(hidden_states, gate_w, w_gate, w_up, w_down):
        import jax, jax.numpy as jnp
        import numpy as np
        B, S, H, I, E = (2, 1024, 256, 128, 8)
        b, s, h = hidden_states.shape
        x = hidden_states.reshape(-1, h)
        logits = x @ gate_w.T
        top_v = jnp.max(logits, axis=-1)
        sel = jnp.argmax(logits, axis=-1)
        rw = jax.nn.sigmoid(top_v)
        out = jnp.zeros_like(x)
        n_exp = gate_w.shape[0]
        for e in range(n_exp):
            mask = (sel == e).astype(x.dtype)
            xs = x * (rw * mask)[:, None]
            g = xs @ w_gate[e].T
            u = xs @ w_up[e].T
            out = out + u * jax.nn.silu(g) @ w_down[e].T
        return out.reshape(b, s, h)

    def _L2_xattn_ref(x1, x2, Wq, bq, Wk, bk, Wv, bv):
        import jax, jax.numpy as jnp
        import numpy as np
        B, SQ, SK, D, H = (4, 512, 512, 256, 16)
        SCALE = (D / H) ** 0.5
        q = x1 @ Wq.T + bq
        k = x2 @ Wk.T + bk
        v = x2 @ Wv.T + bv
        qk = jnp.einsum('bqd,bkd->bqk', q, k) * SCALE
        attn = jax.nn.softmax(qk, axis=-1)
        return jnp.einsum('bqk,bkd->bqd', attn, v)

    def _L2_attn_ref(x, W_k, W_v, W_o):
        import jax, jax.numpy as jnp
        import numpy as np
        NUM_HEADS = 16
        B, S, D = x.shape
        H = NUM_HEADS
        dk = D // H
        inv_sqrt_dk = 1.0 / jnp.sqrt(jnp.asarray(dk, dtype=x.dtype))
        Q = (x @ W_k.T).reshape(B, S, H, dk).transpose(0, 2, 1, 3)
        sq_norm = jnp.sum(Q * Q, axis=-1, keepdims=True)
        dot = jnp.einsum('bhsk,bhtk->bhst', Q, Q)
        squared_dist = sq_norm - 2.0 * dot + sq_norm.transpose(0, 1, 3, 2)
        scores = -squared_dist * inv_sqrt_dk
        attn = jax.nn.softmax(scores, axis=-1)
        context_q = jnp.einsum('bhst,bhtk->bhsk', attn, Q)
        Wq_h = W_k.reshape(H, dk, D)
        Wv_h = W_v.reshape(H, dk, D)
        merged = jnp.einsum('hkd,hvd->hkv', Wq_h, Wv_h)
        attn_out = jnp.einsum('bhsk,hkv->bhsv', context_q, merged) * inv_sqrt_dk
        attn_out = attn_out.transpose(0, 2, 1, 3).reshape(B, S, D)
        return attn_out @ W_o.T

    def _L2_ffn_ref(x, router_w, router_b, routed_w1, routed_w3, routed_w2, shared_w1, shared_w3, shared_w2):
        import jax, jax.numpy as jnp
        import numpy as np
        BEST_K = 2

        def _expert(xf, w1, w3, w2):
            return jax.nn.silu(xf @ w1) * (xf @ w3) @ w2
        B, S, D = x.shape
        T = B * S
        xf = x.reshape(T, D)
        logits = xf @ router_w + router_b
        topk_vals, topk_idx = jax.lax.top_k(logits, BEST_K)
        sparse = jnp.full_like(logits, -jnp.inf)
        sparse = sparse.at[jnp.arange(T)[:, None], topk_idx].set(topk_vals)
        gates = jax.nn.softmax(sparse, axis=-1)
        routed = jax.vmap(_expert, in_axes=(None, 0, 0, 0))(xf, routed_w1, routed_w3, routed_w2)
        routed_out = jnp.einsum('etd,te->td', routed, gates)
        shared_out = jax.vmap(_expert, in_axes=(None, 0, 0, 0))(xf, shared_w1, shared_w3, shared_w2).sum(axis=0)
        return (routed_out + shared_out).reshape(B, S, D)

    def _L3_xattn_ref(hidden_states, context, attention_mask, q_w, q_b, k_w, k_b, v_w, v_b):
        import jax, jax.numpy as jnp
        import numpy as np
        B, LQ, LK, D = (4, 512, 512, 256)
        H = 16
        HD = D // H

        def _split_heads(x):
            b, l, _ = x.shape
            return x.reshape(b, l, H, HD).transpose(0, 2, 1, 3)
        q = _split_heads(hidden_states @ q_w.T + q_b)
        k = _split_heads(context @ k_w.T + k_b)
        v = _split_heads(context @ v_w.T + v_b)
        scores = jnp.einsum('bhqd,bhkd->bhqk', q, k) / jnp.sqrt(jnp.float32(HD))
        mask = (attention_mask > 0)[:, None, None, :]
        scores = jnp.where(mask, -jnp.inf, scores)
        probs = jax.nn.softmax(scores, axis=-1)
        ctx = jnp.einsum('bhqk,bhkd->bhqd', probs, v)
        ctx = ctx.transpose(0, 2, 1, 3).reshape(ctx.shape[0], ctx.shape[2], H * HD)
        return ctx

    def _L3_attn_ref(x, Wq, Wk, Wv, Wg, Wo, gnorm_w):
        import jax, jax.numpy as jnp
        import numpy as np
        D_MODEL = 256
        NUM_HEADS = 4
        EXPAND_K = 1.0
        EXPAND_V = 2.0
        KEY_DIM = int(D_MODEL * EXPAND_K)
        VALUE_DIM = int(D_MODEL * EXPAND_V)
        HEAD_K = KEY_DIM // NUM_HEADS
        HEAD_V = VALUE_DIM // NUM_HEADS
        CHUNK = 64
        EPS = 1e-05
        ROPE_BASE = 10000.0

        def _apply_rotary(q, k):
            d = q.shape[-1]
            half = d // 2
            inv_freq = 1.0 / ROPE_BASE ** (jnp.arange(0, d, 2, dtype=jnp.float32) / d)
            t = jnp.arange(q.shape[1], dtype=jnp.float32)
            freqs = t[:, None] * inv_freq[None, :]
            cos = jnp.cos(freqs)[None, :, None, :]
            sin = jnp.sin(freqs)[None, :, None, :]

            def rot(x):
                x1, x2 = (x[..., :half], x[..., half:])
                return jnp.concatenate([x1 * cos - x2 * sin, x2 * cos + x1 * sin], axis=-1)
            return (rot(q), rot(k))

        def _chunk_retention(q, k, v, gamma):
            B, T, H, dk = q.shape
            dv = v.shape[-1]
            C = CHUNK
            N = T // C
            qc = q.reshape(B, N, C, H, dk).transpose(1, 0, 3, 2, 4)
            kc = k.reshape(B, N, C, H, dk).transpose(1, 0, 3, 2, 4)
            vc = v.reshape(B, N, C, H, dv).transpose(1, 0, 3, 2, 4)
            i = jnp.arange(C, dtype=jnp.float32)
            cross_dec = gamma[:, None] ** (i + 1.0)
            k_dec = gamma[:, None] ** (C - 1.0 - i)
            diff = i[:, None] - i[None, :]
            mask = jnp.where(diff >= 0, gamma[:, None, None] ** diff, 0.0)
            gC = gamma ** C

            def step(S, inp):
                qb, kb, vb = inp
                attn = jnp.einsum('bhid,bhjd->bhij', qb, kb) * mask
                o_intra = jnp.einsum('bhij,bhjv->bhiv', attn, vb)
                o_inter = jnp.einsum('bhid,bhdv->bhiv', qb * cross_dec[:, :, None], S)
                S_new = gC[:, None, None] * S + jnp.einsum('bhjd,bhjv->bhdv', kb * k_dec[:, :, None], vb)
                return (S_new, o_intra + o_inter)
            S0 = jnp.zeros((B, H, dk, dv), dtype=q.dtype)
            _, o = jax.lax.scan(step, S0, (qc, kc, vc))
            return o.transpose(1, 0, 3, 2, 4).reshape(B, T, H, dv)
        B, T, _ = x.shape
        H = NUM_HEADS
        q = (x @ Wq.T).reshape(B, T, H, HEAD_K)
        k = (x @ Wk.T).reshape(B, T, H, HEAD_K)
        v = (x @ Wv.T).reshape(B, T, H, HEAD_V)
        g = (x @ Wg.T).reshape(B, T, H, HEAD_V)
        q, k = _apply_rotary(q, k)
        q = q * HEAD_K ** (-0.5)
        gamma = 1.0 - jnp.exp2(-5.0 - jnp.arange(H, dtype=jnp.float32))
        o = _chunk_retention(q, k, v, gamma)
        var = jnp.mean(o * o, axis=-1, keepdims=True)
        o = o * jax.lax.rsqrt(var + EPS) * gnorm_w
        o = o * (g * jax.nn.sigmoid(g))
        return o.reshape(B, T, H * HEAD_V) @ Wo.T

    def _L3_ffn_ref(x, wq, bq, wk, bk, wv, bv, wo, bo, ln1_g, ln1_b, ln2_g, ln2_b, wr, w1, b1, w2, b2):
        import jax, jax.numpy as jnp
        import numpy as np
        D_MODEL = 256
        N_HEADS = 16
        HEAD_DIM = D_MODEL // N_HEADS
        FFN_DIM = 1024
        N_EXPERTS = 8
        CAP_FRAC = 0.25
        MOE_TOKEN_DROPOUT = 0.2
        LN_EPS = 1e-05
        B, S = (4, 128)

        def _layer_norm(x, g, b):
            mu = x.mean(-1, keepdims=True)
            var = ((x - mu) ** 2).mean(-1, keepdims=True)
            return (x - mu) * jax.lax.rsqrt(var + LN_EPS) * g + b

        def _self_attention(x, wq, bq, wk, bk, wv, bv, wo, bo):
            b, s, d = x.shape
            q = ((x @ wq + bq) * HEAD_DIM ** (-0.5)).reshape(b, s, N_HEADS, HEAD_DIM)
            k = (x @ wk + bk).reshape(b, s, N_HEADS, HEAD_DIM)
            v = (x @ wv + bv).reshape(b, s, N_HEADS, HEAD_DIM)
            scores = jnp.einsum('bqhd,bkhd->bhqk', q, k)
            p = jax.nn.softmax(scores, axis=-1)
            o = jnp.einsum('bhqk,bkhd->bqhd', p, v).reshape(b, s, d)
            return o @ wo + bo

        def _moe_ffn(x, wr, w1, b1, w2, b2):
            T, D = x.shape
            C = int(np.ceil(CAP_FRAC * T))
            logits = x @ wr
            probs = jax.nn.softmax(logits, axis=-1)
            top1 = jnp.argmax(probs, axis=-1)
            m1 = jax.nn.one_hot(top1, N_EXPERTS, dtype=x.dtype)
            top2 = jnp.argmax(jnp.where(m1 > 0, -jnp.inf, logits), axis=-1)
            m2 = jax.nn.one_hot(top2, N_EXPERTS, dtype=x.dtype)
            loc1 = jnp.cumsum(m1, axis=0) - 1.0
            loc2 = jnp.cumsum(m2, axis=0) - 1.0 + m1.sum(0, keepdims=True)
            m1 = m1 * (loc1 < C)
            m2 = m2 * (loc2 < C)
            t1 = (probs * m1).sum(-1)
            t2 = (probs * m2).sum(-1)
            denom = jnp.maximum(t1 + t2, jnp.finfo(x.dtype).eps)
            t1, t2 = (t1 / denom, t2 / denom)
            tok = jnp.arange(T)
            s1 = loc1[tok, top1].astype(jnp.int32)
            s2 = loc2[tok, top2].astype(jnp.int32)
            v1 = m1[tok, top1] > 0
            v2 = m2[tok, top2] > 0
            s1 = jnp.where(v1, s1, C)
            s2 = jnp.where(v2, s2, C)
            buf = jnp.zeros((N_EXPERTS, C, D), x.dtype)
            buf = buf.at[top1, s1].set(x, mode='drop')
            buf = buf.at[top2, s2].set(x, mode='drop')
            h = jax.nn.relu(jnp.einsum('ecd,edf->ecf', buf, w1) + b1[:, None, :])
            y = (jnp.einsum('ecf,efd->ecd', h, w2) + b2[:, None, :]) * (1.0 - MOE_TOKEN_DROPOUT)
            y1 = y[top1, jnp.minimum(s1, C - 1)]
            y2 = y[top2, jnp.minimum(s2, C - 1)]
            g1 = t1 * v1
            g2 = t2 * v2
            return g1[:, None] * y1 + g2[:, None] * y2
        h = _layer_norm(x, ln1_g, ln1_b)
        h = _self_attention(h, wq, bq, wk, bk, wv, bv, wo, bo)
        x = x + h
        h = _layer_norm(x, ln2_g, ln2_b)
        b, s, d = h.shape
        moe = _moe_ffn(h.reshape(b * s, d), wr, w1, b1, w2, b2).reshape(b, s, d)
        return x + moe
    x = x + _L0_xattn_ref(_layernorm(x, axis=-1), ctx_1024, mask_BxS2_bk0, L0_xattn_Wq, L0_xattn_bq, L0_xattn_Wk, L0_xattn_bk, L0_xattn_Wv, L0_xattn_bv, L0_xattn_Wo, L0_xattn_bo)
    x = x + _L0_attn_ref(_layernorm(x, axis=-1), L0_attn_scale1, L0_attn_scale2, L0_attn_gamma, L0_attn_qkv_w, L0_attn_proj_w, L0_attn_proj_b, L0_attn_conv1_w, L0_attn_conv1_b, L0_attn_conv2_w, L0_attn_conv2_b)
    x = x + _L0_ffn_ref(_layernorm(x, axis=-1), L0_ffn_w1_w, L0_ffn_w1_s, L0_ffn_w2_w, L0_ffn_w2_s, L0_ffn_h1_w, L0_ffn_h1_s, L0_ffn_h2_w, L0_ffn_h2_s, L0_ffn_w3_w, L0_ffn_w3_s)
    x = x + _L1_xattn_ref(_layernorm(x, axis=-1), ctx_1024, ctx_1024, L1_xattn_Wq, L1_xattn_bq, L1_xattn_Wk, L1_xattn_bk, L1_xattn_Wv, L1_xattn_bv)
    x = x + _L1_attn_ref(_layernorm(x, axis=-1), L1_attn_Wq, L1_attn_Wk, L1_attn_Wv, L1_attn_gamma)
    x = x + _L1_ffn_ref(_layernorm(x, axis=-1), L1_ffn_gate_w, L1_ffn_w_gate, L1_ffn_w_up, L1_ffn_w_down)
    x = x + _L2_xattn_ref(_layernorm(x, axis=-1), ctx_1024, L2_xattn_Wq, L2_xattn_bq, L2_xattn_Wk, L2_xattn_bk, L2_xattn_Wv, L2_xattn_bv)
    x = x + _L2_attn_ref(_layernorm(x, axis=-1), L2_attn_W_k, L2_attn_W_v, L2_attn_W_o)
    x = x + _L2_ffn_ref(_layernorm(x, axis=-1), L2_ffn_router_w, L2_ffn_router_b, L2_ffn_routed_w1, L2_ffn_routed_w3, L2_ffn_routed_w2, L2_ffn_shared_w1, L2_ffn_shared_w3, L2_ffn_shared_w2)
    x = x + _L3_xattn_ref(_layernorm(x, axis=-1), ctx_1024, mask_BxS2_ik0, L3_xattn_q_w, L3_xattn_q_b, L3_xattn_k_w, L3_xattn_k_b, L3_xattn_v_w, L3_xattn_v_b)
    x = x + _L3_attn_ref(_layernorm(x, axis=-1), L3_attn_Wq, L3_attn_Wk, L3_attn_Wv, L3_attn_Wg, L3_attn_Wo, L3_attn_gnorm_w)
    x = x + _L3_ffn_ref(_layernorm(x, axis=-1), L3_ffn_wq, L3_ffn_bq, L3_ffn_wk, L3_ffn_bk, L3_ffn_wv, L3_ffn_bv, L3_ffn_wo, L3_ffn_bo, L3_ffn_ln1_g, L3_ffn_ln1_b, L3_ffn_ln2_g, L3_ffn_ln2_b, L3_ffn_wr, L3_ffn_w1, L3_ffn_b1, L3_ffn_w2, L3_ffn_b2)
    return x

_drawn_inputs = setup_inputs


def setup_inputs(seed=0):
    import zlib

    import numpy as np

    out = dict(_drawn_inputs(seed))
    spreads = {'L0_attn_scale1': (1.0, 0.2),
     'L0_attn_scale2': (1.0, 0.2),
     'L0_attn_gamma': (1.0, 0.2),
     'L0_attn_proj_b': (0.0, 0.1),
     'L0_attn_conv1_b': (0.0, 0.1),
     'L0_attn_conv2_b': (0.0, 0.1),
     'L2_ffn_router_b': (0.0, 0.1),
     'L3_xattn_q_b': (0.0, 0.1),
     'L3_xattn_k_b': (0.0, 0.1),
     'L3_xattn_v_b': (0.0, 0.1),
     'L3_attn_gnorm_w': (1.0, 0.2)}
    factors = {}
    for name, (base, spread) in spreads.items():
        noise = np.random.default_rng([zlib.crc32(name.encode()), seed]).standard_normal(out[name].shape)
        drawn = base * np.exp(spread * noise) if base else spread * noise
        out[name] = jnp.asarray(drawn.astype(out[name].dtype))
    for name, factor in factors.items():
        out[name] = (out[name] * factor).astype(out[name].dtype)
    return out
```

```python
from contextlib import ExitStack

import numpy as np

import concourse.bass as bass
from concourse import mybir

ALU = mybir.AluOpType
ACT = mybir.ActivationFunctionType
F32 = mybir.dt.float32
BF16 = mybir.dt.bfloat16
U8 = mybir.dt.uint8
I32 = mybir.dt.int32
AX = mybir.AxisListType.X

T = 512
KEYS = 4096
BIG = float(2 ** 30)

PACK = {
    "c": [("ident", 128), ("triu", 128), ("iota8", 32), ("ones", 128)],
    "s0": [("Wq", 512), ("Wk", 512), ("Wv", 512), ("Wo", 512), ("bq", 2), ("bk", 2), ("bv", 2), ("bo", 256)],
    "s1": [("qkv", 1536), ("proj", 512), ("conv1", 1024), ("conv2", 1024), ("s1", 2), ("s2", 2),
           ("gamma", 256), ("pb", 256), ("c1b", 4), ("c2b", 256), ("bd16", 128)],
    "s2": [("w1", 2048), ("w2", 2048), ("w3", 2048), ("w1s", 8), ("w2s", 8), ("h1s", 8), ("h2s", 8), ("w3s", 256)],
    "s2h": [(f"h{i}", 1024) for i in range(16)],
    "s3": [("Wq", 512), ("Wk", 512), ("Wv", 512), ("bq", 2), ("bk", 2), ("bv", 256)],
    "s4": [("Wq", 512), ("Wk", 512), ("Wv", 512), ("gamma", 1)],
    "s5": [("gate", 16), ("esel", 1024)] + [(f"{k}{e}", 256) for e in range(8) for k in ("g", "u", "d")],
    "s6": [("Wq", 512), ("Wk", 512), ("Wv", 512), ("bq", 2), ("bk", 2), ("bv", 256)],
    "s7": [("Wkp", 1024), ("Wk", 512), ("Wvp", 1024), ("Wo", 1024), ("bd32", 128), ("sel16", 128),
           ("sel17", 128), ("dsel", 128), ("c16", 1), ("c17", 1), ("half", 1)],
    "s8": [("rw", 16), ("rb", 32), ("esel", 1024)] + [(f"{k}{e}", 256) for e in range(10) for k in ("g", "u", "d")],
    "s9": [("Wq", 1024), ("Wk", 1024), ("Wv", 512), ("bq", 4), ("bk", 4), ("bv", 256), ("dsel", 128),
           ("selc", 1024), ("e17", 128)],
    "s10": [("Wq", 512), ("Wqs", 512), ("Wk", 512), ("Wks", 512), ("Wv", 1024), ("Wg", 1024), ("Wo", 1024),
            ("gn", 128), ("cos", 256), ("sin", 256), ("decay", 2048)],
    "s11": [("Wq", 1024), ("Wk", 1024), ("Wv", 512), ("Wo", 1024), ("bq", 4), ("bk", 4), ("bv", 256), ("bo", 256),
            ("g1", 2), ("b1n", 2), ("g2", 2), ("b2n", 2), ("wr", 16), ("b1", 64), ("b2", 256), ("dsel", 128)],
    "s11e": [(f"{k}{e}", 2048) for e in range(8) for k in ("w1_", "w2_")],
}


def places():
    at, where, span = 0, {}, {}
    for stage, entries in PACK.items():
        start = at
        for name, cols in entries:
            where[stage, name] = (at - start, cols)
            at += cols
        span[stage] = (start, at - start)
    return where, span, at


WHERE, SPAN, TOTAL = places()


class Queue:

    def __init__(self, sem):
        self.sem, self.ops, self.n, self.seen, self.pending = sem, [], 0, {}, []

    def __call__(self, fn, *deps):
        need = {}
        for s, v in flat(deps) + self.pending:
            if v > max(self.seen.get(s, 0), need.get(s, 0)):
                need[s] = v
        self.pending = []
        self.seen.update(need)
        self.n += 1
        self.ops.append((list(need.items()), fn))
        return (self.sem, self.n)

    def now(self):
        return (self.sem, self.n)

    def emit(self, eng):
        for waits, fn in self.ops:
            for s, v in waits:
                eng.wait_ge(s, v)
            fn().then_inc(self.sem, 1)


def flat(deps):
    out = []
    for d in deps:
        if d is None:
            continue
        if isinstance(d, list):
            out += flat(d)
        else:
            out.append(d)
    return out


class Ring:

    def __init__(self, slots):
        self.slots, self.free, self.i = slots, [None] * len(slots), 0

    def take(self):
        k = self.i % len(self.slots)
        self.i += 1
        return k, self.slots[k], self.free[k]

    def give(self, k, tok):
        self.free[k] = tok


def perceiver(nc, pack, x_in, ctx_n, ctx_t, mask0, mask1, out, only=(0, 99)):
    with ExitStack() as ctx:
        def sb(name, shape, dt=F32):
            return ctx.enter_context(nc.sbuf_tensor(name, shape, dt))

        PS = ctx.enter_context(nc.psum_tensor("PS", [128, 8, 512], F32))
        CT = sb("CT", [128, 2, 8192])
        CN = sb("CN", [128, 64, 256])
        X = sb("X", [128, 4, 256])
        H = sb("H", [128, 4, 256])
        HT = sb("HT", [128, 2, 512])
        CST = sb("CST", [128, SPAN["c"][1]])
        SM = sb("SM", [128, 1200])
        AR = sb("AR", [128, 15640])
        CNf = CN[:].rearrange("p a b -> p (a b)")
        CTf = CT[:].rearrange("p a b -> p (a b)")

        sems = {n: ctx.enter_context(nc.semaphore("s_" + n)) for n in ("pe", "dve", "act", "pool")}
        PE, DV, AC, PL = (Queue(sems[n]) for n in ("pe", "dve", "act", "pool"))
        V, A, G, TE = nc.vector, nc.scalar, nc.gpsimd, nc.tensor
        SP = []
        count = [0]

        def load(dst, src, *deps):
            count[0] += 1
            s = ctx.enter_context(nc.semaphore(f"d{count[0]}"))
            SP.append((flat(deps), dst, src, s))
            return (s, 16)

        sm_at = [0]

        def fence():
            sm_at[0] = 0
            now = [q.now() for q in (PE, DV, AC, PL) if q.n]
            for q in (PE, DV, AC, PL):
                q.pending = list(now)
            return now



        def sm(*shape):
            n = int(np.prod(shape))
            a = SM[:, sm_at[0]:sm_at[0] + n]
            sm_at[0] += n
            if len(shape) == 2:
                a = a.rearrange("p (a b) -> p a b", b=shape[1])
            if len(shape) == 3:
                a = a.rearrange("p (a b c) -> p a b c", b=shape[1], c=shape[2])
            return a

        def view(base, off, *shape):
            n = int(np.prod(shape))
            a = base[:, off:off + n]
            if len(shape) == 2:
                a = a.rearrange("p (a b) -> p a b", b=shape[1])
            if len(shape) == 3:
                a = a.rearrange("p (a b c) -> p a b c", b=shape[1], c=shape[2])
            if len(shape) == 4:
                a = a.rearrange("p (a b c d) -> p a b c d", b=shape[1], c=shape[2], d=shape[3])
            return a

        def weights(stage, base, off, *deps, shapes=()):
            start, n = SPAN[stage]
            tok = load(base[:, off:off + n], pack[:, start:start + n], *deps)
            got = {}
            for name, cols in PACK[stage]:
                o, c = WHERE[stage, name]
                got[name] = base[:, off + o:off + o + c]
            return got, tok

        def mat(a, kt):
            return a.rearrange("p (k o) -> p k o", k=kt)

        def tok(i):
            return slice(i * 128, i * 128 + 128)

        def mms(*jobs):
            def go():
                for o, l, r, a, z in jobs:
                    last = TE.matmul(o, l, r, start=a, stop=z, skip_group_check=True)
                return last
            return go

        def sum_jobs(o, pairs, first=True, final=True):
            n = len(pairs)
            return [(o, l, r, first and k == 0, final and k == n - 1) for k, (l, r) in enumerate(pairs)]

        cst, t_cst = weights("c", CST, 0)
        ident = cst["ident"]
        PB = Ring([0, 1, 2, 3, 4, 5])
        t_x = load(X[:], x_in.rearrange("b (i p) d -> p (b i) d", p=128))

        def bank():
            k, b, dep = PB.take()
            return k, PS[:, b, :], dep

        both = [0]

        def copy(o, i, *deps):
            both[0] ^= 1
            if both[0]:
                return DV(lambda: V.tensor_copy(o, i), *deps)
            return AC(lambda: A.copy(o, i), *deps)

        def to_T(src, dst, deps, post=None):
            ts = []
            for i in range(4):
                k, ps, free = bank()
                def go(i=i, ps=ps):
                    TE.transpose(ps[:, 0:128], src[:, i, 0:128], ident)
                    return TE.transpose(ps[:, 128:256], src[:, i, 128:256], ident)
                t = PE(go, free, deps[i], t_cst)
                if post is None:
                    t = copy(dst[:, :, tok(i)], ps[:, 0:256].rearrange("p (k t) -> p k t", k=2), t)
                    ts.append(t)
                    PB.give(k, t)
                else:
                    t = [post(dst[:, kt, tok(i)], ps[:, kt * 128:kt * 128 + 128], kt, t) for kt in range(2)]
                    ts.append(t)
                    PB.give(k, t)
            return ts

        def rsqrt(dst, src, scale, eps, *deps):
            t = DV(lambda: V.tensor_scalar(dst, src, scale, eps, ALU.mult, ALU.add), *deps)
            t = DV(lambda: V.reciprocal(dst, dst), t)
            return AC(lambda: A.activation(dst, dst, ACT.Sqrt), t)

        def norm_rows(src, dst, deps, eps=1e-5):
            st, mv, rs = sm(4, 6), sm(4, 2), sm(4)
            ts = []
            for i in range(4):
                t = DV(lambda i=i: V.bn_stats(st[:, i, :], src[:, i, :]), deps)
                ts.append(DV(lambda i=i: V.bn_aggr(mv[:, i, :], st[:, i, :]), t))
            t = rsqrt(rs, mv[:, :, 1], 1.0, eps, ts)
            return [DV(lambda i=i: V.tensor_scalar(dst[:, i, :], src[:, i, :], mv[:, i, 0:1], rs[:, i:i + 1],
                                                   ALU.subtract, ALU.mult), t) for i in range(4)]

        def rms_rows(src, dst, junk, deps):
            ss, rs = sm(4), sm(4)
            ts = [AC(lambda i=i: A.activation(junk[:, i, :], src[:, i, :], ACT.Square, accum_out=ss[:, i:i + 1]), deps)
                  for i in range(4)]
            t = rsqrt(rs, ss, 1.0, 0.0, ts)
            return [DV(lambda i=i: V.tensor_scalar(dst[:, i, :], src[:, i, :], rs[:, i:i + 1], None, ALU.mult),
                       t, ts[i]) for i in range(4)]

        def add_to_x(ps, i, n, t):
            v = X[:, i:i + n, :].rearrange("p a b -> p (a b)")
            return DV(lambda: V.tensor_tensor(v, ps, v, ALU.add), t)

        def add_row_x(row, *deps):
            return [PL(lambda i=i: G.tensor_tensor(X[:, i, :], X[:, i, :], row, ALU.add), *deps) for i in range(4)]

        def xattn(stage, W, t_w, scale, t_ct, t_cn, masks, last):
            hs = norm_rows(X, H, t_x_now[0])
            t_ht = to_T(H, HT, hs)
            Wq, Wk, Wv = (mat(W[k], 2) for k in ("Wq", "Wk", "Wv"))
            S = [view(AR, 4096 * k, KEYS) for k in range(2)]
            PTR = Ring([view(AR, 8192 + 512 * k, 512) for k in range(4)])
            QT, Q2 = view(AR, 8192, 2, 512), view(AR, 9216, 2, 512)
            OT, CX = HT, H[:].rearrange("p a b -> p (a b)").rearrange("p (k t) -> p k t", k=2)
            t_q = []
            for m in range(2):
                k, ps, free = bank()
                t = PE(mms(*sum_jobs(ps, [(Wq[:, kt, tok(m)], HT[:, kt, :]) for kt in range(2)])), free, t_ht, t_w)
                t = DV(lambda m=m, ps=ps: V.tensor_scalar(QT[:, m, :], ps, W["bq"][:, m:m + 1], scale,
                                                          ALU.add, ALU.mult), t)
                PB.give(k, t)
                t_q.append(t)
            cadd = sm(4)
            k, ps, free = bank()
            jobs = []
            for i in range(4):
                jobs += sum_jobs(ps[:, i:i + 1], [(QT[:, m, tok(i)], W["bk"][:, m:m + 1]) for m in range(2)])
            t = PE(mms(*jobs), free, t_q)
            t_c = DV(lambda ps=ps: V.tensor_copy(cadd, ps[:, 0:4]), t)
            PB.give(k, t_c)
            t_q2 = []
            for m in range(2):
                k, ps, free = bank()
                t = PE(mms(*sum_jobs(ps, [(Wk[:, h, tok(m)], QT[:, h, :]) for h in range(2)])), free, t_q)
                t = AC(lambda m=m, ps=ps: A.copy(QN[:, m, :], ps), t, t_q)
                PB.give(k, t)
                t_q2.append(t)
            q_done = PE.now()

            t_s, s_free, mx, nb, rs, ri = {}, [None, masks[1] if masks else None], sm(4), sm(4), sm(4), sm(4)
            t_pt_first = q_done

            def scores(i):
                b = i // 2
                ts = []
                for c in range(8):
                    k, ps, free = bank()
                    rhs = [CT[:, kt, b * KEYS + c * 512:b * KEYS + c * 512 + 512] for kt in range(2)]
                    t = PE(mms(*sum_jobs(ps, [(QN[:, kt, tok(i)], rhs[kt]) for kt in range(2)])),
                           free, t_q2, t_ct[b * 4 + c // 2])
                    o = S[i % 2][:, c * 512:c * 512 + 512]
                    if masks:
                        m = masks[0][:, c * 512:c * 512 + 512]
                        t = DV(lambda o=o, ps=ps, m=m, i=i: V.scalar_tensor_tensor(
                            out=o, in0=ps, scalar=cadd[:, i:i + 1], in1=m, op0=ALU.add, op1=ALU.min),
                            t, t_c, masks[1 + b], s_free[i % 2])
                    elif c % 4 == 3:
                        t = DV(lambda o=o, ps=ps, i=i: V.tensor_scalar(o, ps, cadd[:, i:i + 1], None, ALU.add),
                               t, t_c, s_free[i % 2])
                    else:
                        t = AC(lambda o=o, ps=ps, i=i: A.activation(o, ps, ACT.Identity, bias=cadd[:, i:i + 1]),
                               t, t_c, s_free[i % 2])
                    PB.give(k, t)
                    ts.append(t)
                if masks and i == 1:
                    masks.append(masks_next(DV.now()))
                t = DV(lambda: V.tensor_reduce(mx[:, i:i + 1], S[i % 2], AX, ALU.max), ts)
                t = DV(lambda: V.tensor_scalar(nb[:, i:i + 1], mx[:, i:i + 1], -1.0, None, ALU.mult), t)
                t = AC(lambda: A.activation(S[i % 2], S[i % 2], ACT.Exp, bias=nb[:, i:i + 1],
                                            accum_out=rs[:, i:i + 1]), t, ts)
                t_s[i] = t
                return DV(lambda: V.reciprocal(ri[:, i:i + 1], rs[:, i:i + 1]), t)

            masks_next = masks.pop() if masks else None
            t_r, t_o, o_free = {}, [], [None, None]
            t_r[0] = scores(0)
            for i in range(4):
                if i + 1 < 4:
                    t_r[i + 1] = scores(i + 1)
                b = i // 2
                O = PS[:, 6 + i % 2, 0:256]

                def turn(c, i=i):
                    k, ps, free = bank()
                    def go():
                        for y in range(4):
                            u = c * 4 + y
                            l = TE.transpose(ps[:, y * 128:y * 128 + 128], S[i % 2][:, u * 128:u * 128 + 128], ident)
                        return l
                    t = PE(go, free, t_s[i])
                    kk, pt, pfree = PTR.take()
                    t = copy(pt, ps, t, pfree, t_pt_first)
                    PB.give(k, t)
                    return kk, pt, t
                nxt = [turn(0), turn(1)]
                for c in range(8):
                    kk, pt, t = nxt.pop(0)
                    if c + 2 < 8:
                        nxt.append(turn(c + 2))
                    jobs = [(O, pt[:, y * 128:y * 128 + 128], CN[:, b * 32 + c * 4 + y, :],
                             c == 0 and y == 0, c == 7 and y == 3) for y in range(4)]
                    t = PE(mms(*jobs), t, t_cn[b * 2 + c // 4], o_free[i % 2])
                    PTR.give(kk, t)
                s_free[i % 2] = t
                t = DV(lambda i=i, O=O: V.tensor_scalar(OB[:, i, :], O, ri[:, i:i + 1], None, ALU.mult), t, t_r[i])
                o_free[i % 2] = t
                t_o.append(t)
            t_ot = to_T(OB, OT, t_o)
            if "Wo" in W:
                Wo = mat(W["Wo"], 2)
                t_row = add_row_x(W["bo"], hs, t_w)
                tc = []
                for m in range(2):
                    k, ps, free = bank()
                    t = PE(mms(*sum_jobs(ps, [(Wv[:, kt, tok(m)], OT[:, kt, :]) for kt in range(2)])), free, t_ot)
                    t = DV(lambda m=m, ps=ps: V.tensor_scalar(CX[:, m, :], ps, W["bv"][:, m:m + 1], None, ALU.add),
                           t, t_ot)
                    PB.give(k, t)
                    tc.append(t)
                src, Wf = CX, Wo
            else:
                t_row = add_row_x(W["bv"], hs, t_w)
                src, Wf, tc = OT, Wv, t_ot
            for i in range(4):
                k, ps, free = bank()
                t = PE(mms(*sum_jobs(ps[:, 0:256], [(src[:, kt, tok(i)], Wf[:, kt, :]) for kt in range(2)])), free, tc)
                t = add_to_x(ps[:, 0:256], i, 1, [t, t_row[i]])
                PB.give(k, t)

        QN = HT
        OB = H
        t_x_now = [t_x]

        W0, t_w0 = weights("s0", AR, 12288)
        MB = view(AR, 10240, 2048).bitcast(BF16)
        MW = [view(AR, 4096, 1024).bitcast(I32), view(AR, 14600, 1024).bitcast(I32)]
        MU = [w.bitcast(U8) for w in MW]
        t_ct, t_cn = [], []
        t_mu = [load(MW[b], mask0[b:b + 1, :].partition_broadcast(128)) for b in range(2)]
        for q in range(4):
            t_ct.append(load(CT[:, :, q * 1024:q * 1024 + 1024], ctx_t[:, :, q * 1024:q * 1024 + 1024]))
        for q in range(2):
            t_cn.append(load(CN[:, q * 16:q * 16 + 16, :], ctx_n[:, q * 16:q * 16 + 16, :]))
        for q in range(4, 8):
            t_ct.append(load(CT[:, :, q * 1024:q * 1024 + 1024], ctx_t[:, :, q * 1024:q * 1024 + 1024]))
        for q in range(2, 4):
            t_cn.append(load(CN[:, q * 16:q * 16 + 16, :], ctx_n[:, q * 16:q * 16 + 16, :]))

        def bounds(b, *deps):
            return DV(lambda: V.tensor_scalar(MB, MU[b], 2 * BIG, -BIG, ALU.mult, ALU.add), t_mu[b], *deps)

        if only[0] <= 0 <= only[1]:
            xattn("s0", W0, t_w0, 1.0 / 16, t_ct, t_cn,
                  [MB, bounds(0), lambda d: bounds(1, d)], None)
        f = fence()

        def stage_1(f):
            W, t_w = weights("s1", AR, 0, f)
            o = SPAN["s1"][1]
            hs = norm_rows(X, H, None)
            Y, Z = view(AR, o, 4, 256), view(AR, o + 1024, 4, 256)
            ZT = HT
            OT = view(AR, o + 2048, 2, 512)
            QF = view(AR, o + 3072, 2, 512)
            KV = view(AR, o + 4096, 4, 512)
            HD = view(AR, o + 6144, 4, 512)
            KM = view(AR, o + 6144, 2, 2, 128)
            KS = view(AR, o + 6656, 2, 2, 128)
            tmp = view(AR, o + 7168, 2, 512)
            qkv, proj, conv1, conv2 = mat(W["qkv"], 2), mat(W["proj"], 2), mat(W["conv1"], 2), mat(W["conv2"], 4)

            def scaled(col):
                def post(dst, ps, kt, t):
                    return DV(lambda: V.tensor_scalar(dst, ps, col[:, kt:kt + 1], 16.0 + 1e-6, ALU.mult, ALU.mult),
                              t, t_w)
                return post
            rs = rms_rows(H, Z, Y, hs)
            t_zt = to_T(Z, ZT, rs, scaled(W["s1"]))
            t_qf = []
            for m in range(2):
                k, ps, free = bank()
                t = PE(mms(*sum_jobs(ps, [(qkv[:, kt, tok(m)], ZT[:, kt, :]) for kt in range(2)])), free, t_zt)
                t = AC(lambda m=m, ps=ps: A.activation(QF[:, m, :], ps, ACT.Square), t)
                PB.give(k, t)
                t_qf.append(AC(lambda m=m: A.activation(QF[:, m, :], QF[:, m, :], ACT.Exp, scale=-0.5), t))
            t_kv = []
            for i in range(4):
                k, ps, free = bank()
                t = PE(mms(*sum_jobs(ps, [(ZT[:, kt, tok(i)], qkv[:, kt, 256:768]) for kt in range(2)])), free, t_zt)
                t1 = AC(lambda i=i, ps=ps: A.activation(KV[:, i, 0:256], ps[:, 0:256], ACT.Square), t)
                t2 = DV(lambda i=i, ps=ps: V.tensor_copy(KV[:, i, 256:512], ps[:, 256:512]), t1)
                PB.give(k, [t1, t2])
                t_kv.append([t2, AC(lambda i=i: A.activation(KV[:, i, 0:256], KV[:, i, 0:256], ACT.Exp, scale=-0.5),
                                    t1)])
            ksum = sm(4)
            t_at = []
            ones = cst["ones"]
            for b in range(2):
                for m in range(2):
                    k, ps, free = bank()
                    jobs = sum_jobs(ps[:, 0:128], [(KV[:, 2 * b + i, tok(m)], KV[:, 2 * b + i, 256 + m * 128:384 + m * 128])
                                                   for i in range(2)])
                    jobs += sum_jobs(ps[:, 128:129], [(KV[:, 2 * b + i, tok(m)], ones[:, 0:1]) for i in range(2)])
                    t = PE(mms(*jobs), free, t_kv[2 * b], t_kv[2 * b + 1])
                    t1 = DV(lambda b=b, m=m, ps=ps: V.tensor_tensor(KM[:, b, m, :], ps[:, 0:128], W["bd16"], ALU.mult), t)
                    c = ksum[:, 2 * b + m:2 * b + m + 1]
                    t2 = DV(lambda c=c, ps=ps: V.tensor_copy(c, ps[:, 128:129]), t)
                    PB.give(k, [t1, t2])
                    t2 = DV(lambda b=b, m=m, c=c: V.tensor_scalar(KS[:, b, m, :], W["bd16"], c, None, ALU.mult), t2)
                    q = QF[:, m, b * 256:b * 256 + 256]
                    k, ps, free = bank()
                    t = PE(mms((ps[:, 0:256], KM[:, b, m, :], q, True, True),
                               (ps[:, 256:512], KS[:, b, m, :], q, True, True)), free, t1, t2, t_qf)
                    w = tmp[:, m, 0:256]
                    t = DV(lambda w=w, ps=ps: V.tensor_scalar(w, ps[:, 256:512], 1e-6, None, ALU.add), t)
                    t = DV(lambda w=w: V.reciprocal(w, w), t)
                    t = DV(lambda b=b, m=m, ps=ps, w=w: V.tensor_tensor(OT[:, m, b * 256:b * 256 + 256], ps[:, 0:256],
                                                                        w, ALU.mult), t)
                    PB.give(k, t)
                    t_at.append(t)
            ty = []
            for i in range(4):
                k, ps, free = bank()
                t = PE(mms(*sum_jobs(ps[:, 0:256], [(OT[:, m, tok(i)], proj[:, m, :]) for m in range(2)])), free, t_at)
                y = Y[:, i, :]
                t = DV(lambda y=y, ps=ps: V.tensor_tensor(y, ps[:, 0:256], W["pb"], ALU.add), t)
                PB.give(k, t)
                t = DV(lambda y=y: V.tensor_tensor(y, y, W["gamma"], ALU.mult), t)
                ty.append(DV(lambda y=y, i=i: V.tensor_tensor(y, y, H[:, i, :], ALU.add), t))
            rs = rms_rows(Y, Z, H, ty)
            t_zt = to_T(Z, ZT, rs, scaled(W["s2"]))
            th = []
            for m in range(4):
                k, ps, free = bank()
                t = PE(mms(*sum_jobs(ps, [(conv1[:, kt, tok(m)], ZT[:, kt, :]) for kt in range(2)])), free, t_zt)
                t = AC(lambda m=m, ps=ps: A.activation(HD[:, m, :], ps, ACT.Gelu, bias=W["c1b"][:, m:m + 1]), t, t_at)
                PB.give(k, t)
                th.append(t)
            for i in range(4):
                k, ps, free = bank()
                t = PE(mms(*sum_jobs(ps[:, 0:256], [(HD[:, m, tok(i)], conv2[:, m, :]) for m in range(4)])), free, th)
                z = Z[:, i, :]
                t = DV(lambda z=z, ps=ps: V.tensor_tensor(z, ps[:, 0:256], W["c2b"], ALU.add), t)
                PB.give(k, t)
                t = DV(lambda z=z: V.tensor_tensor(z, z, W["gamma"], ALU.mult), t)
                t = DV(lambda z=z, i=i: V.tensor_tensor(z, z, Y[:, i, :], ALU.add), t)
                DV(lambda z=z, i=i: V.tensor_tensor(X[:, i, :], X[:, i, :], z, ALU.add), t)
            return fence()

        if only[0] <= 1 <= only[1]:
            f = stage_1(f)

        def stage_2(f):
            W, t_w = weights("s2", AR, 8192, f)
            hA, hB = view(AR, 0, 8, 512), view(AR, 4096, 8, 512)
            w1, w2, w3 = mat(W["w1"], 2), mat(W["w2"], 2), mat(W["w3"], 8)
            t_ht = to_T(H, HT, norm_rows(X, H, None))
            ts = []
            for m in range(8):
                k1, p1, f1 = bank()
                ta = PE(mms(*sum_jobs(p1, [(w1[:, kt, tok(m)], HT[:, kt, :]) for kt in range(2)])), f1, t_ht, t_w)
                k2, p2, f2 = bank()
                tb = PE(mms(*sum_jobs(p2, [(w2[:, kt, tok(m)], HT[:, kt, :]) for kt in range(2)])), f2)
                ta = AC(lambda m=m, p=p1: A.activation(hB[:, m, :], p, ACT.Silu, scale=W["w1s"][:, m:m + 1]), ta)
                PB.give(k1, ta)
                tb = DV(lambda m=m, p=p2: V.scalar_tensor_tensor(out=hA[:, m, :], in0=p, scalar=W["w2s"][:, m:m + 1],
                                                                 in1=hB[:, m, :], op0=ALU.mult, op1=ALU.mult), ta, tb)
                PB.give(k2, tb)
                ts.append(tb)
            ring = Ring([view(AR, 8192 + 1024 * k, 8, 128) for k in range(4)])
            over = PE.now()
            src, dst = hA, hB
            for layer in range(2):
                nts = []
                for m in range(8):
                    kk, w, wf = ring.take()
                    n = layer * 8 + m
                    s0 = SPAN["s2h"][0] + n * 1024
                    t_l = load(w.rearrange("p a b -> p (a b)"), pack[:, s0:s0 + 1024], over if wf is None else wf)
                    k, ps, free = bank()
                    t = PE(mms(*sum_jobs(ps, [(w[:, kt, :], src[:, kt, :]) for kt in range(8)])), free, t_l, ts)
                    ring.give(kk, t)
                    t = AC(lambda m=m, ps=ps, dst=dst, s=W["h1s" if layer == 0 else "h2s"]: A.activation(
                        dst[:, m, :], ps, ACT.Gelu, scale=s[:, m:m + 1]), t, ts)
                    PB.give(k, t)
                    nts.append(t)
                src, dst, ts = dst, src, nts
            for i in range(4):
                k, ps, free = bank()
                t = PE(mms(*sum_jobs(ps[:, 0:256], [(src[:, m, tok(i)], w3[:, m, :]) for m in range(8)])), free, ts)
                o = H[:, i, :]
                t = DV(lambda o=o, ps=ps: V.tensor_tensor(o, ps[:, 0:256], W["w3s"], ALU.mult), t)
                PB.give(k, t)
                DV(lambda o=o, i=i: V.tensor_tensor(X[:, i, :], X[:, i, :], o, ALU.add), t)
            return fence()

        if only[0] <= 2 <= only[1]:
            f = stage_2(f)

        def stage_3(f):
            W, t_w = weights("s3", AR, 12288, f)
            t_x_now[0] = None
            xattn("s3", W, t_w, 1.0, t_ct, t_cn, [], None)
            return fence()

        if only[0] <= 3 <= only[1]:
            f = stage_3(f)

        def stage_4(f):
            W, t_w = weights("s4", AR, 0, f)
            hs = norm_rows(X, H, None)
            t_ht = to_T(H, HT, hs)
            FT, GT = view(AR, 2048, 2, 512), view(AR, 3072, 2, 512)
            HV = view(AR, 4096, 4, 256)
            P, PT = view(AR, 5120, 4, 256), view(AR, 6144, 4, 256)
            Wq, Wk, Wv = (mat(W[k], 2) for k in ("Wq", "Wk", "Wv"))
            ts = []
            for w, o in ((Wq, FT), (Wk, GT)):
                for m in range(2):
                    k, ps, free = bank()
                    t = PE(mms(*sum_jobs(ps, [(w[:, kt, tok(m)], HT[:, kt, :]) for kt in range(2)])), free, t_ht, t_w)
                    t = copy(o[:, m, :], ps, t)
                    PB.give(k, t)
                    ts.append(t)
            tv = []
            for i in range(4):
                k, ps, free = bank()
                t = PE(mms(*sum_jobs(ps[:, 0:256], [(HT[:, kt, tok(i)], Wv[:, kt, :]) for kt in range(2)])), free)
                t = copy(HV[:, i, :], ps[:, 0:256], t)
                PB.give(k, t)
                tv.append(t)
            mx, nb, rs, ri = sm(4), sm(4), sm(4), sm(4)
            for i in range(4):
                b = i // 2
                k, ps, free = bank()
                t = PE(mms(*sum_jobs(ps[:, 0:256], [(GT[:, m, tok(i)], FT[:, m, b * 256:b * 256 + 256])
                                                    for m in range(2)])), free, ts)
                t1 = DV(lambda i=i, ps=ps: V.tensor_reduce(mx[:, i:i + 1], ps[:, 0:256], AX, ALU.max), t)
                t1 = DV(lambda i=i: V.tensor_scalar(nb[:, i:i + 1], mx[:, i:i + 1], -1.0, None, ALU.mult), t1)
                t1 = AC(lambda i=i, ps=ps: A.activation(P[:, i, :], ps[:, 0:256], ACT.Exp, bias=nb[:, i:i + 1],
                                                        accum_out=rs[:, i:i + 1]), t1)
                PB.give(k, t1)
                t2 = DV(lambda i=i: V.reciprocal(ri[:, i:i + 1], rs[:, i:i + 1]), t1)
                k, ps, free = bank()
                def go(i=i, ps=ps):
                    TE.transpose(ps[:, 0:128], P[:, i, 0:128], ident)
                    return TE.transpose(ps[:, 128:256], P[:, i, 128:256], ident)
                t = PE(go, free, t1)
                t = copy(PT[:, i, :], ps[:, 0:256], t)
                PB.give(k, t)
                k, ps, free = bank()
                t = PE(mms(*sum_jobs(ps[:, 0:256], [(PT[:, i, tok(y)], HV[:, 2 * b + y, :]) for y in range(2)])),
                       free, t, tv)
                p = P[:, i, :]
                t = DV(lambda i=i, ps=ps, p=p: V.tensor_scalar(p, ps[:, 0:256], ri[:, i:i + 1], W["gamma"],
                                                               ALU.mult, ALU.mult), t, t2)
                PB.give(k, t)
                t = DV(lambda i=i, p=p: V.tensor_tensor(p, p, H[:, i, :], ALU.add), t)
                DV(lambda i=i, p=p: V.tensor_tensor(X[:, i, :], X[:, i, :], p, ALU.add), t)
            return fence()

        if only[0] <= 4 <= only[1]:
            f = stage_4(f)

        def first_of_max(src, *deps):
            top, w, m, oh = sm(4), sm(4, 8), sm(4), sm(4, 8)
            up = lambda a: a.unsqueeze(2).to_broadcast([128, 4, 8])
            t = DV(lambda: V.tensor_reduce(top, src, AX, ALU.max), *deps)
            t = DV(lambda: V.tensor_tensor(w, src, up(top), ALU.is_equal), t)
            t = DV(lambda: V.tensor_tensor(w, w, cst["iota8"].rearrange("p (a b) -> p a b", b=8), ALU.mult), t)
            t = DV(lambda: V.tensor_reduce(m, w, AX, ALU.max), t)
            t = DV(lambda: V.tensor_tensor(oh, w, up(m), ALU.is_equal), t)
            return oh, top, t

        def logits8(w, row, *deps):
            lg = sm(4, 8)
            k, ps, free = bank()
            jobs = []
            for i in range(4):
                jobs += sum_jobs(ps[:, i * 8:i * 8 + 8], [(HT[:, kt, tok(i)], w[:, kt, :]) for kt in range(2)])
            t = PE(mms(*jobs), free, *deps)
            p = ps[:, 0:32].rearrange("p (a b) -> p a b", b=8)
            if row is None:
                t = DV(lambda: V.tensor_copy(lg, p), t)
            else:
                t = DV(lambda: V.tensor_tensor(lg, p, row.rearrange("p (a b) -> p a b", b=8), ALU.add), t)
            PB.give(k, t)
            return lg, t

        def rows8(R, dst, *deps):
            k, ps, free = bank()
            def go():
                for i in range(4):
                    l = TE.transpose(ps[0:8, tok(i)], R[:, i, :], ident)
                return l
            t = PE(go, free, *deps)
            t = DV(lambda: V.tensor_copy(dst, ps[0:8, :]), t)
            PB.give(k, t)
            return t

        def up8(a):
            return a.unsqueeze(2).to_broadcast([128, 4, 8])

        def experts(W, n, n_gated, RT, t_rt, t_ht, work, gate_first):
            acc = [PS[:, 6 + i // 2, (i % 2) * 256:(i % 2) * 256 + 256] for i in range(4)]
            esel = W["esel"]
            rb_r = Ring([view(AR, work + 512 * k, 512) for k in range(2)])
            g_r = Ring([view(AR, work + 1024 + 512 * k, 512) for k in range(2)])
            h_r = Ring([view(AR, work + 2048 + 512 * k, 512) for k in range(3)])
            pend = []

            def down(e, hk, h, t):
                wd = W[f"d{e}"]
                jobs = [(acc[i], h[:, tok(i)], wd, e == 0 and i % 2 == 0, e == n - 1) for i in range(4)]
                t = PE(mms(*jobs), t)
                h_r.give(hk, t)
                return t
            for e in range(n):
                wg, wu = mat(W[f"g{e}"], 2), mat(W[f"u{e}"], 2)
                gated = e < n_gated
                tr = None
                if gated:
                    k, ps, free = bank()
                    t = PE(mms((ps, esel[0:8, e * 128:e * 128 + 128], RT, True, True)), free, t_rt)
                    rk, rb, rf = rb_r.take()
                    tr = AC(lambda rb=rb, ps=ps: A.copy(rb, ps), t, rf)
                    PB.give(k, tr)
                k1, p1, f1 = bank()
                ta = PE(mms(*sum_jobs(p1, [(wg[:, kt, :], HT[:, kt, :]) for kt in range(2)])), f1, t_ht)
                k2, p2, f2 = bank()
                tb = PE(mms(*sum_jobs(p2, [(wu[:, kt, :], HT[:, kt, :]) for kt in range(2)])), f2)
                gk, g, gf = g_r.take()
                hk, h, hf = h_r.take()
                if gate_first:
                    ta = DV(lambda p1=p1, g=g, rb=rb: V.tensor_tensor(g, p1, rb, ALU.mult), ta, tr, gf)
                    PB.give(k1, ta)
                    ta = AC(lambda g=g: A.activation(g, g, ACT.Silu), ta)
                    tb = DV(lambda p2=p2, h=h, rb=rb: V.tensor_tensor(h, p2, rb, ALU.mult), tb, tr, hf)
                    PB.give(k2, tb)
                    rb_r.give(rk, tb)
                    tb = DV(lambda g=g, h=h: V.tensor_tensor(h, h, g, ALU.mult), ta, tb)
                    g_r.give(gk, tb)
                else:
                    ta = AC(lambda p1=p1, g=g: A.activation(g, p1, ACT.Silu), ta, gf)
                    PB.give(k1, ta)
                    tb = DV(lambda p2=p2, h=h, g=g: V.tensor_tensor(h, p2, g, ALU.mult), tb, ta, hf)
                    PB.give(k2, tb)
                    g_r.give(gk, tb)
                    if gated:
                        tb = DV(lambda h=h, rb=rb: V.tensor_tensor(h, h, rb, ALU.mult), tb, tr)
                        rb_r.give(rk, tb)
                pend.append((e, hk, h, tb))
                if len(pend) > 1:
                    down(*pend.pop(0))
            t = down(*pend.pop(0))
            add_to_x(PS[:, 6, :], 0, 2, t)
            add_to_x(PS[:, 7, :], 2, 2, t)

        def stage_5(f):
            W, t_w = weights("s5", AR, 0, f)
            t_ht = to_T(H, HT, norm_rows(X, H, None))
            lg, t = logits8(mat(W["gate"], 2), None, t_ht, t_w)
            oh, top, t = first_of_max(lg, t)
            rw, R = sm(4), sm(4, 8)
            t = AC(lambda: A.activation(rw, top, ACT.Sigmoid), t)
            t = DV(lambda: V.tensor_tensor(R, oh, up8(rw), ALU.mult), t)
            RT = AR[0:8, 8000:8512]
            t = rows8(R, RT, t)
            experts(W, 8, 8, RT, t, t_ht, 8600, True)
            return fence()

        if only[0] <= 5 <= only[1]:
            f = stage_5(f)

        def stage_6(f):
            W, t_w = weights("s6", AR, 12288, f)
            xattn("s6", W, t_w, 4.0, t_ct, t_cn, [], None)
            return fence()

        if only[0] <= 6 <= only[1]:
            f = stage_6(f)

        def heads_max(QA, kcols, nch, width, g, b, MX, NM, *deps):
            ts = []
            for i in range(2):
                tt = tok(2 * b + i)
                for c in range(nch):
                    for j in range(4):
                        r = slice(32 * j, 32 * j + 32)
                        k, ps, free = bank()
                        t = PE(mms((ps[:, 0:width], QA[r, g, tt], kcols(c)[r], True, True)), free, *deps)
                        t = DV(lambda i=i, j=j, c=c, ps=ps: V.tensor_reduce(MX[:, i, j, c:c + 1], ps[:, 0:width],
                                                                            AX, ALU.max), t, *deps)
                        PB.give(k, t)
                        ts.append(t)
            out_ts = []
            for i in range(2):
                nm = NM[:, i, :].rearrange("p (j r) -> p j r", j=4)[:, :, 16]
                out_ts.append(DV(lambda i=i, nm=nm: V.tensor_reduce(nm, MX[:, i, :, 0:nch], AX, ALU.max), ts))
            last_mm = PE.now()
            for i in range(2):
                k, ps, free = bank()
                t = PE(lambda i=i, ps=ps: TE.transpose(ps[:, 0:128], NM[:, i, :], ident), free, out_ts[i])
                q = QA[:, g, tok(2 * b + i)]
                t = DV(lambda q=q, ps=ps: V.tensor_tensor(q, ps[:, 0:128], q, ALU.add), t, last_mm)
                PB.give(k, t)
                out_ts[i] = t
            return out_ts

        def heads_mix(QA, krow, vrow, nkt, g, b, CTX, PTR, cb, *deps):
            C = PS[:, 6 + cb % 2, 0:256]
            pend = []

            def pv(kt, jj, kk, pt, t):
                jobs = []
                for y in range(2):
                    j = 2 * jj + y
                    h = 4 * g + j
                    jobs.append((C[32 * j:32 * j + 32, :], vrow(kt)[:, 17 * h:17 * h + 32], pt[:, y, :],
                                 kt == 0, kt == nkt - 1))
                t = PE(mms(*jobs), t, c_free[cb % 2])
                PTR.give(kk, t)
                return t
            for kt in range(nkt):
                for jj in range(2):
                    k, ps2, free = pair()
                    jobs = []
                    for y in range(2):
                        r = slice(32 * (2 * jj + y), 32 * (2 * jj + y) + 32)
                        jobs.append((ps2[:, y, 0:256], krow(kt)[r], QA[r, g, b * 256:b * 256 + 256], True, True))
                    t = PE(mms(*jobs), free, *deps)
                    kk, pt, pf = PTR.take()
                    t = AC(lambda ps2=ps2, pt=pt: A.activation(pt, ps2[:, :, 0:256], ACT.Exp), t, pf)
                    give_pair(k, t)
                    pend.append((kt, jj, kk, pt, t))
                    if len(pend) > 2:
                        pv(*pend.pop(0))
            while pend:
                t = pv(*pend.pop(0))
            t = DV(lambda: V.tensor_copy(CTX[:, g, b * 256:b * 256 + 256], C), t)
            c_free[cb % 2] = t
            return t

        c_free = [None, None]
        pair_i = [0]

        def pair():
            k = pair_i[0] % 3
            pair_i[0] += 1
            return k, PS[:, 2 * k:2 * k + 2, :], [PB.free[2 * k], PB.free[2 * k + 1]]

        def give_pair(k, t):
            PB.free[2 * k] = PB.free[2 * k + 1] = t

        def heads_norm(CTX, RC, dsel, t_c):
            ts = []
            for g in range(4):
                k, ps, free = bank()
                t = PE(mms((ps, dsel, CTX[:, g, :], True, True)), free, t_c)
                t = DV(lambda g=g, ps=ps: V.reciprocal(RC[:, g % 2, :], ps), t)
                PB.give(k, t)
                ts.append(DV(lambda g=g: V.tensor_tensor(CTX[:, g, :], CTX[:, g, :], RC[:, g % 2, :], ALU.mult), t))
            return ts

        def values(W_, HTs, n, vrow, row, t_dep, t_ones):
            k, ps, free = bank()
            t = PE(mms(*sum_jobs(ps[:, 0:256], [(HTs[kt], W_[:, kt, :]) for kt in range(2)])), free, t_dep)
            o = vrow(n)[:, 0:272].rearrange("p (h r) -> p h r", r=17)[:, :, 0:16]
            p = ps[:, 0:256].rearrange("p (h r) -> p h r", r=16)
            if row is None:
                t = DV(lambda: V.tensor_copy(o, p), t, t_ones)
            else:
                t = DV(lambda: V.tensor_tensor(o, p, row.rearrange("p (h r) -> p h r", r=16), ALU.add), t, t_ones)
            PB.give(k, t)
            return t

        def stage_7(f):
            W, t_w = weights("s7", AR, 0, f)
            o = SPAN["s7"][1]
            KA, QA, CTX = view(AR, o, 4, 512), view(AR, o + 2048, 4, 512), view(AR, o + 4096, 4, 512)
            VP = view(AR, o + 6144, 4, 288)
            PTR = Ring([view(AR, o + 7296 + 512 * k, 2, 256) for k in range(3)])
            QP, SQ = view(AR, o + 8832, 512), view(AR, o + 9344, 512)
            BD = view(AR, o + 8832, 4, 128)
            RC = view(AR, o + 7296, 2, 512)
            Wkp, Wk, Wvp, Wo = mat(W["Wkp"], 2), mat(W["Wk"], 2), mat(W["Wvp"], 2), mat(W["Wo"], 4)
            t_ones = PL(lambda: G.memset(VP, 1.0))
            t_ht = to_T(H, HT, norm_rows(X, H, None))
            t_a = []
            td = None
            for g in range(4):
                k, ps, free = bank()
                t = PE(mms(*sum_jobs(ps, [(Wkp[:, kt, tok(g)], HT[:, kt, :]) for kt in range(2)])), free, t_ht, t_w)
                t1 = DV(lambda ps=ps: V.tensor_copy(QP, ps), t, td)
                t2 = AC(lambda ps=ps: A.activation(SQ, ps, ACT.Square), t1, td)
                PB.give(k, [t1, t2])
                k1, p1, f1 = bank()
                k2, p2, f2 = bank()
                t = PE(mms((p1, W["sel16"], SQ, True, True), (p2, W["sel17"], SQ, True, True)), f1, f2, t1, t2)
                ta = DV(lambda g=g, p=p1: V.scalar_tensor_tensor(out=KA[:, g, :], in0=p, scalar=W["c17"], in1=QP,
                                                                 op0=ALU.add, op1=ALU.add), t, t1)
                PB.give(k1, ta)
                tb = DV(lambda: V.tensor_scalar(SQ, QP, W["half"], W["c16"], ALU.mult, ALU.add), t, t1)
                tb = DV(lambda g=g, p=p2: V.tensor_tensor(QA[:, g, :], p, SQ, ALU.add), tb)
                PB.give(k2, tb)
                t_a += [ta, tb]
                td = [ta, tb]
            for g in range(4):
                k, ps, free = bank()
                t = PE(mms(*sum_jobs(ps[:, 0:128], [(Wkp[:, kt, tok(g)], Wvp[:, kt, tok(g)]) for kt in range(2)])), free)
                t = DV(lambda g=g, ps=ps: V.tensor_tensor(BD[:, g, :], ps[:, 0:128], W["bd32"], ALU.mult), t, td)
                PB.give(k, t)
            t_bd = t
            tv = [values(Wk, [HT[:, kt, tok(n)] for kt in range(2)], n, lambda n: VP[:, n, :], None, None, t_ones)
                  for n in range(4)]
            t_c = []
            for b in range(2):
                for g in range(4):
                    t_c.append(heads_mix(QA, lambda kt, b=b, g=g: KA[:, g, tok(2 * b + kt)],
                                         lambda kt, b=b: VP[:, 2 * b + kt, :], 2, g, b, CTX, PTR, 4 * b + g, t_a, tv))
            t_n = heads_norm(CTX, RC, W["dsel"], [t_c, PE.now()])
            AO = QA
            ts = []
            for g in range(4):
                k, ps, free = bank()
                t = PE(mms((ps, BD[:, g, :], CTX[:, g, :], True, True)), free, t_n[g], t_bd)
                t = AC(lambda g=g, ps=ps: A.mul(AO[:, g, :], ps, 0.25), t)
                PB.give(k, t)
                ts.append(t)
            for i in range(4):
                k, ps, free = bank()
                t = PE(mms(*sum_jobs(ps[:, 0:256], [(AO[:, g, tok(i)], Wo[:, g, :]) for g in range(4)])), free, ts)
                t = add_to_x(ps[:, 0:256], i, 1, t)
                PB.give(k, t)
            return fence()

        if only[0] <= 7 <= only[1]:
            f = stage_7(f)

        def stage_8(f):
            W, t_w = weights("s8", AR, 0, f)
            t_ht = to_T(H, HT, norm_rows(X, H, None))
            lg, t = logits8(mat(W["rw"], 2), W["rb"], t_ht, t_w)
            oh1, top, t1 = first_of_max(lg, t)
            l2, ex, R, den = sm(4, 8), sm(4, 8), sm(4, 8), sm(4)
            t = DV(lambda: V.tensor_scalar(l2, oh1, -3e38, None, ALU.mult), t1)
            t = DV(lambda: V.tensor_tensor(l2, l2, lg, ALU.add), t)
            oh2, _, t = first_of_max(l2, t)
            t = DV(lambda: V.tensor_tensor(oh2, oh2, oh1, ALU.add), t)
            t2 = DV(lambda: V.tensor_tensor(ex, lg, up8(top), ALU.subtract), t)
            t2 = AC(lambda: A.activation(ex, ex, ACT.Exp), t2)
            t = DV(lambda: V.tensor_tensor(R, ex, oh2, ALU.mult), t2, t)
            t = DV(lambda: V.tensor_reduce(den, R, AX, ALU.add), t)
            t = DV(lambda: V.reciprocal(den, den), t)
            t = DV(lambda: V.tensor_tensor(R, R, up8(den), ALU.mult), t)
            RT = AR[0:8, 9000:9512]
            t = rows8(R, RT, t)
            experts(W, 10, 8, RT, t, t_ht, 9600, False)
            return fence()

        if only[0] <= 8 <= only[1]:
            f = stage_8(f)

        def stage_9(f):
            W, t_w = weights("s9", AR, 0, f)
            o = SPAN["s9"][1]
            QA, CTX = view(AR, o, 4, 512), view(AR, o + 2048, 4, 512)
            PTR = Ring([view(AR, o + 4096 + 512 * k, 2, 256) for k in range(3)])
            MX, NM = view(AR, o + 5632, 2, 4, 8), view(AR, o + 5696, 2, 128)
            RC = view(AR, o + 4096, 2, 512)
            VP = view(CNf, 0, 32, 288)
            KA = view(CNf, 9216, KEYS)
            mr = AR[0:1, o + 5952:o + 5952 + KEYS]
            Wq, Wk, Wv = mat(W["Wq"], 2), mat(W["Wk"], 2), mat(W["Wv"], 2)
            t_ones = [PL(lambda: G.memset(VP, 1.0)), PL(lambda: G.memset(NM, 0.0))]
            t_ht = to_T(H, HT, norm_rows(X, H, None))
            t_q = []
            for g in range(4):
                k, ps, free = bank()
                t = PE(mms(*sum_jobs(ps, [(Wq[:, kt, tok(g)], HT[:, kt, :]) for kt in range(2)])), free, t_ht, t_w)
                t = DV(lambda g=g, ps=ps: V.tensor_scalar(QA[:, g, :], ps, W["bq"][:, g:g + 1], 0.25,
                                                          ALU.add, ALU.mult), t)
                PB.give(k, t)
                t_q.append(t)
            t_c = []
            n = 0
            for b in range(2):
                t_mr = load(mr.bitcast(I32), mask1[b:b + 1, :], f, PE.now() if b else None)
                t_mr = DV(lambda: V.tensor_scalar(mr, mr.bitcast(I32), 0.0, -1e30, ALU.is_gt, ALU.mult), t_mr)
                ctx_of = lambda n, b=b: [CT[:, kt, b * KEYS + n * 128:b * KEYS + n * 128 + 128] for kt in range(2)]
                tv = [values(Wv, ctx_of(m), m, lambda m: VP[:, m, :], W["bv"], [PE.now(), t_w], t_ones) if not b else
                      values(Wv, ctx_of(m), m, lambda m: VP[:, m, :], W["bv"], None, PE_end) for m in range(32)]
                for g in range(4):
                    before = PE.now()
                    tk = []
                    for c in range(8):
                        k, ps, free = bank()
                        jobs = sum_jobs(ps, [(Wk[:, kt, tok(g)], CT[:, kt, b * KEYS + c * 512:b * KEYS + c * 512 + 512])
                                             for kt in range(2)], final=False)
                        jobs.append((ps, W["e17"][0:1, :], mr[:, c * 512:c * 512 + 512], False, True))
                        t = PE(mms(*jobs), free, t_mr)
                        t = AC(lambda c=c, ps=ps, g=g: A.activation(KA[:, c * 512:c * 512 + 512], ps, ACT.Identity,
                                                                    bias=W["bk"][:, g:g + 1]), t, before)
                        PB.give(k, t)
                        tk.append(t)
                    t_m = heads_max(QA, lambda c: KA[:, c * 512:c * 512 + 512], 8, 512, g, b, MX, NM,
                                    tk, t_q, t_ones, before)
                    t_c.append(heads_mix(QA, lambda kt: KA[:, kt * 128:kt * 128 + 128],
                                         lambda kt: VP[:, kt, :], 32, g, b, CTX, PTR, n, t_m, tv, tk))
                    n += 1
                PE_end = PE.now()
            t_n = heads_norm(CTX, RC, W["dsel"], [t_c, PE.now()])
            selc = mat(W["selc"], 4)
            for i in range(4):
                k, ps, free = bank()
                t = PE(mms(*sum_jobs(ps[:, 0:256], [(CTX[:, g, tok(i)], selc[:, g, :]) for g in range(4)])), free, t_n)
                t = add_to_x(ps[:, 0:256], i, 1, t)
                PB.give(k, t)
            return fence()

        if only[0] <= 9 <= only[1]:
            f = stage_9(f)

        def stage_10(f):
            W, t_w = weights("s10", AR, 0, f)
            B0 = CNf
            RQ, RK = view(B0, 0, 2, 512), view(B0, 1024, 2, 512)
            VV, GG, OO = view(B0, 2048, 4, 512), view(B0, 4096, 4, 512), view(B0, 6144, 4, 512)
            AT = view(B0, 8192, 8, 512)
            OT = view(B0, 12288, 4, 512)
            tA, tB = view(B0, 14336, 512), view(B0, 14848, 512)
            t_ht = to_T(H, HT, norm_rows(X, H, None))
            cos = W["cos"].unsqueeze(1).to_broadcast([128, 2, 256])
            sin = W["sin"].unsqueeze(1).to_broadcast([128, 2, 256])
            ts, td = [], None
            for (a, s, dst, sc) in (("Wq", "Wqs", RQ, 0.125), ("Wk", "Wks", RK, 1.0)):
                wa, ws = mat(W[a], 2), mat(W[s], 2)
                for m in range(2):
                    k1, p1, f1 = bank()
                    k2, p2, f2 = bank()
                    t1 = PE(mms(*sum_jobs(p1, [(wa[:, kt, tok(m)], HT[:, kt, :]) for kt in range(2)])), f1, t_ht, t_w)
                    t2 = PE(mms(*sum_jobs(p2, [(ws[:, kt, tok(m)], HT[:, kt, :]) for kt in range(2)])), f2)
                    v2 = lambda p: p.rearrange("p (b t) -> p b t", b=2)
                    t1 = DV(lambda p=p1: V.tensor_tensor(v2(tA), v2(p), cos, ALU.mult), t1, td)
                    PB.give(k1, t1)
                    t2 = DV(lambda p=p2: V.tensor_tensor(v2(tB), v2(p), sin, ALU.mult), t2, td)
                    PB.give(k2, t2)
                    t = DV(lambda: V.tensor_tensor(tA, tA, tB, ALU.add), t1, t2)
                    td = DV(lambda m=m, dst=dst, sc=sc: V.tensor_scalar(dst[:, m, :], tA, sc, None, ALU.mult), t)
                    ts.append(td)
            tv, tg = [], []
            wv, wg = mat(W["Wv"], 2), mat(W["Wg"], 2)
            for i in range(4):
                k, ps, free = bank()
                t = PE(mms(*sum_jobs(ps, [(HT[:, kt, tok(i)], wv[:, kt, :]) for kt in range(2)])), free)
                t = AC(lambda i=i, ps=ps: A.copy(VV[:, i, :], ps), t)
                PB.give(k, t)
                tv.append(t)
                k, ps, free = bank()
                t = PE(mms(*sum_jobs(ps, [(HT[:, kt, tok(i)], wg[:, kt, :]) for kt in range(2)])), free)
                t = AC(lambda i=i, ps=ps: A.activation(GG[:, i, :], ps, ACT.Silu), t)
                PB.give(k, t)
                tg.append(t)
            dec = W["decay"].rearrange("p (j h t) -> p j h t", j=2, h=4)
            ss, rr = sm(4, 4), sm(4, 4)
            t_at = {}
            for b in range(2):
                for h in range(4):
                    r = slice(64 * (h % 2), 64 * (h % 2) + 64)
                    k, ps, free = bank()
                    q = RQ[r, h // 2, b * 256:b * 256 + 256]
                    jobs = [(ps[:, j * 256:j * 256 + 256], RK[r, h // 2, tok(2 * b + j)], q, True, True)
                            for j in range(2)]
                    t = PE(mms(*jobs), free, ts)
                    t = DV(lambda b=b, h=h, ps=ps: V.tensor_tensor(
                        AT[:, 4 * b + h, :].rearrange("p (j t) -> p j t", j=2), ps.rearrange("p (j t) -> p j t", j=2),
                        dec[:, :, h, :], ALU.mult), t, t_w)
                    PB.give(k, t)
                    t_at[b, h] = t
            tn = []
            for i in range(4):
                b, l = i // 2, i % 2
                k, ps, free = bank()
                jobs = []
                for h in range(4):
                    pairs = [(AT[:, 4 * b + h, j * 256 + l * 128:j * 256 + l * 128 + 128],
                              VV[:, 2 * b + j, tok(h)]) for j in range(l + 1)]
                    jobs += sum_jobs(ps[:, tok(h)], pairs)
                t = PE(mms(*jobs), free, tv, [t_at[b, h] for h in range(4)])
                t = DV(lambda i=i, ps=ps: V.tensor_copy(OO[:, i, :], ps), t)
                PB.give(k, t)
                tq_before = AC.now()
                tq = []
                for h in range(4):
                    tq.append(AC(lambda i=i, h=h: A.activation((tA, tB)[i % 2][:, tok(h)], OO[:, i, tok(h)],
                                                               ACT.Square, accum_out=ss[:, i, h:h + 1]), t,
                                 ts, tq_before))
                t2 = rsqrt(rr[:, i, :], ss[:, i, :], 1.0 / 128, 1e-5, tq)
                t3 = DV(lambda i=i: V.tensor_tensor(
                    GG[:, i, :].rearrange("p (h d) -> p h d", h=4), GG[:, i, :].rearrange("p (h d) -> p h d", h=4),
                    W["gn"].unsqueeze(1).to_broadcast([128, 4, 128]), ALU.mult), tg[i])
                for h in range(4):
                    t = DV(lambda i=i, h=h: V.scalar_tensor_tensor(
                        out=OO[:, i, tok(h)], in0=OO[:, i, tok(h)], scalar=rr[:, i, h:h + 1], in1=GG[:, i, tok(h)],
                        op0=ALU.mult, op1=ALU.mult), t2, t3, tq)
                k, ps, free = bank()
                def go(i=i, ps=ps):
                    for h in range(4):
                        z = TE.transpose(ps[:, tok(h)], OO[:, i, tok(h)], ident)
                    return z
                t = PE(go, free, t)
                t = DV(lambda i=i, ps=ps: V.tensor_copy(OT[:, :, tok(i)], ps.rearrange("p (h t) -> p h t", h=4)), t)
                PB.give(k, t)
                tn.append(t)
            wo = mat(W["Wo"], 4)
            for i in range(4):
                k, ps, free = bank()
                t = PE(mms(*sum_jobs(ps[:, 0:256], [(OT[:, h, tok(i)], wo[:, h, :]) for h in range(4)])), free, tn)
                t = add_to_x(ps[:, 0:256], i, 1, t)
                PB.give(k, t)
            return fence()

        if only[0] <= 10 <= only[1]:
            f = stage_10(f)

        def stage_11(f):
            ER = Ring([view(CTf, 4096 * k, 4096) for k in range(4)])
            expert_w = []

            def load_expert(e, *deps):
                s0 = SPAN["s11e"][0] + e * 4096
                kk, w, wf = ER.take()
                return kk, w, load(w, pack[:, s0:s0 + 4096], wf, *deps)
            W, t_w = weights("s11", AR, 0, f)
            for e in range(4):
                expert_w.append(load_expert(e, f))
            B0 = CNf
            X1, X2 = view(B0, 0, 4, 256), view(B0, 1024, 4, 256)
            QA, KA, CTX = view(B0, 2048, 4, 512), view(B0, 4096, 4, 512), view(B0, 6144, 4, 512)
            VP = view(B0, 8192, 4, 288)
            PTR = Ring([view(B0, 9344 + 512 * k, 2, 256) for k in range(3)])
            RC = view(B0, 9344, 2, 512)
            MX, NM = view(B0, 10880, 2, 4, 8), view(B0, 10944, 2, 128)
            HH = [view(B0, 2048, 8, 512), view(AR, 7000, 8, 512)]
            ACC = view(B0, 11264, 4, 256)
            GT = B0[0:8, 12288:12800]
            M1, M2 = view(B0, 12800, 4, 8), view(B0, 12832, 4, 8)
            t_ones = [PL(lambda: G.memset(VP, 1.0)), PL(lambda: G.memset(NM, 0.0))]
            x1 = norm_rows(X, X1, None)

            def affine(g_, b_):
                def post(dst, ps, kt, t):
                    return DV(lambda: V.tensor_scalar(dst, ps, W[g_][:, kt:kt + 1], W[b_][:, kt:kt + 1],
                                                      ALU.mult, ALU.add), t, t_w)
                return post
            t_ht = to_T(H, HT, norm_rows(X1, H, x1), affine("g1", "b1n"))
            wq, wk, wv = mat(W["Wq"], 2), mat(W["Wk"], 2), mat(W["Wv"], 2)
            ts = []
            for w, bias, dst, sc in ((wq, "bq", QA, 0.25), (wk, "bk", KA, 1.0)):
                for g in range(4):
                    k, ps, free = bank()
                    t = PE(mms(*sum_jobs(ps, [(w[:, kt, tok(g)], HT[:, kt, :]) for kt in range(2)])), free, t_ht, t_w)
                    t = DV(lambda g=g, ps=ps, bias=bias, dst=dst, sc=sc: V.tensor_scalar(
                        dst[:, g, :], ps, W[bias][:, g:g + 1], sc, ALU.add, ALU.mult), t)
                    PB.give(k, t)
                    ts.append(t)
            tv = [values(wv, [HT[:, kt, tok(m)] for kt in range(2)], m, lambda m: VP[:, m, :], W["bv"], None, t_ones)
                  for m in range(4)]
            t_c = []
            for b in range(2):
                for g in range(4):
                    t_m = heads_max(QA, lambda c, b=b, g=g: KA[:, g, b * 256:b * 256 + 256], 1, 256, g, b, MX, NM,
                                    ts, t_ones, PE.now())
                    t_c.append(heads_mix(QA, lambda kt, b=b, g=g: KA[:, g, tok(2 * b + kt)],
                                         lambda kt, b=b: VP[:, 2 * b + kt, :], 2, g, b, CTX, PTR, 4 * b + g, t_m, tv))
            t_n = heads_norm(CTX, RC, W["dsel"], [t_c, PE.now()])
            wo = mat(W["Wo"], 4)
            x2 = []
            for i in range(4):
                t0 = PL(lambda i=i: G.tensor_tensor(X1[:, i, :], X1[:, i, :], W["bo"], ALU.add), x1, t_ht)
                k, ps, free = bank()
                t = PE(mms(*sum_jobs(ps[:, 0:256], [(CTX[:, g, tok(i)], wo[:, g, :]) for g in range(4)])), free, t_n)
                t = DV(lambda i=i, ps=ps: V.tensor_tensor(X2[:, i, :], ps[:, 0:256], X1[:, i, :], ALU.add), t, t0)
                PB.give(k, t)
                x2.append(t)
            t_ht = to_T(H, HT, norm_rows(X2, H, x2), affine("g2", "b2n"))
            lg, t = logits8(mat(W["wr"], 2), None, t_ht)
            pr, mxl, den, l2 = sm(4, 8), sm(4), sm(4), sm(4, 8)
            t1 = DV(lambda: V.tensor_reduce(mxl, lg, AX, ALU.max), t)
            t1 = DV(lambda: V.tensor_tensor(pr, lg, up8(mxl), ALU.subtract), t1)
            t1 = AC(lambda: A.activation(pr, pr, ACT.Exp), t1)
            t1 = DV(lambda: V.tensor_reduce(den, pr, AX, ALU.add), t1)
            t1 = DV(lambda: V.reciprocal(den, den), t1)
            t_p = DV(lambda: V.tensor_tensor(pr, pr, up8(den), ALU.mult), t1)
            oh1, _, t1 = first_of_max(pr, t_p)
            t = DV(lambda: V.tensor_scalar(l2, oh1, -3e38, None, ALU.mult), t1)
            t = DV(lambda: V.tensor_tensor(l2, l2, lg, ALU.add), t)
            oh2, _, t = first_of_max(l2, t)
            t1 = DV(lambda: V.tensor_copy(M1, oh1), t1)
            t2 = DV(lambda: V.tensor_copy(M2, oh2), t)
            k, ps, free = bank()
            jobs = []
            for i in range(4):
                prs = [(cst["ones"], M1[:, n, :]) for n in range(i)] + [(cst["triu"], M1[:, i, :])]
                jobs += sum_jobs(ps[:, i * 8:i * 8 + 8], prs)
                prs = [(cst["ones"], M1[:, n, :]) for n in range(4)] + [(cst["ones"], M2[:, n, :]) for n in range(i)] + [
                    (cst["triu"], M2[:, i, :])]
                jobs += sum_jobs(ps[:, 32 + i * 8:40 + i * 8], prs)
            t = PE(mms(*jobs), free, t1, t2)
            k1_, k2_ = sm(4, 8), sm(4, 8)
            v8 = lambda p: p.rearrange("p (a b) -> p a b", b=8)
            ta = DV(lambda ps=ps: V.scalar_tensor_tensor(out=k1_, in0=v8(ps[:, 0:32]), scalar=128.5, in1=oh1,
                                                         op0=ALU.is_lt, op1=ALU.mult), t)
            tb = DV(lambda ps=ps: V.scalar_tensor_tensor(out=k2_, in0=v8(ps[:, 32:64]), scalar=128.5, in1=oh2,
                                                         op0=ALU.is_lt, op1=ALU.mult), t)
            PB.give(k, [ta, tb])
            t = DV(lambda: V.tensor_tensor(k1_, k1_, k2_, ALU.add), ta, tb)
            t = DV(lambda: V.tensor_tensor(k1_, k1_, pr, ALU.mult), t)
            dn = sm(4)
            t = DV(lambda: V.tensor_reduce(dn, k1_, AX, ALU.add), t)
            t = DV(lambda: V.tensor_scalar(dn, dn, float(np.finfo(np.float32).eps), None, ALU.max), t)
            t = DV(lambda: V.reciprocal(dn, dn), t)
            GG = k2_
            t_g = DV(lambda: V.tensor_tensor(GG, k1_, up8(dn), ALU.mult), t)
            t = rows8(GG, GT, t_g)
            ta = []
            for i in range(4):
                k, ps, free = bank()
                tt = PE(mms((ps[:, 0:256], GT[:, tok(i)], W["b2"][0:8, :], True, True)), free, t)
                tt = copy(ACC[:, i, :], ps[:, 0:256], tt)
                PB.give(k, tt)
                ta.append([tt])
            hfree = [None, None]
            for e in range(8):
                kk, w, t_e = expert_w.pop(0)
                w1, w2 = mat(w[:, 0:2048], 2), mat(w[:, 2048:4096], 8)
                hh = HH[e % 2]
                th = []
                for m in range(8):
                    k, ps, free = bank()
                    t = PE(mms(*sum_jobs(ps, [(w1[:, kt, tok(m)], HT[:, kt, :]) for kt in range(2)])), free, t_e, t_ht)
                    c = W["b1"][:, e * 8 + m:e * 8 + m + 1]
                    if m % 2:
                        t = AC(lambda c=c, ps=ps, hh=hh, m=m: A.activation(hh[:, m, :], ps, ACT.Relu, bias=c),
                               t, hfree[e % 2])
                    else:
                        t = DV(lambda c=c, ps=ps, hh=hh, m=m: V.tensor_scalar(hh[:, m, :], ps, c, 0.0, ALU.add, ALU.max),
                               t, hfree[e % 2])
                    PB.give(k, t)
                    th.append(t)
                for i in range(4):
                    k, ps, free = bank()
                    t = PE(mms(*sum_jobs(ps[:, 0:256], [(hh[:, m, tok(i)], w2[:, m, :]) for m in range(8)])), free, th)
                    t2 = DV(lambda i=i, e=e, ps=ps: V.scalar_tensor_tensor(
                        out=ACC[:, i, :], in0=ps[:, 0:256], scalar=GG[:, i, e:e + 1], in1=ACC[:, i, :],
                        op0=ALU.mult, op1=ALU.add), t, ta[i])
                    PB.give(k, t2)
                    ta[i] = [t2]
                hfree[e % 2] = t
                ER.give(kk, t)
                if e + 4 < 8:
                    expert_w.append(load_expert(e + 4))
            for i in range(4):
                t = DV(lambda i=i: V.scalar_tensor_tensor(out=ACC[:, i, :], in0=ACC[:, i, :], scalar=1.0 - 0.2,
                                                          in1=X2[:, i, :], op0=ALU.mult, op1=ALU.add), ta[i])
                DV(lambda i=i: V.tensor_tensor(X[:, i, :], X[:, i, :], ACC[:, i, :], ALU.add), t)
            return fence()

        if only[0] <= 11 <= only[1]:
            f = stage_11(f)

        s_out = ctx.enter_context(nc.semaphore("s_out"))
        block = ctx.enter_context(nc.Block())

        @block.sync
        def _(eng):
            for deps, dst, src, s in SP:
                for ds, v in deps:
                    eng.wait_ge(ds, v)
                eng.dma_start(dst, src).then_inc(s, 16)
            for ds, v in f:
                eng.wait_ge(ds, v)
            eng.dma_start(out.rearrange("b (i p) d -> p (b i) d", p=128), X[:]).then_inc(s_out, 16)
            eng.wait_ge(s_out, 16)

        @block.tensor
        def _(eng):
            PE.emit(eng)

        @block.vector
        def _(eng):
            DV.emit(eng)

        @block.scalar
        def _(eng):
            AC.emit(eng)

        @block.gpsimd
        def _(eng):
            PL.emit(eng)


def _rows_to_partitions(w):
    w = np.asarray(w)
    k = w.shape[0] // 128
    return np.ascontiguousarray(w.reshape(k, 128, -1).transpose(1, 0, 2)).reshape(128, -1)


def _col(v):
    return np.ascontiguousarray(np.asarray(v).reshape(-1, 128).T)


def _row(v, times=1):
    v = np.tile(np.asarray(v), times)
    return np.broadcast_to(v[None, :], (128, v.size))


def _pad_out(w):
    w = np.asarray(w)
    o = np.zeros((w.shape[0], 16, 32), np.float32)
    o[:, :, :16] = w.reshape(w.shape[0], 16, 16)
    return o.reshape(w.shape[0], 512)


def _pad_in(w):
    w = np.asarray(w)
    o = np.zeros((16, 32, w.shape[1]), np.float32)
    o[:, :16] = w.reshape(16, 16, w.shape[1])
    return _rows_to_partitions(o.reshape(512, w.shape[1]))


def _pad_col(v, at, value):
    o = np.zeros((16, 32), np.float32)
    o[:, :16] = np.asarray(v).reshape(16, 16)
    o[:, at] = value
    return _col(o.reshape(512))


def _constants():
    c = {}
    c["ident"] = np.eye(128, dtype=np.float32)
    c["triu"] = np.triu(np.ones((128, 128), np.float32))
    c["iota8"] = _row(np.arange(8, 0, -1).astype(np.float32), 4)
    c["ones"] = np.ones((128, 128), np.float32)
    c["bd16"] = np.kron(np.eye(8), np.ones((16, 16))).astype(np.float32)
    c["bd32"] = np.kron(np.eye(4), np.ones((32, 32))).astype(np.float32)
    s16, s17, ds = (np.zeros((128, 128), np.float32) for _ in range(3))
    selc = np.zeros((128, 4, 256), np.float32)
    for j in range(4):
        s16[32 * j:32 * j + 16, 32 * j + 16] = -0.25
        s17[32 * j:32 * j + 16, 32 * j + 17] = -0.25
        ds[32 * j + 16, 32 * j:32 * j + 32] = 1.0
        for g in range(4):
            for d in range(16):
                selc[32 * j + d, g, (4 * g + j) * 16 + d] = 1.0
    c["sel16"], c["sel17"], c["dsel"], c["selc"] = s16, s17, ds, selc.reshape(128, 1024)
    p = np.arange(128) % 32
    c["c16"] = (p == 16).astype(np.float32)[:, None]
    c["c17"] = (p == 17).astype(np.float32)[:, None]
    c["half"] = np.full((128, 1), 0.5, np.float32)
    e17 = np.zeros((128, 128), np.float32)
    e17[0] = p == 17
    c["e17"] = e17
    esel = np.zeros((128, 8, 128), np.float32)
    for e in range(8):
        esel[e, e, :] = 1.0
    c["esel"] = esel.reshape(128, 1024)
    inv = (1.0 / np.float32(10000.0) ** (np.arange(0, 64, 2, dtype=np.float32) / np.float32(64))).astype(np.float32)
    ang = (np.arange(256, dtype=np.float32)[None, :] * inv[:, None]).astype(np.float32)
    cos, sin = np.cos(ang).astype(np.float32), np.sin(ang).astype(np.float32)
    c["cos"] = np.concatenate([cos, cos, cos, cos])
    c["sin"] = np.concatenate([-sin, sin, -sin, sin])
    gam = (1.0 - np.exp2(-5.0 - np.arange(4, dtype=np.float32))).astype(np.float32)
    d = np.arange(256)[None, :] - np.arange(256)[:, None]
    dec = np.where(d[None] >= 0, gam[:, None, None].astype(np.float64) ** np.maximum(d, 0)[None], 0.0)
    c["decay"] = np.ascontiguousarray(dec.reshape(4, 2, 128, 256).transpose(2, 1, 0, 3)).reshape(128, 2048).astype(np.float32)
    return c


def _pack(a):
    R = _rows_to_partitions
    c = _constants()
    g = {}

    def put(stage, **kw):
        for k, v in kw.items():
            g[stage, k] = v

    L = "L0_xattn_"
    put("s0", Wq=R(a[L + "Wq"]), Wk=R(a[L + "Wk"].T), Wv=R(a[L + "Wv"]), Wo=R(a[L + "Wo"]), bq=_col(a[L + "bq"]),
        bk=_col(a[L + "bk"]), bv=_col(a[L + "bv"]), bo=_row(a[L + "bo"]))
    L = "L0_attn_"
    put("s1", qkv=R(a[L + "qkv_w"].T), proj=R(a[L + "proj_w"].T), conv1=R(a[L + "conv1_w"].T),
        conv2=R(a[L + "conv2_w"].T), s1=_col(a[L + "scale1"]), s2=_col(a[L + "scale2"]), gamma=_row(a[L + "gamma"]),
        pb=_row(a[L + "proj_b"]), c1b=_col(a[L + "conv1_b"]), c2b=_row(a[L + "conv2_b"]))
    L = "L0_ffn_"
    put("s2", w1=R(a[L + "w1_w"].T), w2=R(a[L + "w2_w"].T), w3=R(a[L + "w3_w"].T), w1s=_col(a[L + "w1_s"]),
        w2s=_col(a[L + "w2_s"]), h1s=_col(a[L + "h1_s"]), h2s=_col(a[L + "h2_s"]), w3s=_row(a[L + "w3_s"]))
    for l, n in enumerate(("h1_w", "h2_w")):
        w = a[L + n].T
        for m in range(8):
            g["s2h", f"h{8 * l + m}"] = R(w[:, m * 128:m * 128 + 128])
    for st, L in (("s3", "L1_xattn_"), ("s6", "L2_xattn_")):
        put(st, Wq=R(a[L + "Wq"].T), Wk=R(a[L + "Wk"]), Wv=R(a[L + "Wv"].T), bq=_col(a[L + "bq"]),
            bk=_col(a[L + "bk"]), bv=_row(a[L + "bv"]))
    L = "L1_attn_"
    put("s4", Wq=R(a[L + "Wq"].T), Wk=R(a[L + "Wk"].T), Wv=R(a[L + "Wv"].T),
        gamma=np.broadcast_to(a[L + "gamma"].reshape(1, 1), (128, 1)))
    L = "L1_ffn_"
    put("s5", gate=R(a[L + "gate_w"].T))
    for e in range(8):
        put("s5", **{f"g{e}": R(a[L + "w_gate"][e].T), f"u{e}": R(a[L + "w_up"][e].T), f"d{e}": a[L + "w_down"][e].T})
    L = "L2_attn_"
    put("s7", Wkp=R(_pad_out(a[L + "W_k"].T)), Wk=R(a[L + "W_k"].T), Wvp=R(_pad_out(a[L + "W_v"].T)),
        Wo=_pad_in(a[L + "W_o"].T))
    L = "L2_ffn_"
    put("s8", rw=R(a[L + "router_w"]), rb=_row(a[L + "router_b"], 4))
    for e in range(10):
        k, n = ("routed", e) if e < 8 else ("shared", e - 8)
        put("s8", **{f"g{e}": R(a[f"{L}{k}_w1"][n]), f"u{e}": R(a[f"{L}{k}_w3"][n]), f"d{e}": a[f"{L}{k}_w2"][n]})
    L = "L3_xattn_"
    put("s9", Wq=R(_pad_out(a[L + "q_w"].T)), Wk=R(_pad_out(a[L + "k_w"].T)), Wv=R(a[L + "v_w"].T),
        bq=_pad_col(a[L + "q_b"], 17, 4.0), bk=_pad_col(a[L + "k_b"], 16, -1.0), bv=_row(a[L + "v_b"]))
    L = "L3_attn_"

    def swap(w):
        return np.ascontiguousarray(w.reshape(4, 2, 32, 256)[:, ::-1]).reshape(256, 256)
    put("s10", Wq=R(a[L + "Wq"].T), Wqs=R(swap(a[L + "Wq"]).T), Wk=R(a[L + "Wk"].T), Wks=R(swap(a[L + "Wk"]).T),
        Wv=R(a[L + "Wv"].T), Wg=R(a[L + "Wg"].T), Wo=R(a[L + "Wo"].T), gn=_row(a[L + "gnorm_w"]))
    L = "L3_ffn_"
    b2 = np.zeros((128, 256), np.float32)
    b2[:8] = a[L + "b2"]
    put("s11", Wq=R(_pad_out(a[L + "wq"])), Wk=R(_pad_out(a[L + "wk"])), Wv=R(a[L + "wv"]), Wo=_pad_in(a[L + "wo"]),
        bq=_pad_col(a[L + "bq"], 17, 0.0), bk=_pad_col(a[L + "bk"], 16, -1.0), bv=_row(a[L + "bv"]), bo=_row(a[L + "bo"]),
        g1=_col(a[L + "ln1_g"]), b1n=_col(a[L + "ln1_b"]), g2=_col(a[L + "ln2_g"]), b2n=_col(a[L + "ln2_b"]),
        wr=R(a[L + "wr"]), b1=_col(a[L + "b1"].reshape(-1)), b2=b2)
    for e in range(8):
        put("s11e", **{f"w1_{e}": R(a[L + "w1"][e]), f"w2_{e}": R(a[L + "w2"][e])})
    out = np.empty((128, TOTAL), np.float32)
    for stage, entries in PACK.items():
        for name, cols in entries:
            o, _ = WHERE[stage, name]
            v = g[stage, name] if (stage, name) in g else c[name]
            s = SPAN[stage][0] + o
            assert v.shape == (128, cols), (stage, name, v.shape, cols)
            out[:, s:s + cols] = v
    return out


def build(nc, arrays, only=(0, 99)):
    args = [nc.dram_tensor(n, a.shape, mybir.dt.from_np(a.dtype), kind="ExternalInput").ap()
            for n, a in arrays.items()]
    out = nc.dram_tensor("out_dram", (2, 256, 256), F32, kind="ExternalOutput").ap()
    perceiver(nc, *args, out, only=only)


def lay_out(inputs):
    a = {k: np.asarray(v) for k, v in inputs.items()}
    ctxt = a["ctx_1024"].reshape(8192, 256)
    return {
        "pack": _pack(a),
        "x_in": np.ascontiguousarray(a["x"]),
        "ctx_n": np.ascontiguousarray(ctxt.reshape(64, 128, 256).transpose(1, 0, 2)),
        "ctx_t": np.ascontiguousarray(ctxt.reshape(8192, 2, 128).transpose(2, 1, 0)),
        "mask0": np.ascontiguousarray(a["mask_BxS2_bk0"]).view(np.int32),
        "mask1": np.ascontiguousarray(a["mask_BxS2_ik0"]),
    }


def kernel(**inputs):
    import concourse.bacc as _bacc
    from concourse.bass_utils import run_bass_kernel_spmd as _run

    nc = _bacc.Bacc("TRN2", target_bir_lowering=False, num_devices=1)
    arrays = lay_out(inputs)
    build(nc, arrays)
    r = _run(nc, [arrays], core_ids=[0])
    return r.results[0]["out_dram"]
```

```python
from contextlib import ExitStack

import numpy as np

import concourse.bass as bass
from concourse import mybir

ALU = mybir.AluOpType
ACT = mybir.ActivationFunctionType
F32 = mybir.dt.float32
BF16 = mybir.dt.bfloat16
U8 = mybir.dt.uint8
I32 = mybir.dt.int32
AX = mybir.AxisListType.X

T = 512
KEYS = 4096
BIG = float(2 ** 30)

PACK = {
    "c": [("ident", 128), ("triu", 128), ("iota8", 32), ("ones", 128)],
    "s0": [("Wq", 512), ("Wk", 512), ("Wv", 512), ("Wo", 512), ("bq", 2), ("bk", 2), ("bv", 2), ("bo", 256)],
    "s1": [("qkv", 1536), ("proj", 512), ("conv1", 1024), ("conv2", 1024), ("s1", 2), ("s2", 2),
           ("gamma", 256), ("pb", 256), ("c1b", 4), ("c2b", 256), ("bd16", 128)],
    "s2": [("w1", 2048), ("w2", 2048), ("w3", 2048), ("w1s", 8), ("w2s", 8), ("h1s", 8), ("h2s", 8), ("w3s", 256)],
    "s2h": [(f"h{i}", 1024) for i in range(16)],
    "s3": [("Wq", 512), ("Wk", 512), ("Wv", 512), ("bq", 2), ("bk", 2), ("bv", 256)],
    "s4": [("Wq", 512), ("Wk", 512), ("Wv", 512), ("gamma", 1)],
    "s5": [("gate", 16), ("esel", 1024)] + [(f"{k}{e}", 256) for e in range(8) for k in ("g", "u", "d")],
    "s6": [("Wq", 512), ("Wk", 512), ("Wv", 512), ("bq", 2), ("bk", 2), ("bv", 256)],
    "s7": [("Wkp", 1024), ("Wk", 512), ("Wvp", 1024), ("Wo", 1024), ("bd32", 128), ("sel16", 128),
           ("sel17", 128), ("dsel", 128), ("c16", 1), ("c17", 1), ("half", 1)],
    "s8": [("rw", 16), ("rb", 32), ("esel", 1024)] + [(f"{k}{e}", 256) for e in range(10) for k in ("g", "u", "d")],
    "s9": [("Wq", 512), ("Wk", 512), ("Wv", 512), ("bq", 2), ("bk", 2), ("bv", 256), ("sum17", 17)],
    "s10": [("Wq", 512), ("Wqs", 512), ("Wk", 512), ("Wks", 512), ("Wv", 1024), ("Wg", 1024), ("Wo", 1024),
            ("gn", 128), ("cos", 256), ("sin", 256), ("decay", 2048)],
    "s11": [("Wq", 1024), ("Wk", 1024), ("Wv", 512), ("Wo", 1024), ("bq", 4), ("bk", 4), ("bv", 256), ("bo", 256),
            ("g1", 2), ("b1n", 2), ("g2", 256), ("b2n", 256), ("wr", 16), ("b1", 64), ("b2", 256), ("dsel", 128),
            ("iota", 128)],
    "s11e": [(f"{k}{e}", 2048) for e in range(8) for k in ("w1_", "w2_")],
}


def places():
    at, where, span = 0, {}, {}
    for stage, entries in PACK.items():
        start = at
        for name, cols in entries:
            where[stage, name] = (at - start, cols)
            at += cols
        span[stage] = (start, at - start)
    return where, span, at


WHERE, SPAN, TOTAL = places()


class Queue:

    def __init__(self, sem):
        self.sem, self.ops, self.n, self.seen, self.pending = sem, [], 0, {}, []

    def __call__(self, fn, *deps):
        need = {}
        for s, v in flat(deps) + self.pending:
            if v > max(self.seen.get(s, 0), need.get(s, 0)):
                need[s] = v
        self.pending = []
        self.seen.update(need)
        self.n += 1
        self.ops.append((list(need.items()), fn))
        return (self.sem, self.n)

    def now(self):
        return (self.sem, self.n)

    def emit(self, eng):
        for waits, fn in self.ops:
            for s, v in waits:
                eng.wait_ge(s, v)
            fn().then_inc(self.sem, 1)


def flat(deps):
    out = []
    for d in deps:
        if d is None:
            continue
        if isinstance(d, list):
            out += flat(d)
        else:
            out.append(d)
    return out


class Ring:

    def __init__(self, slots):
        self.slots, self.free, self.i = slots, [None] * len(slots), 0

    def take(self):
        k = self.i % len(self.slots)
        self.i += 1
        return k, self.slots[k], self.free[k]

    def give(self, k, tok):
        self.free[k] = tok


def perceiver(nc, pack, x_in, ctx_n, ctx_t, mask0, mask1, out, only=(0, 99)):
    with ExitStack() as ctx:
        def sb(name, shape, dt=F32):
            return ctx.enter_context(nc.sbuf_tensor(name, shape, dt))

        PS = ctx.enter_context(nc.psum_tensor("PS", [128, 8, 512], F32))
        CT = sb("CT", [128, 2, 8192])
        CN = sb("CN", [128, 64, 256])
        X = sb("X", [128, 4, 256])
        H = sb("H", [128, 4, 256])
        HT = sb("HT", [128, 2, 512])
        CST = sb("CST", [128, SPAN["c"][1]])
        SM = sb("SM", [128, 1200])
        AR = sb("AR", [128, 15640])
        CNf = CN[:].rearrange("p a b -> p (a b)")
        CTf = CT[:].rearrange("p a b -> p (a b)")

        sems = {n: ctx.enter_context(nc.semaphore("s_" + n)) for n in ("pe", "dve", "act", "pool")}
        PE, DV, AC, PL = (Queue(sems[n]) for n in ("pe", "dve", "act", "pool"))
        V, A, G, TE = nc.vector, nc.scalar, nc.gpsimd, nc.tensor
        SP = []
        count = [0]

        def load(dst, src, *deps):
            count[0] += 1
            s = ctx.enter_context(nc.semaphore(f"d{count[0]}"))
            SP.append((flat(deps), dst, src, s))
            return (s, 16)

        sm_at = [0]

        def fence():
            sm_at[0] = 0
            now = [q.now() for q in (PE, DV, AC, PL) if q.n]
            for q in (PE, DV, AC, PL):
                q.pending = list(now)
            return now



        def sm(*shape):
            n = int(np.prod(shape))
            a = SM[:, sm_at[0]:sm_at[0] + n]
            sm_at[0] += n
            if len(shape) == 2:
                a = a.rearrange("p (a b) -> p a b", b=shape[1])
            if len(shape) == 3:
                a = a.rearrange("p (a b c) -> p a b c", b=shape[1], c=shape[2])
            return a

        def view(base, off, *shape):
            n = int(np.prod(shape))
            a = base[:, off:off + n]
            if len(shape) == 2:
                a = a.rearrange("p (a b) -> p a b", b=shape[1])
            if len(shape) == 3:
                a = a.rearrange("p (a b c) -> p a b c", b=shape[1], c=shape[2])
            if len(shape) == 4:
                a = a.rearrange("p (a b c d) -> p a b c d", b=shape[1], c=shape[2], d=shape[3])
            return a

        def weights(stage, base, off, *deps, shapes=()):
            start, n = SPAN[stage]
            tok = load(base[:, off:off + n], pack[:, start:start + n], *deps)
            got = {}
            for name, cols in PACK[stage]:
                o, c = WHERE[stage, name]
                got[name] = base[:, off + o:off + o + c]
            return got, tok

        def mat(a, kt):
            return a.rearrange("p (k o) -> p k o", k=kt)

        def tok(i):
            return slice(i * 128, i * 128 + 128)

        def mms(*jobs):
            def go():
                for o, l, r, a, z in jobs:
                    last = TE.matmul(o, l, r, start=a, stop=z, skip_group_check=True)
                return last
            return go

        def sum_jobs(o, pairs, first=True, final=True):
            n = len(pairs)
            return [(o, l, r, first and k == 0, final and k == n - 1) for k, (l, r) in enumerate(pairs)]

        cst, t_cst = weights("c", CST, 0)
        ident = cst["ident"]
        PB = Ring([0, 1, 2, 3, 4, 5])
        t_x = load(X[:], x_in.rearrange("b (i p) d -> p (b i) d", p=128))

        def bank():
            k, b, dep = PB.take()
            return k, PS[:, b, :], dep

        both = [0]

        def copy(o, i, *deps):
            both[0] ^= 1
            if both[0]:
                return DV(lambda: V.tensor_copy(o, i), *deps)
            return AC(lambda: A.copy(o, i), *deps)

        def to_T(src, dst, deps, post=None):
            ts = []
            for i in range(4):
                k, ps, free = bank()
                def go(i=i, ps=ps):
                    TE.transpose(ps[:, 0:128], src[:, i, 0:128], ident)
                    return TE.transpose(ps[:, 128:256], src[:, i, 128:256], ident)
                t = PE(go, free, deps[i], t_cst)
                if post is None:
                    t = copy(dst[:, :, tok(i)], ps[:, 0:256].rearrange("p (k t) -> p k t", k=2), t)
                    ts.append(t)
                    PB.give(k, t)
                else:
                    t = [post(dst[:, kt, tok(i)], ps[:, kt * 128:kt * 128 + 128], kt, t) for kt in range(2)]
                    ts.append(t)
                    PB.give(k, t)
            return ts

        def rsqrt(dst, src, scale, eps, *deps):
            t = DV(lambda: V.tensor_scalar(dst, src, scale, eps, ALU.mult, ALU.add), *deps)
            t = DV(lambda: V.reciprocal(dst, dst), t)
            return AC(lambda: A.activation(dst, dst, ACT.Sqrt), t)

        def norm_rows(src, dst, deps, eps=1e-5):
            st, mv, rs = sm(4, 6), sm(4, 2), sm(4)
            ts = []
            for i in range(4):
                t = DV(lambda i=i: V.bn_stats(st[:, i, :], src[:, i, :]), deps)
                ts.append(DV(lambda i=i: V.bn_aggr(mv[:, i, :], st[:, i, :]), t))
            t = rsqrt(rs, mv[:, :, 1], 1.0, eps, ts)
            return [DV(lambda i=i: V.tensor_scalar(dst[:, i, :], src[:, i, :], mv[:, i, 0:1], rs[:, i:i + 1],
                                                   ALU.subtract, ALU.mult), t) for i in range(4)]

        def rms_rows(src, dst, junk, deps):
            ss, rs = sm(4), sm(4)
            ts = [AC(lambda i=i: A.activation(junk[:, i, :], src[:, i, :], ACT.Square, accum_out=ss[:, i:i + 1]), deps)
                  for i in range(4)]
            t = rsqrt(rs, ss, 1.0, 0.0, ts)
            return [DV(lambda i=i: V.tensor_scalar(dst[:, i, :], src[:, i, :], rs[:, i:i + 1], None, ALU.mult),
                       t, ts[i]) for i in range(4)]

        def add_to_x(ps, i, n, t):
            v = X[:, i:i + n, :].rearrange("p a b -> p (a b)")
            return DV(lambda: V.tensor_tensor(v, ps, v, ALU.add), t)

        def add_row_x(row, *deps):
            return [PL(lambda i=i: G.tensor_tensor(X[:, i, :], X[:, i, :], row, ALU.add), *deps) for i in range(4)]

        def xattn(stage, W, t_w, scale, t_ct, t_cn, masks, last):
            hs = norm_rows(X, H, t_x_now[0])
            t_ht = to_T(H, HT, hs)
            Wq, Wk, Wv = (mat(W[k], 2) for k in ("Wq", "Wk", "Wv"))
            S = [view(AR, 4096 * k, KEYS) for k in range(2)]
            PTR = Ring([view(AR, 8192 + 512 * k, 512) for k in range(4)])
            QT, Q2 = view(AR, 8192, 2, 512), view(AR, 9216, 2, 512)
            OT, CX = HT, H[:].rearrange("p a b -> p (a b)").rearrange("p (k t) -> p k t", k=2)
            t_q = []
            for m in range(2):
                k, ps, free = bank()
                t = PE(mms(*sum_jobs(ps, [(Wq[:, kt, tok(m)], HT[:, kt, :]) for kt in range(2)])), free, t_ht, t_w)
                t = DV(lambda m=m, ps=ps: V.tensor_scalar(QT[:, m, :], ps, W["bq"][:, m:m + 1], scale,
                                                          ALU.add, ALU.mult), t)
                PB.give(k, t)
                t_q.append(t)
            cadd = sm(4)
            k, ps, free = bank()
            jobs = []
            for i in range(4):
                jobs += sum_jobs(ps[:, i:i + 1], [(QT[:, m, tok(i)], W["bk"][:, m:m + 1]) for m in range(2)])
            t = PE(mms(*jobs), free, t_q)
            t_c = DV(lambda ps=ps: V.tensor_copy(cadd, ps[:, 0:4]), t)
            PB.give(k, t_c)
            t_q2 = []
            for m in range(2):
                k, ps, free = bank()
                t = PE(mms(*sum_jobs(ps, [(Wk[:, h, tok(m)], QT[:, h, :]) for h in range(2)])), free, t_q)
                t = AC(lambda m=m, ps=ps: A.copy(QN[:, m, :], ps), t, t_q)
                PB.give(k, t)
                t_q2.append(t)
            q_done = PE.now()

            t_s, s_free, mx, nb, rs, ri = {}, [None, masks[1] if masks else None], sm(4), sm(4), sm(4), sm(4)
            t_pt_first = q_done

            def scores(i):
                b = i // 2
                ts = []
                for c in range(8):
                    k, ps, free = bank()
                    rhs = [CT[:, kt, b * KEYS + c * 512:b * KEYS + c * 512 + 512] for kt in range(2)]
                    t = PE(mms(*sum_jobs(ps, [(QN[:, kt, tok(i)], rhs[kt]) for kt in range(2)])),
                           free, t_q2, t_ct[b * 4 + c // 2])
                    o = S[i % 2][:, c * 512:c * 512 + 512]
                    if masks:
                        m = masks[0][:, c * 512:c * 512 + 512]
                        t = DV(lambda o=o, ps=ps, m=m, i=i: V.scalar_tensor_tensor(
                            out=o, in0=ps, scalar=cadd[:, i:i + 1], in1=m, op0=ALU.add, op1=ALU.min),
                            t, t_c, masks[1 + b], s_free[i % 2])
                    elif c % 4 == 3:
                        t = DV(lambda o=o, ps=ps, i=i: V.tensor_scalar(o, ps, cadd[:, i:i + 1], None, ALU.add),
                               t, t_c, s_free[i % 2])
                    else:
                        t = AC(lambda o=o, ps=ps, i=i: A.activation(o, ps, ACT.Identity, bias=cadd[:, i:i + 1]),
                               t, t_c, s_free[i % 2])
                    PB.give(k, t)
                    ts.append(t)
                if masks and i == 1:
                    masks.append(masks_next(DV.now()))
                t = DV(lambda: V.tensor_reduce(mx[:, i:i + 1], S[i % 2], AX, ALU.max), ts)
                t = DV(lambda: V.tensor_scalar(nb[:, i:i + 1], mx[:, i:i + 1], -1.0, None, ALU.mult), t)
                t = AC(lambda: A.activation(S[i % 2], S[i % 2], ACT.Exp, bias=nb[:, i:i + 1],
                                            accum_out=rs[:, i:i + 1]), t, ts)
                t_s[i] = t
                return DV(lambda: V.reciprocal(ri[:, i:i + 1], rs[:, i:i + 1]), t)

            masks_next = masks.pop() if masks else None
            t_r, t_o, o_free = {}, [], [None, None]
            t_r[0] = scores(0)
            for i in range(4):
                if i + 1 < 4:
                    t_r[i + 1] = scores(i + 1)
                b = i // 2
                O = PS[:, 6 + i % 2, 0:256]

                def turn(c, i=i):
                    k, ps, free = bank()
                    def go():
                        for y in range(4):
                            u = c * 4 + y
                            l = TE.transpose(ps[:, y * 128:y * 128 + 128], S[i % 2][:, u * 128:u * 128 + 128], ident)
                        return l
                    t = PE(go, free, t_s[i])
                    kk, pt, pfree = PTR.take()
                    t = copy(pt, ps, t, pfree, t_pt_first)
                    PB.give(k, t)
                    return kk, pt, t
                nxt = [turn(0), turn(1)]
                for c in range(8):
                    kk, pt, t = nxt.pop(0)
                    if c + 2 < 8:
                        nxt.append(turn(c + 2))
                    jobs = [(O, pt[:, y * 128:y * 128 + 128], CN[:, b * 32 + c * 4 + y, :],
                             c == 0 and y == 0, c == 7 and y == 3) for y in range(4)]
                    t = PE(mms(*jobs), t, t_cn[b * 2 + c // 4], o_free[i % 2])
                    PTR.give(kk, t)
                s_free[i % 2] = t
                t = DV(lambda i=i, O=O: V.tensor_scalar(OB[:, i, :], O, ri[:, i:i + 1], None, ALU.mult), t, t_r[i])
                o_free[i % 2] = t
                t_o.append(t)
            t_ot = to_T(OB, OT, t_o)
            if "Wo" in W:
                Wo = mat(W["Wo"], 2)
                t_row = add_row_x(W["bo"], hs, t_w)
                tc = []
                for m in range(2):
                    k, ps, free = bank()
                    t = PE(mms(*sum_jobs(ps, [(Wv[:, kt, tok(m)], OT[:, kt, :]) for kt in range(2)])), free, t_ot)
                    t = DV(lambda m=m, ps=ps: V.tensor_scalar(CX[:, m, :], ps, W["bv"][:, m:m + 1], None, ALU.add),
                           t, t_ot)
                    PB.give(k, t)
                    tc.append(t)
                src, Wf = CX, Wo
            else:
                t_row = add_row_x(W["bv"], hs, t_w)
                src, Wf, tc = OT, Wv, t_ot
            for i in range(4):
                k, ps, free = bank()
                t = PE(mms(*sum_jobs(ps[:, 0:256], [(src[:, kt, tok(i)], Wf[:, kt, :]) for kt in range(2)])), free, tc)
                t = add_to_x(ps[:, 0:256], i, 1, [t, t_row[i]])
                PB.give(k, t)

        QN = HT
        OB = H
        t_x_now = [t_x]

        W0, t_w0 = weights("s0", AR, 12288)
        MB = view(AR, 10240, 2048).bitcast(BF16)
        MW = [view(AR, 4096, 1024).bitcast(I32), view(AR, 14600, 1024).bitcast(I32)]
        MU = [w.bitcast(U8) for w in MW]
        t_ct, t_cn = [], []
        t_mu = [load(MW[b], mask0[b:b + 1, :].partition_broadcast(128)) for b in range(2)]
        for q in range(4):
            t_ct.append(load(CT[:, :, q * 1024:q * 1024 + 1024], ctx_t[:, :, q * 1024:q * 1024 + 1024]))
        for q in range(2):
            t_cn.append(load(CN[:, q * 16:q * 16 + 16, :], ctx_n[:, q * 16:q * 16 + 16, :]))
        for q in range(4, 8):
            t_ct.append(load(CT[:, :, q * 1024:q * 1024 + 1024], ctx_t[:, :, q * 1024:q * 1024 + 1024]))
        for q in range(2, 4):
            t_cn.append(load(CN[:, q * 16:q * 16 + 16, :], ctx_n[:, q * 16:q * 16 + 16, :]))

        def bounds(b, *deps):
            return DV(lambda: V.tensor_scalar(MB, MU[b], 2 * BIG, -BIG, ALU.mult, ALU.add), t_mu[b], *deps)

        if only[0] <= 0 <= only[1]:
            xattn("s0", W0, t_w0, 1.0 / 16, t_ct, t_cn,
                  [MB, bounds(0), lambda d: bounds(1, d)], None)
        f = fence()

        def stage_1(f):
            W, t_w = weights("s1", AR, 0, f)
            o = SPAN["s1"][1]
            hs = norm_rows(X, H, None)
            Y, Z = view(AR, o, 4, 256), view(AR, o + 1024, 4, 256)
            ZT = HT
            OT = view(AR, o + 2048, 2, 512)
            QF = view(AR, o + 3072, 2, 512)
            KV = view(AR, o + 4096, 4, 512)
            HD = view(AR, o + 6144, 4, 512)
            KM = view(AR, o + 6144, 2, 2, 128)
            KS = view(AR, o + 6656, 2, 2, 128)
            tmp = view(AR, o + 7168, 2, 512)
            qkv, proj, conv1, conv2 = mat(W["qkv"], 2), mat(W["proj"], 2), mat(W["conv1"], 2), mat(W["conv2"], 4)

            def scaled(col):
                def post(dst, ps, kt, t):
                    return DV(lambda: V.tensor_scalar(dst, ps, col[:, kt:kt + 1], 16.0 + 1e-6, ALU.mult, ALU.mult),
                              t, t_w)
                return post
            rs = rms_rows(H, Z, Y, hs)
            t_zt = to_T(Z, ZT, rs, scaled(W["s1"]))
            t_qf = []
            for m in range(2):
                k, ps, free = bank()
                t = PE(mms(*sum_jobs(ps, [(qkv[:, kt, tok(m)], ZT[:, kt, :]) for kt in range(2)])), free, t_zt)
                t = AC(lambda m=m, ps=ps: A.activation(QF[:, m, :], ps, ACT.Square), t)
                PB.give(k, t)
                t_qf.append(AC(lambda m=m: A.activation(QF[:, m, :], QF[:, m, :], ACT.Exp, scale=-0.5), t))
            t_kv = []
            for i in range(4):
                k, ps, free = bank()
                t = PE(mms(*sum_jobs(ps, [(ZT[:, kt, tok(i)], qkv[:, kt, 256:768]) for kt in range(2)])), free, t_zt)
                t1 = AC(lambda i=i, ps=ps: A.activation(KV[:, i, 0:256], ps[:, 0:256], ACT.Square), t)
                t2 = DV(lambda i=i, ps=ps: V.tensor_copy(KV[:, i, 256:512], ps[:, 256:512]), t1)
                PB.give(k, [t1, t2])
                t_kv.append([t2, AC(lambda i=i: A.activation(KV[:, i, 0:256], KV[:, i, 0:256], ACT.Exp, scale=-0.5),
                                    t1)])
            ksum = sm(4)
            t_at = []
            ones = cst["ones"]
            for b in range(2):
                for m in range(2):
                    k, ps, free = bank()
                    jobs = sum_jobs(ps[:, 0:128], [(KV[:, 2 * b + i, tok(m)], KV[:, 2 * b + i, 256 + m * 128:384 + m * 128])
                                                   for i in range(2)])
                    jobs += sum_jobs(ps[:, 128:129], [(KV[:, 2 * b + i, tok(m)], ones[:, 0:1]) for i in range(2)])
                    t = PE(mms(*jobs), free, t_kv[2 * b], t_kv[2 * b + 1])
                    t1 = DV(lambda b=b, m=m, ps=ps: V.tensor_tensor(KM[:, b, m, :], ps[:, 0:128], W["bd16"], ALU.mult), t)
                    c = ksum[:, 2 * b + m:2 * b + m + 1]
                    t2 = DV(lambda c=c, ps=ps: V.tensor_copy(c, ps[:, 128:129]), t)
                    PB.give(k, [t1, t2])
                    t2 = DV(lambda b=b, m=m, c=c: V.tensor_scalar(KS[:, b, m, :], W["bd16"], c, None, ALU.mult), t2)
                    q = QF[:, m, b * 256:b * 256 + 256]
                    k, ps, free = bank()
                    t = PE(mms((ps[:, 0:256], KM[:, b, m, :], q, True, True),
                               (ps[:, 256:512], KS[:, b, m, :], q, True, True)), free, t1, t2, t_qf)
                    w = tmp[:, m, 0:256]
                    t = DV(lambda w=w, ps=ps: V.tensor_scalar(w, ps[:, 256:512], 1e-6, None, ALU.add), t)
                    t = DV(lambda w=w: V.reciprocal(w, w), t)
                    t = DV(lambda b=b, m=m, ps=ps, w=w: V.tensor_tensor(OT[:, m, b * 256:b * 256 + 256], ps[:, 0:256],
                                                                        w, ALU.mult), t)
                    PB.give(k, t)
                    t_at.append(t)
            ty = []
            for i in range(4):
                k, ps, free = bank()
                t = PE(mms(*sum_jobs(ps[:, 0:256], [(OT[:, m, tok(i)], proj[:, m, :]) for m in range(2)])), free, t_at)
                y = Y[:, i, :]
                t = DV(lambda y=y, ps=ps: V.tensor_tensor(y, ps[:, 0:256], W["pb"], ALU.add), t)
                PB.give(k, t)
                t = DV(lambda y=y: V.tensor_tensor(y, y, W["gamma"], ALU.mult), t)
                ty.append(DV(lambda y=y, i=i: V.tensor_tensor(y, y, H[:, i, :], ALU.add), t))
            rs = rms_rows(Y, Z, H, ty)
            t_zt = to_T(Z, ZT, rs, scaled(W["s2"]))
            th = []
            for m in range(4):
                k, ps, free = bank()
                t = PE(mms(*sum_jobs(ps, [(conv1[:, kt, tok(m)], ZT[:, kt, :]) for kt in range(2)])), free, t_zt)
                t = AC(lambda m=m, ps=ps: A.activation(HD[:, m, :], ps, ACT.Gelu, bias=W["c1b"][:, m:m + 1]), t, t_at)
                PB.give(k, t)
                th.append(t)
            for i in range(4):
                k, ps, free = bank()
                t = PE(mms(*sum_jobs(ps[:, 0:256], [(HD[:, m, tok(i)], conv2[:, m, :]) for m in range(4)])), free, th)
                z = Z[:, i, :]
                t = DV(lambda z=z, ps=ps: V.tensor_tensor(z, ps[:, 0:256], W["c2b"], ALU.add), t)
                PB.give(k, t)
                t = DV(lambda z=z: V.tensor_tensor(z, z, W["gamma"], ALU.mult), t)
                t = DV(lambda z=z, i=i: V.tensor_tensor(z, z, Y[:, i, :], ALU.add), t)
                DV(lambda z=z, i=i: V.tensor_tensor(X[:, i, :], X[:, i, :], z, ALU.add), t)
            return fence()

        if only[0] <= 1 <= only[1]:
            f = stage_1(f)

        def stage_2(f):
            W, t_w = weights("s2", AR, 8192, f)
            hA, hB = view(AR, 0, 8, 512), view(AR, 4096, 8, 512)
            w1, w2, w3 = mat(W["w1"], 2), mat(W["w2"], 2), mat(W["w3"], 8)
            t_ht = to_T(H, HT, norm_rows(X, H, None))
            ts = []
            for m in range(8):
                k1, p1, f1 = bank()
                ta = PE(mms(*sum_jobs(p1, [(w1[:, kt, tok(m)], HT[:, kt, :]) for kt in range(2)])), f1, t_ht, t_w)
                k2, p2, f2 = bank()
                tb = PE(mms(*sum_jobs(p2, [(w2[:, kt, tok(m)], HT[:, kt, :]) for kt in range(2)])), f2)
                ta = AC(lambda m=m, p=p1: A.activation(hB[:, m, :], p, ACT.Silu, scale=W["w1s"][:, m:m + 1]), ta)
                PB.give(k1, ta)
                tb = DV(lambda m=m, p=p2: V.scalar_tensor_tensor(out=hA[:, m, :], in0=p, scalar=W["w2s"][:, m:m + 1],
                                                                 in1=hB[:, m, :], op0=ALU.mult, op1=ALU.mult), ta, tb)
                PB.give(k2, tb)
                ts.append(tb)
            ring = Ring([view(AR, 8192 + 1024 * k, 8, 128) for k in range(4)])
            over = PE.now()
            src, dst = hA, hB
            for layer in range(2):
                nts = []
                for m in range(8):
                    kk, w, wf = ring.take()
                    n = layer * 8 + m
                    s0 = SPAN["s2h"][0] + n * 1024
                    t_l = load(w.rearrange("p a b -> p (a b)"), pack[:, s0:s0 + 1024], over if wf is None else wf)
                    k, ps, free = bank()
                    t = PE(mms(*sum_jobs(ps, [(w[:, kt, :], src[:, kt, :]) for kt in range(8)])), free, t_l, ts)
                    ring.give(kk, t)
                    t = AC(lambda m=m, ps=ps, dst=dst, s=W["h1s" if layer == 0 else "h2s"]: A.activation(
                        dst[:, m, :], ps, ACT.Gelu, scale=s[:, m:m + 1]), t, ts)
                    PB.give(k, t)
                    nts.append(t)
                src, dst, ts = dst, src, nts
            for i in range(4):
                k, ps, free = bank()
                t = PE(mms(*sum_jobs(ps[:, 0:256], [(src[:, m, tok(i)], w3[:, m, :]) for m in range(8)])), free, ts)
                o = H[:, i, :]
                t = DV(lambda o=o, ps=ps: V.tensor_tensor(o, ps[:, 0:256], W["w3s"], ALU.mult), t)
                PB.give(k, t)
                DV(lambda o=o, i=i: V.tensor_tensor(X[:, i, :], X[:, i, :], o, ALU.add), t)
            return fence()

        if only[0] <= 2 <= only[1]:
            f = stage_2(f)

        def stage_3(f):
            W, t_w = weights("s3", AR, 12288, f)
            t_x_now[0] = None
            xattn("s3", W, t_w, 1.0, t_ct, t_cn, [], None)
            return fence()

        if only[0] <= 3 <= only[1]:
            f = stage_3(f)

        def stage_4(f):
            W, t_w = weights("s4", AR, 0, f)
            hs = norm_rows(X, H, None)
            t_ht = to_T(H, HT, hs)
            FT, GT = view(AR, 2048, 2, 512), view(AR, 3072, 2, 512)
            HV = view(AR, 4096, 4, 256)
            P, PT = view(AR, 5120, 4, 256), view(AR, 6144, 4, 256)
            Wq, Wk, Wv = (mat(W[k], 2) for k in ("Wq", "Wk", "Wv"))
            ts = []
            for w, o in ((Wq, FT), (Wk, GT)):
                for m in range(2):
                    k, ps, free = bank()
                    t = PE(mms(*sum_jobs(ps, [(w[:, kt, tok(m)], HT[:, kt, :]) for kt in range(2)])), free, t_ht, t_w)
                    t = copy(o[:, m, :], ps, t)
                    PB.give(k, t)
                    ts.append(t)
            tv = []
            for i in range(4):
                k, ps, free = bank()
                t = PE(mms(*sum_jobs(ps[:, 0:256], [(HT[:, kt, tok(i)], Wv[:, kt, :]) for kt in range(2)])), free)
                t = copy(HV[:, i, :], ps[:, 0:256], t)
                PB.give(k, t)
                tv.append(t)
            mx, nb, rs, ri = sm(4), sm(4), sm(4), sm(4)
            for i in range(4):
                b = i // 2
                k, ps, free = bank()
                t = PE(mms(*sum_jobs(ps[:, 0:256], [(GT[:, m, tok(i)], FT[:, m, b * 256:b * 256 + 256])
                                                    for m in range(2)])), free, ts)
                t1 = DV(lambda i=i, ps=ps: V.tensor_reduce(mx[:, i:i + 1], ps[:, 0:256], AX, ALU.max), t)
                t1 = DV(lambda i=i: V.tensor_scalar(nb[:, i:i + 1], mx[:, i:i + 1], -1.0, None, ALU.mult), t1)
                t1 = AC(lambda i=i, ps=ps: A.activation(P[:, i, :], ps[:, 0:256], ACT.Exp, bias=nb[:, i:i + 1],
                                                        accum_out=rs[:, i:i + 1]), t1)
                PB.give(k, t1)
                t2 = DV(lambda i=i: V.reciprocal(ri[:, i:i + 1], rs[:, i:i + 1]), t1)
                k, ps, free = bank()
                def go(i=i, ps=ps):
                    TE.transpose(ps[:, 0:128], P[:, i, 0:128], ident)
                    return TE.transpose(ps[:, 128:256], P[:, i, 128:256], ident)
                t = PE(go, free, t1)
                t = copy(PT[:, i, :], ps[:, 0:256], t)
                PB.give(k, t)
                k, ps, free = bank()
                t = PE(mms(*sum_jobs(ps[:, 0:256], [(PT[:, i, tok(y)], HV[:, 2 * b + y, :]) for y in range(2)])),
                       free, t, tv)
                p = P[:, i, :]
                t = DV(lambda i=i, ps=ps, p=p: V.tensor_scalar(p, ps[:, 0:256], ri[:, i:i + 1], W["gamma"],
                                                               ALU.mult, ALU.mult), t, t2)
                PB.give(k, t)
                t = DV(lambda i=i, p=p: V.tensor_tensor(p, p, H[:, i, :], ALU.add), t)
                DV(lambda i=i, p=p: V.tensor_tensor(X[:, i, :], X[:, i, :], p, ALU.add), t)
            return fence()

        if only[0] <= 4 <= only[1]:
            f = stage_4(f)

        def first_of_max(src, *deps):
            top, w, m, oh = sm(4), sm(4, 8), sm(4), sm(4, 8)
            up = lambda a: a.unsqueeze(2).to_broadcast([128, 4, 8])
            t = DV(lambda: V.tensor_reduce(top, src, AX, ALU.max), *deps)
            t = DV(lambda: V.tensor_tensor(w, src, up(top), ALU.is_equal), t)
            t = DV(lambda: V.tensor_tensor(w, w, cst["iota8"].rearrange("p (a b) -> p a b", b=8), ALU.mult), t)
            t = DV(lambda: V.tensor_reduce(m, w, AX, ALU.max), t)
            t = DV(lambda: V.tensor_tensor(oh, w, up(m), ALU.is_equal), t)
            return oh, top, t

        def logits8(w, row, *deps):
            lg = sm(4, 8)
            k, ps, free = bank()
            jobs = []
            for i in range(4):
                jobs += sum_jobs(ps[:, i * 8:i * 8 + 8], [(HT[:, kt, tok(i)], w[:, kt, :]) for kt in range(2)])
            t = PE(mms(*jobs), free, *deps)
            p = ps[:, 0:32].rearrange("p (a b) -> p a b", b=8)
            if row is None:
                t = DV(lambda: V.tensor_copy(lg, p), t)
            else:
                t = DV(lambda: V.tensor_tensor(lg, p, row.rearrange("p (a b) -> p a b", b=8), ALU.add), t)
            PB.give(k, t)
            return lg, t

        def rows8(R, dst, *deps):
            k, ps, free = bank()
            def go():
                for i in range(4):
                    l = TE.transpose(ps[0:8, tok(i)], R[:, i, :], ident)
                return l
            t = PE(go, free, *deps)
            t = DV(lambda: V.tensor_copy(dst, ps[0:8, :]), t)
            PB.give(k, t)
            return t

        def up8(a):
            return a.unsqueeze(2).to_broadcast([128, 4, 8])

        def experts(W, n, n_gated, RT, t_rt, t_ht, work, gate_first):
            acc = [PS[:, 6 + i // 2, (i % 2) * 256:(i % 2) * 256 + 256] for i in range(4)]
            esel = W["esel"]
            rb_r = Ring([view(AR, work + 512 * k, 512) for k in range(2)])
            g_r = Ring([view(AR, work + 1024 + 512 * k, 512) for k in range(2)])
            h_r = Ring([view(AR, work + 2048 + 512 * k, 512) for k in range(3)])
            pend = []

            def down(e, hk, h, t):
                wd = W[f"d{e}"]
                jobs = [(acc[i], h[:, tok(i)], wd, e == 0 and i % 2 == 0, e == n - 1) for i in range(4)]
                t = PE(mms(*jobs), t)
                h_r.give(hk, t)
                return t
            for e in range(n):
                wg, wu = mat(W[f"g{e}"], 2), mat(W[f"u{e}"], 2)
                gated = e < n_gated
                tr = None
                if gated:
                    k, ps, free = bank()
                    t = PE(mms((ps, esel[0:8, e * 128:e * 128 + 128], RT, True, True)), free, t_rt)
                    rk, rb, rf = rb_r.take()
                    tr = AC(lambda rb=rb, ps=ps: A.copy(rb, ps), t, rf)
                    PB.give(k, tr)
                k1, p1, f1 = bank()
                ta = PE(mms(*sum_jobs(p1, [(wg[:, kt, :], HT[:, kt, :]) for kt in range(2)])), f1, t_ht)
                k2, p2, f2 = bank()
                tb = PE(mms(*sum_jobs(p2, [(wu[:, kt, :], HT[:, kt, :]) for kt in range(2)])), f2)
                gk, g, gf = g_r.take()
                hk, h, hf = h_r.take()
                if gate_first:
                    ta = DV(lambda p1=p1, g=g, rb=rb: V.tensor_tensor(g, p1, rb, ALU.mult), ta, tr, gf)
                    PB.give(k1, ta)
                    ta = AC(lambda g=g: A.activation(g, g, ACT.Silu), ta)
                    tb = DV(lambda p2=p2, h=h, rb=rb: V.tensor_tensor(h, p2, rb, ALU.mult), tb, tr, hf)
                    PB.give(k2, tb)
                    rb_r.give(rk, tb)
                    tb = DV(lambda g=g, h=h: V.tensor_tensor(h, h, g, ALU.mult), ta, tb)
                    g_r.give(gk, tb)
                else:
                    ta = AC(lambda p1=p1, g=g: A.activation(g, p1, ACT.Silu), ta, gf)
                    PB.give(k1, ta)
                    tb = DV(lambda p2=p2, h=h, g=g: V.tensor_tensor(h, p2, g, ALU.mult), tb, ta, hf)
                    PB.give(k2, tb)
                    g_r.give(gk, tb)
                    if gated:
                        tb = DV(lambda h=h, rb=rb: V.tensor_tensor(h, h, rb, ALU.mult), tb, tr)
                        rb_r.give(rk, tb)
                pend.append((e, hk, h, tb))
                if len(pend) > 1:
                    down(*pend.pop(0))
            t = down(*pend.pop(0))
            add_to_x(PS[:, 6, :], 0, 2, t)
            add_to_x(PS[:, 7, :], 2, 2, t)

        def stage_5(f):
            W, t_w = weights("s5", AR, 0, f)
            t_ht = to_T(H, HT, norm_rows(X, H, None))
            lg, t = logits8(mat(W["gate"], 2), None, t_ht, t_w)
            oh, top, t = first_of_max(lg, t)
            rw, R = sm(4), sm(4, 8)
            t = AC(lambda: A.activation(rw, top, ACT.Sigmoid), t)
            t = DV(lambda: V.tensor_tensor(R, oh, up8(rw), ALU.mult), t)
            RT = AR[0:8, 8000:8512]
            t = rows8(R, RT, t)
            experts(W, 8, 8, RT, t, t_ht, 8600, True)
            return fence()

        if only[0] <= 5 <= only[1]:
            f = stage_5(f)

        def stage_6(f):
            W, t_w = weights("s6", AR, 12288, f)
            xattn("s6", W, t_w, 4.0, t_ct, t_cn, [], None)
            return fence()

        if only[0] <= 6 <= only[1]:
            f = stage_6(f)

        def heads_max(QA, kcols, nch, width, g, b, MX, NM, *deps):
            ts = []
            for i in range(2):
                tt = tok(2 * b + i)
                for c in range(nch):
                    for j in range(4):
                        r = slice(32 * j, 32 * j + 32)
                        k, ps, free = bank()
                        t = PE(mms((ps[:, 0:width], QA[r, g, tt], kcols(c)[r], True, True)), free, *deps)
                        t = DV(lambda i=i, j=j, c=c, ps=ps: V.tensor_reduce(MX[:, i, j, c:c + 1], ps[:, 0:width],
                                                                            AX, ALU.max), t, *deps)
                        PB.give(k, t)
                        ts.append(t)
            out_ts = []
            for i in range(2):
                nm = NM[:, i, :].rearrange("p (j r) -> p j r", j=4)[:, :, 16]
                out_ts.append(DV(lambda i=i, nm=nm: V.tensor_reduce(nm, MX[:, i, :, 0:nch], AX, ALU.max), ts))
            last_mm = PE.now()
            for i in range(2):
                k, ps, free = bank()
                t = PE(lambda i=i, ps=ps: TE.transpose(ps[:, 0:128], NM[:, i, :], ident), free, out_ts[i])
                q = QA[:, g, tok(2 * b + i)]
                t = DV(lambda q=q, ps=ps: V.tensor_tensor(q, ps[:, 0:128], q, ALU.add), t, last_mm)
                PB.give(k, t)
                out_ts[i] = t
            return out_ts

        def heads_mix(QA, krow, vrow, nkt, g, b, CTX, PTR, cb, *deps):
            C = PS[:, 6 + cb % 2, 0:256]
            pend = []

            def pv(kt, jj, kk, pt, t):
                jobs = []
                for y in range(2):
                    j = 2 * jj + y
                    h = 4 * g + j
                    jobs.append((C[32 * j:32 * j + 32, :], vrow(kt)[:, 17 * h:17 * h + 32], pt[:, y, :],
                                 kt == 0, kt == nkt - 1))
                t = PE(mms(*jobs), t, c_free[cb % 2])
                PTR.give(kk, t)
                return t
            for kt in range(nkt):
                for jj in range(2):
                    k, ps2, free = pair()
                    jobs = []
                    for y in range(2):
                        r = slice(32 * (2 * jj + y), 32 * (2 * jj + y) + 32)
                        jobs.append((ps2[:, y, 0:256], krow(kt)[r], QA[r, g, b * 256:b * 256 + 256], True, True))
                    t = PE(mms(*jobs), free, *deps)
                    kk, pt, pf = PTR.take()
                    t = AC(lambda ps2=ps2, pt=pt: A.activation(pt, ps2[:, :, 0:256], ACT.Exp), t, pf)
                    give_pair(k, t)
                    pend.append((kt, jj, kk, pt, t))
                    if len(pend) > 2:
                        pv(*pend.pop(0))
            while pend:
                t = pv(*pend.pop(0))
            t = DV(lambda: V.tensor_copy(CTX[:, g, b * 256:b * 256 + 256], C), t)
            c_free[cb % 2] = t
            return t

        c_free = [None, None]
        pair_i = [0]

        def pair():
            k = pair_i[0] % 3
            pair_i[0] += 1
            return k, PS[:, 2 * k:2 * k + 2, :], [PB.free[2 * k], PB.free[2 * k + 1]]

        def give_pair(k, t):
            PB.free[2 * k] = PB.free[2 * k + 1] = t

        def heads_norm(CTX, RC, dsel, t_c):
            ts = []
            for g in range(4):
                k, ps, free = bank()
                t = PE(mms((ps, dsel, CTX[:, g, :], True, True)), free, t_c)
                t = DV(lambda g=g, ps=ps: V.reciprocal(RC[:, g % 2, :], ps), t)
                PB.give(k, t)
                ts.append(DV(lambda g=g: V.tensor_tensor(CTX[:, g, :], CTX[:, g, :], RC[:, g % 2, :], ALU.mult), t))
            return ts

        def values(W_, HTs, n, vrow, row, t_dep, t_ones):
            k, ps, free = bank()
            t = PE(mms(*sum_jobs(ps[:, 0:256], [(HTs[kt], W_[:, kt, :]) for kt in range(2)])), free, t_dep)
            o = vrow(n)[:, 0:272].rearrange("p (h r) -> p h r", r=17)[:, :, 0:16]
            p = ps[:, 0:256].rearrange("p (h r) -> p h r", r=16)
            if row is None:
                t = DV(lambda: V.tensor_copy(o, p), t, t_ones)
            else:
                t = DV(lambda: V.tensor_tensor(o, p, row.rearrange("p (h r) -> p h r", r=16), ALU.add), t, t_ones)
            PB.give(k, t)
            return t

        def stage_7(f):
            W, t_w = weights("s7", AR, 0, f)
            o = SPAN["s7"][1]
            KA, QA, CTX = view(AR, o, 4, 512), view(AR, o + 2048, 4, 512), view(AR, o + 4096, 4, 512)
            VP = view(AR, o + 6144, 4, 288)
            PTR = Ring([view(AR, o + 7296 + 512 * k, 2, 256) for k in range(3)])
            QP, SQ = view(AR, o + 8832, 512), view(AR, o + 9344, 512)
            BD = view(AR, o + 8832, 4, 128)
            RC = view(AR, o + 7296, 2, 512)
            Wkp, Wk, Wvp, Wo = mat(W["Wkp"], 2), mat(W["Wk"], 2), mat(W["Wvp"], 2), mat(W["Wo"], 4)
            t_ones = PL(lambda: G.memset(VP, 1.0))
            t_ht = to_T(H, HT, norm_rows(X, H, None))
            t_a = []
            td = None
            for g in range(4):
                k, ps, free = bank()
                t = PE(mms(*sum_jobs(ps, [(Wkp[:, kt, tok(g)], HT[:, kt, :]) for kt in range(2)])), free, t_ht, t_w)
                t1 = DV(lambda ps=ps: V.tensor_copy(QP, ps), t, td)
                t2 = AC(lambda ps=ps: A.activation(SQ, ps, ACT.Square), t1, td)
                PB.give(k, [t1, t2])
                k1, p1, f1 = bank()
                k2, p2, f2 = bank()
                t = PE(mms((p1, W["sel16"], SQ, True, True), (p2, W["sel17"], SQ, True, True)), f1, f2, t1, t2)
                ta = DV(lambda g=g, p=p1: V.scalar_tensor_tensor(out=KA[:, g, :], in0=p, scalar=W["c17"], in1=QP,
                                                                 op0=ALU.add, op1=ALU.add), t, t1)
                PB.give(k1, ta)
                tb = DV(lambda: V.tensor_scalar(SQ, QP, W["half"], W["c16"], ALU.mult, ALU.add), t, t1)
                tb = DV(lambda g=g, p=p2: V.tensor_tensor(QA[:, g, :], p, SQ, ALU.add), tb)
                PB.give(k2, tb)
                t_a += [ta, tb]
                td = [ta, tb]
            for g in range(4):
                k, ps, free = bank()
                t = PE(mms(*sum_jobs(ps[:, 0:128], [(Wkp[:, kt, tok(g)], Wvp[:, kt, tok(g)]) for kt in range(2)])), free)
                t = DV(lambda g=g, ps=ps: V.tensor_tensor(BD[:, g, :], ps[:, 0:128], W["bd32"], ALU.mult), t, td)
                PB.give(k, t)
            t_bd = t
            tv = [values(Wk, [HT[:, kt, tok(n)] for kt in range(2)], n, lambda n: VP[:, n, :], None, None, t_ones)
                  for n in range(4)]
            t_c = []
            for b in range(2):
                for g in range(4):
                    t_c.append(heads_mix(QA, lambda kt, b=b, g=g: KA[:, g, tok(2 * b + kt)],
                                         lambda kt, b=b: VP[:, 2 * b + kt, :], 2, g, b, CTX, PTR, 4 * b + g, t_a, tv))
            t_n = heads_norm(CTX, RC, W["dsel"], [t_c, PE.now()])
            AO = QA
            ts = []
            for g in range(4):
                k, ps, free = bank()
                t = PE(mms((ps, BD[:, g, :], CTX[:, g, :], True, True)), free, t_n[g], t_bd)
                t = AC(lambda g=g, ps=ps: A.mul(AO[:, g, :], ps, 0.25), t)
                PB.give(k, t)
                ts.append(t)
            for i in range(4):
                k, ps, free = bank()
                t = PE(mms(*sum_jobs(ps[:, 0:256], [(AO[:, g, tok(i)], Wo[:, g, :]) for g in range(4)])), free, ts)
                t = add_to_x(ps[:, 0:256], i, 1, t)
                PB.give(k, t)
            return fence()

        if only[0] <= 7 <= only[1]:
            f = stage_7(f)

        def stage_8(f):
            W, t_w = weights("s8", AR, 0, f)
            t_ht = to_T(H, HT, norm_rows(X, H, None))
            lg, t = logits8(mat(W["rw"], 2), W["rb"], t_ht, t_w)
            oh1, top, t1 = first_of_max(lg, t)
            l2, ex, R, den = sm(4, 8), sm(4, 8), sm(4, 8), sm(4)
            t = DV(lambda: V.tensor_scalar(l2, oh1, -3e38, None, ALU.mult), t1)
            t = DV(lambda: V.tensor_tensor(l2, l2, lg, ALU.add), t)
            oh2, _, t = first_of_max(l2, t)
            t = DV(lambda: V.tensor_tensor(oh2, oh2, oh1, ALU.add), t)
            t2 = DV(lambda: V.tensor_tensor(ex, lg, up8(top), ALU.subtract), t)
            t2 = AC(lambda: A.activation(ex, ex, ACT.Exp), t2)
            t = DV(lambda: V.tensor_tensor(R, ex, oh2, ALU.mult), t2, t)
            t = DV(lambda: V.tensor_reduce(den, R, AX, ALU.add), t)
            t = DV(lambda: V.reciprocal(den, den), t)
            t = DV(lambda: V.tensor_tensor(R, R, up8(den), ALU.mult), t)
            RT = AR[0:8, 9000:9512]
            t = rows8(R, RT, t)
            experts(W, 10, 8, RT, t, t_ht, 9600, False)
            return fence()

        if only[0] <= 8 <= only[1]:
            f = stage_8(f)

        def stage_9(f):
            W, t_w = weights("s9", AR, 0, f)
            o = SPAN["s9"][1]
            ROWS = (0, 0, 0, 1, 1, 2)
            COLS = (0, 1, 2, 0, 1, 0)
            VP = view(CNf, 0, 32, 288)
            KSL = [view(CNf, 9216 + 2048 * k, 2048).bitcast(BF16) for k in range(3)]
            KSL.append(view(AR, o, 2048).bitcast(BF16))
            o += 2048
            QS = view(AR, o, 4096).bitcast(BF16).rearrange("p (h t) -> p h t", h=16)
            o += 4096
            QP = view(AR, o, 1536).bitcast(BF16).rearrange("p (s m t) -> p s m t", s=3, m=2)
            o += 1536
            PTR = Ring([view(AR, o + 1024 * k, 4, 256) for k in range(3)])
            KST = Ring([view(AR, o + 1536 * k, 1536).bitcast(BF16).rearrange("p (s t) -> p s t", s=3)
                        for k in range(2)])
            o += 3072
            RT = Ring([view(AR, o + 512 * k, 512) for k in range(2)])
            CXR = Ring([view(AR, o + 1024 + 256 * k, 256) for k in range(2)])
            o += 1536
            MM = view(AR, o, 256).bitcast(BF16).rearrange("p (a i r) -> p a i r", a=2, i=2)
            MI = view(AR, o + 256, 64).bitcast(I32)
            MB = view(AR, o + 320, 32).bitcast(BF16)
            IDB = view(AR, o + 352, 64).bitcast(BF16)
            assert o + 416 <= 15640
            Wq, Wk, Wv = mat(W["Wq"], 2), mat(W["Wk"], 2), mat(W["Wv"], 2)
            kd = nc.dram_tensor("k_parts", (3, 2, 256, KEYS), BF16, kind="Internal").ap()
            qd = nc.dram_tensor("q_parts", (3, 256, 512), BF16, kind="Internal").ap()
            md = nc.dram_tensor("mask_row", (2, KEYS), BF16, kind="Internal").ap()
            t_mi = load(MI.rearrange("p (b t) -> p b t", b=2), mask1.rearrange("b (p t) -> p b t", p=128), f)
            t_mb = DV(lambda: V.tensor_scalar(MB, MI, 0.0, -1e30, ALU.is_gt, ALU.mult), t_mi)
            t_md = load(md.rearrange("b (p t) -> p b t", p=128), MB.rearrange("p (b t) -> p b t", b=2), t_mb)
            t_idb = DV(lambda: V.tensor_copy(IDB, ident))
            t_init = [PL(lambda: G.memset(VP, 1.0)), DV(lambda: V.memset(MM, 0.0))]
            t_init.append(DV(lambda: V.memset(MM[:, :, :, 96], 1.0), t_init[1]))
            t_rows = [DV(lambda: V.memset(QS[96:99], 0.0))]
            t_rows.append(DV(lambda: V.memset(QS[96:97], 1.0), t_rows[0]))
            t_rows += [PL(lambda ks=ks: G.memset(ks[96:99], -1.0), PL.now()) for ks in KSL]

            def split(x, parts, bias, scale, t, *deps):
                rk, r, rf = RT.take()
                ta = DV(lambda: V.tensor_scalar(r, x, bias, scale, ALU.add, ALU.mult), t, rf)
                t1 = AC(lambda: A.copy(parts[0], r), ta, *deps)
                t2 = DV(lambda: V.tensor_tensor(r, r, parts[0], ALU.subtract), t1)
                t3 = AC(lambda: A.copy(parts[1], r), t2, *deps)
                t4 = PL(lambda: G.tensor_tensor(parts[2], r, parts[1], ALU.subtract), t3, PL.now(), *deps)
                RT.give(rk, t4)
                return ta, [t1, t3, t4]

            t_kd = {}
            for b in range(2):
                for m in range(2):
                    for c in range(4):
                        sk, st, sf = KST.take()
                        ts = []
                        for y in range(2):
                            s0 = b * KEYS + c * 1024 + y * 512
                            k, ps, free = bank()
                            t = PE(mms(*sum_jobs(ps, [(Wk[:, kt, tok(m)], CT[:, kt, s0:s0 + 512])
                                                      for kt in range(2)])), free, t_w)
                            ta, tt = split(ps, [st[:, s, y * 512:y * 512 + 512] for s in range(3)],
                                           W["bk"][:, m:m + 1], 1.0, t, sf)
                            PB.give(k, ta)
                            ts += tt
                        t = load(kd[:, b, m * 128:m * 128 + 128, c * 1024:c * 1024 + 1024].rearrange("s p t -> p s t"),
                                 st, ts)
                        KST.give(sk, t)
                        t_kd.setdefault((b, m), []).append(t)
            t_stage = KST.free

            hs = norm_rows(X, H, None)
            t_ht = to_T(H, HT, hs)
            tq = []
            for m in range(2):
                k, ps, free = bank()
                t = PE(mms(*sum_jobs(ps, [(Wq[:, kt, tok(m)], HT[:, kt, :]) for kt in range(2)])), free, t_ht)
                ta, tt = split(ps, [QP[:, s, m, :] for s in range(3)], W["bq"][:, m:m + 1], 0.25, t)
                PB.give(k, ta)
                tq += tt
            t = [load(qd[s].rearrange("(m p) t -> p m t", p=128), QP[:, s], tq) for s in range(3)]
            t_qs = [load(QS[16 * r:16 * r + 16], qd[s].rearrange("(h d) t -> d h t", d=16), t)
                    for r, s in enumerate(COLS)]

            def values_of(b, n, *deps):
                s0 = b * KEYS + n * 128
                return values(Wv, [CT[:, kt, s0:s0 + 128] for kt in range(2)], n, lambda n: VP[:, n, :], W["bv"],
                              list(deps), t_init)

            ksem = [ctx.enter_context(nc.semaphore(f"ks{k}")) for k in range(4)]
            kuse = [0, 0, 0, 0]
            t_ks = {}
            heads = [(b, h) for b in range(2) for h in range(16)]

            def fetch(n, *deps):
                b, h = heads[n]
                k = n % 4
                for r, s in enumerate(ROWS):
                    SP.append((flat([t_kd[b, h // 8], t_rows, list(deps)]), KSL[k][16 * r:16 * r + 16],
                               kd[s, b, 16 * h:16 * h + 16, :], ksem[k]))
                SP.append((flat([t_md, t_rows]), KSL[k][96:97], md[b:b + 1, :], ksem[k]))
                kuse[k] += 1
                t_ks[n] = (ksem[k], 16 * 7 * kuse[k])

            for n in range(4):
                fetch(n)
            t_v = [values_of(0, n) for n in range(32)]

            MX, mxs = sm(2, 2, 8), sm(2, 2)
            P1 = Ring([0, 1])
            P1.free = [PB.free[0], PB.free[1]]
            ST = Ring([2, 4])
            ST.free = [[PB.free[2], PB.free[3]], [PB.free[4], PB.free[5]]]
            CB = Ring([6, 7])
            t_red, t_aux, t_st = {}, {}, {}
            mm_free, t_mm = [None, None], [None, None]

            def best(n, u):
                b, h = heads[n]
                i, c = u // 8, u % 8
                k, bk, free = P1.take()
                ps = PS[:, bk, :]
                t = PE(mms((ps, QS[0:97, h, tok(2 * b + i)], KSL[n % 4][0:97, c * 512:c * 512 + 512], True, True)),
                       free, t_ks[n], t_qs, t_rows)
                t = DV(lambda: V.tensor_reduce(MX[:, n % 2, i, c:c + 1], ps, AX, ALU.max), t, t_red.get((n - 2, "all")))
                P1.give(k, t)
                t_red.setdefault(n, []).append(t)

            def best_rows(n):
                a = n % 2
                m = mxs[:, a, :]
                t = DV(lambda: V.tensor_reduce(m, MX[:, a], AX, ALU.max), t_red[n])
                t_red[n, "all"] = t
                t = DV(lambda: V.tensor_copy(MM[:, a, :, 97], m), t, t_init, mm_free[a])
                t_mm[a] = DV(lambda: V.tensor_tensor(MM[:, a, :, 98], m, MM[:, a, :, 97], ALU.subtract), t)

            def turn_rows(n):
                b, h = heads[n]
                a = n % 2
                t = t_mm[a]
                k, bk, free = P1.take()
                pb = PS[:, bk, 0:128].bitcast(BF16)
                def go():
                    TE.transpose(pb[:, 0:128], MM[:, a, 0, :], IDB)
                    return TE.transpose(pb[:, 128:256], MM[:, a, 1, :], IDB)
                t = PE(go, free, t, t_idb)
                mm_free[a] = t
                t = DV(lambda: V.tensor_copy(QS[96:99, h, b * 256:b * 256 + 256], pb[96:99, :]), t)
                P1.give(k, t)
                t_aux[n] = t

            def close_head(n, cb, ck, t):
                C = PS[:, cb, 0:256]
                xk, cx, xf = CXR.take()
                t = AC(lambda: A.copy(cx, C), t, xf)
                CB.give(ck, t)
                return n, xk, cx, t

            def finish_head(n, xk, cx, t):
                b, h = heads[n]
                k, bk, free = P1.take()
                ps = PS[:, bk, 0:34].rearrange("p (i r) -> p i r", i=2)
                t = PE(mms(*[(ps[:, i, :], cx[:, tok(i)], W["sum17"], True, True) for i in range(2)]), free, t)
                CXR.give(xk, t)
                ri = sm(2)
                t = DV(lambda: V.reciprocal(ri, ps[:, :, 16]), t)
                for i in range(2):
                    x = X[:, 2 * b + i, 16 * h:16 * h + 16]
                    t = DV(lambda i=i, x=x: V.scalar_tensor_tensor(out=x, in0=ps[:, i, 0:16], scalar=ri[:, i:i + 1],
                                                                   in1=x, op0=ALU.mult, op1=ALU.add), t, hs)
                P1.give(k, t)

            for n in range(2):
                for u in range(16):
                    best(n, u)
            best_rows(0)
            turn_rows(0)
            pend = []
            late = None

            def mix(n, s, kk, pt, t, cb, ck, cf):
                h = heads[n][1]
                jobs = [(PS[32 * y:32 * y + 32, cb, 0:256], VP[:, 4 * s + y, 17 * h:17 * h + 32], pt[:, y, :],
                         s == 0, s == 7) for y in range(4)]
                t = PE(mms(*jobs), t, cf, t_v)
                PTR.give(kk, t)
                return t

            for n in range(32):
                b, h = heads[n]
                if n == 16:
                    while pend:
                        args = pend.pop(0)
                        t = mix(*args)
                        if args[1] == 7:
                            finish_head(*close_head(args[0], args[5], args[6], t))
                    over = PE.now()
                    t_v = []
                    for m in range(32):
                        k, bk, free = P1.take()
                        ps = PS[:, bk, 0:256]
                        s0 = KEYS + m * 128
                        t = PE(mms(*sum_jobs(ps, [(CT[:, kt, s0:s0 + 128], Wv[:, kt, :]) for kt in range(2)])), free)
                        ov = VP[:, m, 0:272].rearrange("p (h r) -> p h r", r=17)[:, :, 0:16]
                        t = DV(lambda ov=ov, ps=ps: V.tensor_tensor(
                            ov, ps.rearrange("p (h r) -> p h r", r=16),
                            W["bv"].rearrange("p (h r) -> p h r", r=16), ALU.add), t, over)
                        P1.give(k, t)
                        t_v.append(t)
                ck, cb, cf = CB.take()
                for s in range(8):
                    k, bk, free = ST.take()
                    jobs = [(PS[:, bk + y // 2, (y % 2) * 256:(y % 2) * 256 + 256],
                             KSL[n % 4][0:99, (4 * s + y) * 128:(4 * s + y) * 128 + 128],
                             QS[0:99, h, b * 256:b * 256 + 256], True, True) for y in range(4)]
                    t = PE(mms(*jobs), free, t_aux[n])
                    st = t
                    kk, pt, pf = PTR.take()
                    t = AC(lambda bk=bk, pt=pt: A.activation(
                        pt, PS[:, bk:bk + 2, :].rearrange("p a (c q) -> p (a c) q", c=2), ACT.Exp), t, pf, t_stage)
                    ST.give(k, t)
                    pend.append((n, s, kk, pt, t, cb, ck, cf))
                    if n + 2 < 32:
                        best(n + 2, 2 * s)
                        best(n + 2, 2 * s + 1)
                    if s == 0 and n + 1 < 32:
                        best_rows(n + 1)
                    if s == 2 and n + 1 < 32:
                        turn_rows(n + 1)
                    if late and s == 4:
                        finish_head(*late)
                        late = None
                    if len(pend) > 2:
                        args = pend.pop(0)
                        t = mix(*args)
                        if args[1] == 7:
                            late = close_head(args[0], args[5], args[6], t)
                if n + 4 < 32:
                    fetch(n + 4, st)
            while pend:
                args = pend.pop(0)
                t = mix(*args)
                if args[1] == 7:
                    if late:
                        finish_head(*late)
                    late = close_head(args[0], args[5], args[6], t)
            finish_head(*late)
            return fence()

        if only[0] <= 9 <= only[1]:
            f = stage_9(f)

        def stage_10(f):
            W, t_w = weights("s10", AR, 0, f)
            B0 = CNf
            RQ, RK = view(B0, 0, 2, 512), view(B0, 1024, 2, 512)
            VV, GG, OO = view(B0, 2048, 4, 512), view(B0, 4096, 4, 512), view(B0, 6144, 4, 512)
            AT = view(B0, 8192, 8, 512)
            OT = view(B0, 12288, 4, 512)
            tA, tB = view(B0, 14336, 512), view(B0, 14848, 512)
            t_ht = to_T(H, HT, norm_rows(X, H, None))
            cos = W["cos"].unsqueeze(1).to_broadcast([128, 2, 256])
            sin = W["sin"].unsqueeze(1).to_broadcast([128, 2, 256])
            ts, td = [], None
            for (a, s, dst, sc) in (("Wq", "Wqs", RQ, 0.125), ("Wk", "Wks", RK, 1.0)):
                wa, ws = mat(W[a], 2), mat(W[s], 2)
                for m in range(2):
                    k1, p1, f1 = bank()
                    k2, p2, f2 = bank()
                    t1 = PE(mms(*sum_jobs(p1, [(wa[:, kt, tok(m)], HT[:, kt, :]) for kt in range(2)])), f1, t_ht, t_w)
                    t2 = PE(mms(*sum_jobs(p2, [(ws[:, kt, tok(m)], HT[:, kt, :]) for kt in range(2)])), f2)
                    v2 = lambda p: p.rearrange("p (b t) -> p b t", b=2)
                    t1 = DV(lambda p=p1: V.tensor_tensor(v2(tA), v2(p), cos, ALU.mult), t1, td)
                    PB.give(k1, t1)
                    t2 = DV(lambda p=p2: V.tensor_tensor(v2(tB), v2(p), sin, ALU.mult), t2, td)
                    PB.give(k2, t2)
                    t = DV(lambda: V.tensor_tensor(tA, tA, tB, ALU.add), t1, t2)
                    td = DV(lambda m=m, dst=dst, sc=sc: V.tensor_scalar(dst[:, m, :], tA, sc, None, ALU.mult), t)
                    ts.append(td)
            tv, tg = [], []
            wv, wg = mat(W["Wv"], 2), mat(W["Wg"], 2)
            for i in range(4):
                k, ps, free = bank()
                t = PE(mms(*sum_jobs(ps, [(HT[:, kt, tok(i)], wv[:, kt, :]) for kt in range(2)])), free)
                t = AC(lambda i=i, ps=ps: A.copy(VV[:, i, :], ps), t)
                PB.give(k, t)
                tv.append(t)
                k, ps, free = bank()
                t = PE(mms(*sum_jobs(ps, [(HT[:, kt, tok(i)], wg[:, kt, :]) for kt in range(2)])), free)
                t = AC(lambda i=i, ps=ps: A.activation(GG[:, i, :], ps, ACT.Silu), t)
                PB.give(k, t)
                tg.append(t)
            dec = W["decay"].rearrange("p (j h t) -> p j h t", j=2, h=4)
            ss, rr = sm(4, 4), sm(4, 4)
            t_at = {}
            for b in range(2):
                for h in range(4):
                    r = slice(64 * (h % 2), 64 * (h % 2) + 64)
                    k, ps, free = bank()
                    q = RQ[r, h // 2, b * 256:b * 256 + 256]
                    jobs = [(ps[:, j * 256:j * 256 + 256], RK[r, h // 2, tok(2 * b + j)], q, True, True)
                            for j in range(2)]
                    t = PE(mms(*jobs), free, ts)
                    t = DV(lambda b=b, h=h, ps=ps: V.tensor_tensor(
                        AT[:, 4 * b + h, :].rearrange("p (j t) -> p j t", j=2), ps.rearrange("p (j t) -> p j t", j=2),
                        dec[:, :, h, :], ALU.mult), t, t_w)
                    PB.give(k, t)
                    t_at[b, h] = t
            tn = []
            for i in range(4):
                b, l = i // 2, i % 2
                k, ps, free = bank()
                jobs = []
                for h in range(4):
                    pairs = [(AT[:, 4 * b + h, j * 256 + l * 128:j * 256 + l * 128 + 128],
                              VV[:, 2 * b + j, tok(h)]) for j in range(l + 1)]
                    jobs += sum_jobs(ps[:, tok(h)], pairs)
                t = PE(mms(*jobs), free, tv, [t_at[b, h] for h in range(4)])
                t = DV(lambda i=i, ps=ps: V.tensor_copy(OO[:, i, :], ps), t)
                PB.give(k, t)
                tq_before = AC.now()
                tq = []
                for h in range(4):
                    tq.append(AC(lambda i=i, h=h: A.activation((tA, tB)[i % 2][:, tok(h)], OO[:, i, tok(h)],
                                                               ACT.Square, accum_out=ss[:, i, h:h + 1]), t,
                                 ts, tq_before))
                t2 = rsqrt(rr[:, i, :], ss[:, i, :], 1.0 / 128, 1e-5, tq)
                t3 = DV(lambda i=i: V.tensor_tensor(
                    GG[:, i, :].rearrange("p (h d) -> p h d", h=4), GG[:, i, :].rearrange("p (h d) -> p h d", h=4),
                    W["gn"].unsqueeze(1).to_broadcast([128, 4, 128]), ALU.mult), tg[i])
                for h in range(4):
                    t = DV(lambda i=i, h=h: V.scalar_tensor_tensor(
                        out=OO[:, i, tok(h)], in0=OO[:, i, tok(h)], scalar=rr[:, i, h:h + 1], in1=GG[:, i, tok(h)],
                        op0=ALU.mult, op1=ALU.mult), t2, t3, tq)
                k, ps, free = bank()
                def go(i=i, ps=ps):
                    for h in range(4):
                        z = TE.transpose(ps[:, tok(h)], OO[:, i, tok(h)], ident)
                    return z
                t = PE(go, free, t)
                t = DV(lambda i=i, ps=ps: V.tensor_copy(OT[:, :, tok(i)], ps.rearrange("p (h t) -> p h t", h=4)), t)
                PB.give(k, t)
                tn.append(t)
            wo = mat(W["Wo"], 4)
            for i in range(4):
                k, ps, free = bank()
                t = PE(mms(*sum_jobs(ps[:, 0:256], [(OT[:, h, tok(i)], wo[:, h, :]) for h in range(4)])), free, tn)
                t = add_to_x(ps[:, 0:256], i, 1, t)
                PB.give(k, t)
            return fence()

        if only[0] <= 10 <= only[1]:
            f = stage_10(f)

        def stage_11(f):
            ER = Ring([view(CTf, 4096 * k, 4096) for k in range(4)])
            expert_w = []

            def load_expert(e, *deps):
                s0 = SPAN["s11e"][0] + e * 4096
                kk, w, wf = ER.take()
                return kk, w, load(w, pack[:, s0:s0 + 4096], wf, *deps)
            W, t_w = weights("s11", AR, 0, f)
            for e in range(4):
                expert_w.append(load_expert(e, f))
            B0 = CNf
            X1, X2 = view(B0, 0, 4, 256), view(B0, 1024, 4, 256)
            QA, KA, CTX = view(B0, 2048, 4, 512), view(B0, 4096, 4, 512), view(B0, 6144, 4, 512)
            VP = view(B0, 8192, 4, 288)
            PTR = Ring([view(B0, 9344 + 512 * k, 2, 256) for k in range(3)])
            RC = view(B0, 9344, 2, 512)
            MX, NM = view(B0, 10880, 2, 4, 8), view(B0, 10944, 2, 128)
            GT = B0[0:8, 12288:12800]
            M1, M2 = view(B0, 12800, 4, 8), view(B0, 12832, 4, 8)
            t_ones = [PL(lambda: G.memset(VP, 1.0)), PL(lambda: G.memset(NM, 0.0))]
            x1 = norm_rows(X, X1, None)

            def affine(g_, b_):
                def post(dst, ps, kt, t):
                    return DV(lambda: V.tensor_scalar(dst, ps, W[g_][:, kt:kt + 1], W[b_][:, kt:kt + 1],
                                                      ALU.mult, ALU.add), t, t_w)
                return post
            t_ht = to_T(H, HT, norm_rows(X1, H, x1), affine("g1", "b1n"))
            wq, wk, wv = mat(W["Wq"], 2), mat(W["Wk"], 2), mat(W["Wv"], 2)
            ts = []
            for w, bias, dst, sc in ((wq, "bq", QA, 0.25), (wk, "bk", KA, 1.0)):
                for g in range(4):
                    k, ps, free = bank()
                    t = PE(mms(*sum_jobs(ps, [(w[:, kt, tok(g)], HT[:, kt, :]) for kt in range(2)])), free, t_ht, t_w)
                    t = DV(lambda g=g, ps=ps, bias=bias, dst=dst, sc=sc: V.tensor_scalar(
                        dst[:, g, :], ps, W[bias][:, g:g + 1], sc, ALU.add, ALU.mult), t)
                    PB.give(k, t)
                    ts.append(t)
            tv = [values(wv, [HT[:, kt, tok(m)] for kt in range(2)], m, lambda m: VP[:, m, :], W["bv"], None, t_ones)
                  for m in range(4)]
            t_c = []
            for b in range(2):
                for g in range(4):
                    t_m = heads_max(QA, lambda c, b=b, g=g: KA[:, g, b * 256:b * 256 + 256], 1, 256, g, b, MX, NM,
                                    ts, t_ones, PE.now())
                    t_c.append(heads_mix(QA, lambda kt, b=b, g=g: KA[:, g, tok(2 * b + kt)],
                                         lambda kt, b=b: VP[:, 2 * b + kt, :], 2, g, b, CTX, PTR, 4 * b + g, t_m, tv))
            t_n = heads_norm(CTX, RC, W["dsel"], [t_c, PE.now()])
            wo = mat(W["Wo"], 4)
            x2 = []
            for i in range(4):
                t0 = PL(lambda i=i: G.tensor_tensor(X1[:, i, :], X1[:, i, :], W["bo"], ALU.add), x1, t_ht)
                k, ps, free = bank()
                t = PE(mms(*sum_jobs(ps[:, 0:256], [(CTX[:, g, tok(i)], wo[:, g, :]) for g in range(4)])), free, t_n)
                t = DV(lambda i=i, ps=ps: V.tensor_tensor(X2[:, i, :], ps[:, 0:256], X1[:, i, :], ALU.add), t, t0)
                PB.give(k, t)
                x2.append(t)
            hs = norm_rows(X2, H, x2)
            for i in range(4):
                t = DV(lambda i=i: V.tensor_tensor(H[:, i, :], H[:, i, :], W["g2"], ALU.mult), hs[i])
                hs[i] = DV(lambda i=i: V.tensor_tensor(H[:, i, :], H[:, i, :], W["b2n"], ALU.add), t)
            t_ht = to_T(H, HT, hs)
            lg, t = logits8(mat(W["wr"], 2), None, t_ht)
            pr, mxl, den, l2 = sm(4, 8), sm(4), sm(4), sm(4, 8)
            t1 = DV(lambda: V.tensor_reduce(mxl, lg, AX, ALU.max), t)
            t1 = DV(lambda: V.tensor_tensor(pr, lg, up8(mxl), ALU.subtract), t1)
            t1 = AC(lambda: A.activation(pr, pr, ACT.Exp), t1)
            t1 = DV(lambda: V.tensor_reduce(den, pr, AX, ALU.add), t1)
            t1 = DV(lambda: V.reciprocal(den, den), t1)
            t_p = DV(lambda: V.tensor_tensor(pr, pr, up8(den), ALU.mult), t1)
            oh1, _, t1 = first_of_max(pr, t_p)
            t = DV(lambda: V.tensor_scalar(l2, oh1, -3e38, None, ALU.mult), t1)
            t = DV(lambda: V.tensor_tensor(l2, l2, lg, ALU.add), t)
            oh2, _, t = first_of_max(l2, t)
            t1 = DV(lambda: V.tensor_copy(M1, oh1), t1)
            t2 = DV(lambda: V.tensor_copy(M2, oh2), t)
            k, ps, free = bank()
            jobs = []
            for i in range(4):
                prs = [(cst["ones"], M1[:, n, :]) for n in range(i)] + [(cst["triu"], M1[:, i, :])]
                jobs += sum_jobs(ps[:, i * 8:i * 8 + 8], prs)
                prs = [(cst["ones"], M1[:, n, :]) for n in range(4)] + [(cst["ones"], M2[:, n, :]) for n in range(i)] + [
                    (cst["triu"], M2[:, i, :])]
                jobs += sum_jobs(ps[:, 32 + i * 8:40 + i * 8], prs)
            t = PE(mms(*jobs), free, t1, t2)
            k1_, k2_ = sm(4, 8), sm(4, 8)
            v8 = lambda p: p.rearrange("p (a b) -> p a b", b=8)
            ta = DV(lambda ps=ps: V.scalar_tensor_tensor(out=k1_, in0=v8(ps[:, 0:32]), scalar=128.5, in1=oh1,
                                                         op0=ALU.is_lt, op1=ALU.mult), t)
            tb = DV(lambda ps=ps: V.scalar_tensor_tensor(out=k2_, in0=v8(ps[:, 32:64]), scalar=128.5, in1=oh2,
                                                         op0=ALU.is_lt, op1=ALU.mult), t)
            LO, l2_ = sm(4, 8), sm(4, 8)
            tc = DV(lambda ps=ps: V.tensor_tensor(LO, v8(ps[:, 0:32]), k1_, ALU.mult), ta)
            td = DV(lambda ps=ps: V.tensor_tensor(l2_, v8(ps[:, 32:64]), k2_, ALU.mult), tb)
            PB.give(k, [tc, td])
            tc = DV(lambda: V.tensor_tensor(LO, LO, l2_, ALU.add), tc, td)
            t_lo = DV(lambda: V.tensor_scalar(LO, LO, -1.0, None, ALU.add), tc)
            t = DV(lambda: V.tensor_tensor(k1_, k1_, k2_, ALU.add), ta, tb, t_lo)
            t = DV(lambda: V.tensor_tensor(k1_, k1_, pr, ALU.mult), t)
            dn = sm(4)
            t = DV(lambda: V.tensor_reduce(dn, k1_, AX, ALU.add), t)
            t = DV(lambda: V.tensor_scalar(dn, dn, float(np.finfo(np.float32).eps), None, ALU.max), t)
            t = DV(lambda: V.reciprocal(dn, dn), t)
            GG = sm(4, 8)
            t_g = DV(lambda: V.tensor_tensor(GG, k1_, up8(dn), ALU.mult), t)
            t = rows8(GG, GT, t_g)
            acc = [PS[:, 6 + i // 2, (i % 2) * 256:(i % 2) * 256 + 256] for i in range(4)]
            PE(mms(*[(acc[i], GT[:, tok(i)], W["b2"][0:8, :], i % 2 == 0, False) for i in range(4)]), t)
            DS = [view(B0, 2048 + 512 * k, 4, 128) for k in range(4)]
            BT = [view(B0, 4096 + 256 * k, 2, 128) for k in range(2)]
            GDT = [view(B0, 4608 + 512 * k, 512) for k in range(2)]
            HH = [view(B0, 5632 + 1024 * k, 8, 128) for k in range(2)]
            YY = [view(B0, 7680 + 256 * k, 256) for k in range(2)]
            ds_free, bt_free, gd_free, hh_free, yy_free = ([None, None] for _ in range(5))
            att_done = PE.now()
            t_bt, t_gd, t_h, t_y = {}, {}, {}, {}

            def dispatch(e):
                p = e % 2
                D, GD = DS[p], DS[2 + p]
                td, tg = [], []
                for i in range(4):
                    td.append(DV(lambda i=i: V.tensor_scalar(D[:, i, :], W["iota"], LO[:, i, e:e + 1], None,
                                                             ALU.is_equal), t_lo, ds_free[p], att_done))
                    tg.append(DV(lambda i=i: V.tensor_scalar(GD[:, i, :], W["iota"], LO[:, i, e:e + 1],
                                                             GG[:, i, e:e + 1], ALU.is_equal, ALU.mult), t_g))
                k, ps, free = bank()
                jobs = []
                for kt in range(2):
                    jobs += sum_jobs(ps[:, tok(kt)], [(H[:, i, tok(kt)], D[:, i, :]) for i in range(4)])
                t = PE(mms(*jobs), free, td, hs)
                t = AC(lambda ps=ps: A.copy(BT[p], ps[:, 0:256].rearrange("p (k s) -> p k s", k=2)), t, bt_free[p],
                       att_done)
                PB.give(k, t)
                t_bt[e] = t
                k, ps, free = bank()
                def go(ps=ps):
                    for i in range(4):
                        l = TE.transpose(ps[:, tok(i)], GD[:, i, :], ident)
                    return l
                t = PE(go, free, tg)
                ds_free[p] = t
                t = DV(lambda ps=ps: V.tensor_copy(GDT[p], ps), t, gd_free[p])
                PB.give(k, t)
                t_gd[e] = t

            def hidden(e):
                p = e % 2
                w1 = mat(expert_w[e][1][:, 0:2048], 2)
                ts = []
                for q in range(2):
                    k, ps, free = bank()
                    jobs = []
                    for m in range(4):
                        jobs += sum_jobs(ps[:, tok(m)], [(w1[:, kt, tok(4 * q + m)], BT[p][:, kt, :]) for kt in range(2)])
                    t = PE(mms(*jobs), free, t_bt[e], expert_w[e][2])
                    for m in range(4):
                        f_ = 4 * q + m
                        c = W["b1"][:, e * 8 + f_:e * 8 + f_ + 1]
                        if q:
                            t2 = AC(lambda c=c, ps=ps, m=m, f_=f_: A.activation(HH[p][:, f_, :], ps[:, tok(m)], ACT.Relu,
                                                                                bias=c), t, hh_free[p])
                        else:
                            t2 = DV(lambda c=c, ps=ps, m=m, f_=f_: V.tensor_scalar(HH[p][:, f_, :], ps[:, tok(m)], c, 0.0,
                                                                                   ALU.add, ALU.max), t, hh_free[p])
                        ts.append(t2)
                    PB.give(k, t2)
                bt_free[p] = t
                t_h[e] = ts

            def result(e):
                p = e % 2
                w2 = mat(expert_w[e][1][:, 2048:4096], 8)
                k, ps, free = bank()
                t = PE(mms(*sum_jobs(ps[:, 0:256], [(HH[p][:, m, :], w2[:, m, :]) for m in range(8)])), free, t_h[e])
                hh_free[p] = t
                ER.give(expert_w[e][0], t)
                if e + 4 < 8:
                    expert_w.append(load_expert(e + 4))
                t = AC(lambda ps=ps: A.copy(YY[p], ps[:, 0:256]), t, yy_free[p])
                PB.give(k, t)
                t_y[e] = t

            def combine(e):
                p = e % 2
                t = PE(mms(*[(acc[i], GDT[p][:, tok(i)], YY[p], False, e == 7) for i in range(4)]), t_gd[e], t_y[e])
                gd_free[p] = yy_free[p] = t
                return t

            dispatch(0)
            for e in range(8):
                hidden(e)
                if e:
                    combine(e - 1)
                if e + 1 < 8:
                    dispatch(e + 1)
                result(e)
            t = combine(7)
            for q in range(2):
                xv, x2v = (a[:, 2 * q:2 * q + 2, :].rearrange("p a b -> p (a b)") for a in (X, X2))
                tt = DV(lambda q=q, x2v=x2v: V.scalar_tensor_tensor(out=x2v, in0=PS[:, 6 + q, :], scalar=1.0 - 0.2,
                                                                    in1=x2v, op0=ALU.mult, op1=ALU.add), t)
                DV(lambda xv=xv, x2v=x2v: V.tensor_tensor(xv, xv, x2v, ALU.add), tt)
            return fence()

        if only[0] <= 11 <= only[1]:
            f = stage_11(f)

        s_out = ctx.enter_context(nc.semaphore("s_out"))
        block = ctx.enter_context(nc.Block())

        @block.sync
        def _(eng):
            for deps, dst, src, s in SP:
                for ds, v in deps:
                    eng.wait_ge(ds, v)
                eng.dma_start(dst, src).then_inc(s, 16)
            for ds, v in f:
                eng.wait_ge(ds, v)
            eng.dma_start(out.rearrange("b (i p) d -> p (b i) d", p=128), X[:]).then_inc(s_out, 16)
            eng.wait_ge(s_out, 16)

        @block.tensor
        def _(eng):
            PE.emit(eng)

        @block.vector
        def _(eng):
            DV.emit(eng)

        @block.scalar
        def _(eng):
            AC.emit(eng)

        @block.gpsimd
        def _(eng):
            PL.emit(eng)


def _rows_to_partitions(w):
    w = np.asarray(w)
    k = w.shape[0] // 128
    return np.ascontiguousarray(w.reshape(k, 128, -1).transpose(1, 0, 2)).reshape(128, -1)


def _col(v):
    return np.ascontiguousarray(np.asarray(v).reshape(-1, 128).T)


def _row(v, times=1):
    v = np.tile(np.asarray(v), times)
    return np.broadcast_to(v[None, :], (128, v.size))


def _pad_out(w):
    w = np.asarray(w)
    o = np.zeros((w.shape[0], 16, 32), np.float32)
    o[:, :, :16] = w.reshape(w.shape[0], 16, 16)
    return o.reshape(w.shape[0], 512)


def _pad_in(w):
    w = np.asarray(w)
    o = np.zeros((16, 32, w.shape[1]), np.float32)
    o[:, :16] = w.reshape(16, 16, w.shape[1])
    return _rows_to_partitions(o.reshape(512, w.shape[1]))


def _pad_col(v, at, value):
    o = np.zeros((16, 32), np.float32)
    o[:, :16] = np.asarray(v).reshape(16, 16)
    o[:, at] = value
    return _col(o.reshape(512))


def _constants():
    c = {}
    c["ident"] = np.eye(128, dtype=np.float32)
    c["triu"] = np.triu(np.ones((128, 128), np.float32))
    c["iota8"] = _row(np.arange(8, 0, -1).astype(np.float32), 4)
    c["iota"] = _row(np.arange(128).astype(np.float32))
    c["ones"] = np.ones((128, 128), np.float32)
    c["bd16"] = np.kron(np.eye(8), np.ones((16, 16))).astype(np.float32)
    c["bd32"] = np.kron(np.eye(4), np.ones((32, 32))).astype(np.float32)
    s16, s17, ds = (np.zeros((128, 128), np.float32) for _ in range(3))
    for j in range(4):
        s16[32 * j:32 * j + 16, 32 * j + 16] = -0.25
        s17[32 * j:32 * j + 16, 32 * j + 17] = -0.25
        ds[32 * j + 16, 32 * j:32 * j + 32] = 1.0
    c["sel16"], c["sel17"], c["dsel"] = s16, s17, ds
    p = np.arange(128) % 32
    c["c16"] = (p == 16).astype(np.float32)[:, None]
    c["c17"] = (p == 17).astype(np.float32)[:, None]
    c["half"] = np.full((128, 1), 0.5, np.float32)
    c["sum17"] = (p[:, None] == np.arange(17)[None, :]).astype(np.float32)
    esel = np.zeros((128, 8, 128), np.float32)
    for e in range(8):
        esel[e, e, :] = 1.0
    c["esel"] = esel.reshape(128, 1024)
    inv = (1.0 / np.float32(10000.0) ** (np.arange(0, 64, 2, dtype=np.float32) / np.float32(64))).astype(np.float32)
    ang = (np.arange(256, dtype=np.float32)[None, :] * inv[:, None]).astype(np.float32)
    cos, sin = np.cos(ang).astype(np.float32), np.sin(ang).astype(np.float32)
    c["cos"] = np.concatenate([cos, cos, cos, cos])
    c["sin"] = np.concatenate([-sin, sin, -sin, sin])
    gam = (1.0 - np.exp2(-5.0 - np.arange(4, dtype=np.float32))).astype(np.float32)
    d = np.arange(256)[None, :] - np.arange(256)[:, None]
    dec = np.where(d[None] >= 0, gam[:, None, None].astype(np.float64) ** np.maximum(d, 0)[None], 0.0)
    c["decay"] = np.ascontiguousarray(dec.reshape(4, 2, 128, 256).transpose(2, 1, 0, 3)).reshape(128, 2048).astype(np.float32)
    return c


def _pack(a):
    R = _rows_to_partitions
    c = _constants()
    g = {}

    def put(stage, **kw):
        for k, v in kw.items():
            g[stage, k] = v

    L = "L0_xattn_"
    put("s0", Wq=R(a[L + "Wq"]), Wk=R(a[L + "Wk"].T), Wv=R(a[L + "Wv"]), Wo=R(a[L + "Wo"]), bq=_col(a[L + "bq"]),
        bk=_col(a[L + "bk"]), bv=_col(a[L + "bv"]), bo=_row(a[L + "bo"]))
    L = "L0_attn_"
    put("s1", qkv=R(a[L + "qkv_w"].T), proj=R(a[L + "proj_w"].T), conv1=R(a[L + "conv1_w"].T),
        conv2=R(a[L + "conv2_w"].T), s1=_col(a[L + "scale1"]), s2=_col(a[L + "scale2"]), gamma=_row(a[L + "gamma"]),
        pb=_row(a[L + "proj_b"]), c1b=_col(a[L + "conv1_b"]), c2b=_row(a[L + "conv2_b"]))
    L = "L0_ffn_"
    put("s2", w1=R(a[L + "w1_w"].T), w2=R(a[L + "w2_w"].T), w3=R(a[L + "w3_w"].T), w1s=_col(a[L + "w1_s"]),
        w2s=_col(a[L + "w2_s"]), h1s=_col(a[L + "h1_s"]), h2s=_col(a[L + "h2_s"]), w3s=_row(a[L + "w3_s"]))
    for l, n in enumerate(("h1_w", "h2_w")):
        w = a[L + n].T
        for m in range(8):
            g["s2h", f"h{8 * l + m}"] = R(w[:, m * 128:m * 128 + 128])
    for st, L in (("s3", "L1_xattn_"), ("s6", "L2_xattn_")):
        put(st, Wq=R(a[L + "Wq"].T), Wk=R(a[L + "Wk"]), Wv=R(a[L + "Wv"].T), bq=_col(a[L + "bq"]),
            bk=_col(a[L + "bk"]), bv=_row(a[L + "bv"]))
    L = "L1_attn_"
    put("s4", Wq=R(a[L + "Wq"].T), Wk=R(a[L + "Wk"].T), Wv=R(a[L + "Wv"].T),
        gamma=np.broadcast_to(a[L + "gamma"].reshape(1, 1), (128, 1)))
    L = "L1_ffn_"
    put("s5", gate=R(a[L + "gate_w"].T))
    for e in range(8):
        put("s5", **{f"g{e}": R(a[L + "w_gate"][e].T), f"u{e}": R(a[L + "w_up"][e].T), f"d{e}": a[L + "w_down"][e].T})
    L = "L2_attn_"
    put("s7", Wkp=R(_pad_out(a[L + "W_k"].T)), Wk=R(a[L + "W_k"].T), Wvp=R(_pad_out(a[L + "W_v"].T)),
        Wo=_pad_in(a[L + "W_o"].T))
    L = "L2_ffn_"
    put("s8", rw=R(a[L + "router_w"]), rb=_row(a[L + "router_b"], 4))
    for e in range(10):
        k, n = ("routed", e) if e < 8 else ("shared", e - 8)
        put("s8", **{f"g{e}": R(a[f"{L}{k}_w1"][n]), f"u{e}": R(a[f"{L}{k}_w3"][n]), f"d{e}": a[f"{L}{k}_w2"][n]})
    L = "L3_xattn_"
    put("s9", Wq=R(a[L + "q_w"].T), Wk=R(a[L + "k_w"].T), Wv=R(a[L + "v_w"].T), bq=_col(a[L + "q_b"]),
        bk=_col(a[L + "k_b"]), bv=_row(a[L + "v_b"]))
    L = "L3_attn_"

    def swap(w):
        return np.ascontiguousarray(w.reshape(4, 2, 32, 256)[:, ::-1]).reshape(256, 256)
    put("s10", Wq=R(a[L + "Wq"].T), Wqs=R(swap(a[L + "Wq"]).T), Wk=R(a[L + "Wk"].T), Wks=R(swap(a[L + "Wk"]).T),
        Wv=R(a[L + "Wv"].T), Wg=R(a[L + "Wg"].T), Wo=R(a[L + "Wo"].T), gn=_row(a[L + "gnorm_w"]))
    L = "L3_ffn_"
    b2 = np.zeros((128, 256), np.float32)
    b2[:8] = a[L + "b2"]
    put("s11", Wq=R(_pad_out(a[L + "wq"])), Wk=R(_pad_out(a[L + "wk"])), Wv=R(a[L + "wv"]), Wo=_pad_in(a[L + "wo"]),
        bq=_pad_col(a[L + "bq"], 17, 0.0), bk=_pad_col(a[L + "bk"], 16, -1.0), bv=_row(a[L + "bv"]), bo=_row(a[L + "bo"]),
        g1=_col(a[L + "ln1_g"]), b1n=_col(a[L + "ln1_b"]), g2=_row(a[L + "ln2_g"]), b2n=_row(a[L + "ln2_b"]),
        wr=R(a[L + "wr"]), b1=_col(a[L + "b1"].reshape(-1)), b2=b2)
    for e in range(8):
        put("s11e", **{f"w1_{e}": R(a[L + "w1"][e]), f"w2_{e}": R(a[L + "w2"][e])})
    out = np.empty((128, TOTAL), np.float32)
    for stage, entries in PACK.items():
        for name, cols in entries:
            o, _ = WHERE[stage, name]
            v = g[stage, name] if (stage, name) in g else c[name]
            s = SPAN[stage][0] + o
            assert v.shape == (128, cols), (stage, name, v.shape, cols)
            out[:, s:s + cols] = v
    return out


def build(nc, arrays, only=(0, 99)):
    args = [nc.dram_tensor(n, a.shape, mybir.dt.from_np(a.dtype), kind="ExternalInput").ap()
            for n, a in arrays.items()]
    out = nc.dram_tensor("out_dram", (2, 256, 256), F32, kind="ExternalOutput").ap()
    perceiver(nc, *args, out, only=only)


def lay_out(inputs):
    a = {k: np.asarray(v) for k, v in inputs.items()}
    ctxt = a["ctx_1024"].reshape(8192, 256)
    return {
        "pack": _pack(a),
        "x_in": np.ascontiguousarray(a["x"]),
        "ctx_n": np.ascontiguousarray(ctxt.reshape(64, 128, 256).transpose(1, 0, 2)),
        "ctx_t": np.ascontiguousarray(ctxt.reshape(8192, 2, 128).transpose(2, 1, 0)),
        "mask0": np.ascontiguousarray(a["mask_BxS2_bk0"]).view(np.int32),
        "mask1": np.ascontiguousarray(a["mask_BxS2_ik0"]),
    }


def kernel(**inputs):
    import concourse.bacc as _bacc
    from concourse.bass_utils import run_bass_kernel_spmd as _run

    nc = _bacc.Bacc("TRN2", target_bir_lowering=False, num_devices=1)
    arrays = lay_out(inputs)
    build(nc, arrays)
    r = _run(nc, [arrays], core_ids=[0])
    return r.results[0]["out_dram"]
```

```python
from contextlib import ExitStack

import numpy as np

import concourse.bass as bass
from concourse import mybir

ALU = mybir.AluOpType
ACT = mybir.ActivationFunctionType
F32 = mybir.dt.float32
BF16 = mybir.dt.bfloat16
U8 = mybir.dt.uint8
I32 = mybir.dt.int32
AX = mybir.AxisListType.X

T = 512
KEYS = 4096
BIG = float(2 ** 30)
ONES2 = float(np.array([0x3F803F80], np.uint32).view(np.float32)[0])
MINUS2 = float(np.array([0xBF80BF80], np.uint32).view(np.float32)[0])

PACK = {
    "c": [("ident", 128), ("triu", 128), ("iota8", 32), ("ones", 128)],
    "s0": [("Wq", 512), ("Wk", 512), ("Wv", 512), ("Wo", 512), ("bq", 2), ("bk", 2), ("bv", 2), ("bo", 256)],
    "s1": [("qkv", 1536), ("proj", 512), ("conv1", 1024), ("conv2", 1024), ("s1", 2), ("s2", 2),
           ("gamma", 256), ("pb", 256), ("c1b", 4), ("c2b", 256), ("bd16", 128)],
    "s2": [("w1", 2048), ("w2", 2048), ("w3", 2048), ("w1s", 8), ("w2s", 8), ("h1s", 8), ("h2s", 8), ("w3s", 256)],
    "s2h": [(f"h{i}", 1024) for i in range(16)],
    "s3": [("Wq", 512), ("Wk", 512), ("Wv", 512), ("bq", 2), ("bk", 2), ("bv", 256)],
    "s4": [("Wq", 512), ("Wk", 512), ("Wv", 512), ("gamma", 1)],
    "s5": [("gate", 16), ("esel", 1024)] + [(f"{k}{e}", 256) for e in range(8) for k in ("g", "u", "d")],
    "s6": [("Wq", 512), ("Wk", 512), ("Wv", 512), ("bq", 2), ("bk", 2), ("bv", 256)],
    "s7": [("Wkp", 1024), ("Wk", 512), ("Wvp", 1024), ("Wo", 1024), ("bd32", 128), ("hsel", 32),
           ("dsel", 128)],
    "s8": [("rw", 16), ("rb", 32), ("esel", 1024)] + [(f"{k}{e}", 256) for e in range(10) for k in ("g", "u", "d")],
    "s9": [("Wq", 512), ("Wk", 512), ("Wv", 512), ("bq", 2), ("bk", 2), ("bv", 256), ("sum17", 17)],
    "s10": [("Wq", 512), ("Wqs", 512), ("Wk", 512), ("Wks", 512), ("Wv", 1024), ("Wg", 1024), ("Wo", 1024),
            ("gn", 128), ("cos", 256), ("sin", 256), ("decay", 2048)],
    "s11": [("Wq", 512), ("Wk", 512), ("Wv", 512), ("Wo", 1024), ("bq", 2), ("bk", 2), ("bv", 256), ("bo", 256),
            ("g1", 2), ("b1n", 2), ("g2", 256), ("b2n", 256), ("wr", 16), ("b1", 64), ("b2", 256), ("dsel", 128),
            ("iota", 128)],
    "s11e": [(f"{k}{e}", 2048) for e in range(8) for k in ("w1_", "w2_")],
}


def places():
    at, where, span = 0, {}, {}
    for stage, entries in PACK.items():
        start = at
        for name, cols in entries:
            where[stage, name] = (at - start, cols)
            at += cols
        span[stage] = (start, at - start)
    return where, span, at


WHERE, SPAN, TOTAL = places()


class Queue:

    def __init__(self, sem):
        self.sem, self.ops, self.n, self.seen, self.pending = sem, [], 0, {}, []

    def __call__(self, fn, *deps):
        need = {}
        for s, v in flat(deps) + self.pending:
            if v > max(self.seen.get(s, 0), need.get(s, 0)):
                need[s] = v
        self.pending = []
        self.seen.update(need)
        self.n += 1
        self.ops.append((list(need.items()), fn))
        return (self.sem, self.n)

    def now(self):
        return (self.sem, self.n)

    def emit(self, eng):
        for waits, fn in self.ops:
            for s, v in waits:
                eng.wait_ge(s, v)
            fn().then_inc(self.sem, 1)


def flat(deps):
    out = []
    for d in deps:
        if d is None:
            continue
        if isinstance(d, list):
            out += flat(d)
        else:
            out.append(d)
    return out


class Ring:

    def __init__(self, slots):
        self.slots, self.free, self.i = slots, [None] * len(slots), 0

    def take(self):
        k = self.i % len(self.slots)
        self.i += 1
        return k, self.slots[k], self.free[k]

    def give(self, k, tok):
        self.free[k] = tok


def perceiver(nc, pack, x_in, ctx_n, ctx_t, mask0, mask1, out, only=(0, 99)):
    with ExitStack() as ctx:
        def sb(name, shape, dt=F32):
            return ctx.enter_context(nc.sbuf_tensor(name, shape, dt))

        PS = ctx.enter_context(nc.psum_tensor("PS", [128, 8, 512], F32))
        CT = sb("CT", [128, 2, 8192])
        CN = sb("CN", [128, 64, 256])
        X = sb("X", [128, 4, 256])
        H = sb("H", [128, 4, 256])
        HT = sb("HT", [128, 2, 512])
        CST = sb("CST", [128, SPAN["c"][1]])
        SM = sb("SM", [128, 1200])
        AR = sb("AR", [128, 15640])
        CNf = CN[:].rearrange("p a b -> p (a b)")
        CTf = CT[:].rearrange("p a b -> p (a b)")

        sems = {n: ctx.enter_context(nc.semaphore("s_" + n)) for n in ("pe", "dve", "act", "pool")}
        PE, DV, AC, PL = (Queue(sems[n]) for n in ("pe", "dve", "act", "pool"))
        V, A, G, TE = nc.vector, nc.scalar, nc.gpsimd, nc.tensor
        SP = []
        count = [0]

        def load(dst, src, *deps):
            count[0] += 1
            s = ctx.enter_context(nc.semaphore(f"d{count[0]}"))
            SP.append((flat(deps), dst, src, s))
            return (s, 16)

        sm_at = [0]

        def warm(func):
            AC(lambda: A.activation(SM[:, 1199:1200], SM[:, 1199:1200], func), t_warm, AC.now() if AC.n else None)

        def fence():
            sm_at[0] = 0
            warm(ACT.Sqrt)
            now = [q.now() for q in (PE, DV, AC, PL) if q.n]
            for q in (PE, DV, AC, PL):
                q.pending = list(now)
            return now



        def sm(*shape):
            n = int(np.prod(shape))
            a = SM[:, sm_at[0]:sm_at[0] + n]
            sm_at[0] += n
            assert sm_at[0] < 1150
            if len(shape) == 2:
                a = a.rearrange("p (a b) -> p a b", b=shape[1])
            if len(shape) == 3:
                a = a.rearrange("p (a b c) -> p a b c", b=shape[1], c=shape[2])
            return a

        def view(base, off, *shape):
            n = int(np.prod(shape))
            a = base[:, off:off + n]
            if len(shape) == 2:
                a = a.rearrange("p (a b) -> p a b", b=shape[1])
            if len(shape) == 3:
                a = a.rearrange("p (a b c) -> p a b c", b=shape[1], c=shape[2])
            if len(shape) == 4:
                a = a.rearrange("p (a b c d) -> p a b c d", b=shape[1], c=shape[2], d=shape[3])
            return a

        def weights(stage, base, off, *deps, shapes=()):
            start, n = SPAN[stage]
            tok = load(base[:, off:off + n], pack[:, start:start + n], *deps)
            got = {}
            for name, cols in PACK[stage]:
                o, c = WHERE[stage, name]
                got[name] = base[:, off + o:off + o + c]
            return got, tok

        def weights_in(stage, *pieces):
            start, n = SPAN[stage]
            names = [name for name, _ in PACK[stage]]
            firsts = [names.index(p[0]) for p in pieces] + [len(names)]
            got, toks = {}, []
            for k, (_, base, off, deps) in enumerate(pieces):
                lo = WHERE[stage, names[firsts[k]]][0]
                hi = WHERE[stage, names[firsts[k + 1]]][0] if k + 1 < len(pieces) else n
                toks.append(load(base[:, off:off + hi - lo], pack[:, start + lo:start + hi], deps))
                for name in names[firsts[k]:firsts[k + 1]]:
                    o, c = WHERE[stage, name]
                    got[name] = base[:, off + o - lo:off + o - lo + c]
            return got, toks

        ahead = {}

        def mat(a, kt):
            return a.rearrange("p (k o) -> p k o", k=kt)

        def tok(i):
            return slice(i * 128, i * 128 + 128)

        def mms(*jobs):
            def go():
                for o, l, r, a, z in jobs:
                    last = TE.matmul(o, l, r, start=a, stop=z, skip_group_check=True)
                return last
            return go

        def sum_jobs(o, pairs, first=True, final=True):
            n = len(pairs)
            return [(o, l, r, first and k == 0, final and k == n - 1) for k, (l, r) in enumerate(pairs)]

        t_warm = DV(lambda: V.memset(SM[:, 1199:1200], 1.0))
        warm(ACT.Sqrt)
        cst, t_cst = weights("c", CST, 0)
        ident = cst["ident"]
        PB = Ring([0, 1, 2, 3, 4, 5])
        t_x = load(X[:], x_in.rearrange("b (i p) d -> p (b i) d", p=128))

        def bank():
            k, b, dep = PB.take()
            return k, PS[:, b, :], dep

        both = [0]

        def copy(o, i, *deps):
            both[0] ^= 1
            if both[0]:
                return DV(lambda: V.tensor_copy(o, i), *deps)
            return AC(lambda: A.copy(o, i), *deps)

        def to_T(src, dst, deps, post=None):
            ts = []
            for i in range(4):
                k, ps, free = bank()
                def go(i=i, ps=ps):
                    TE.transpose(ps[:, 0:128], src[:, i, 0:128], ident)
                    return TE.transpose(ps[:, 128:256], src[:, i, 128:256], ident)
                t = PE(go, free, deps[i], t_cst)
                if post is None:
                    t = copy(dst[:, :, tok(i)], ps[:, 0:256].rearrange("p (k t) -> p k t", k=2), t)
                    ts.append(t)
                    PB.give(k, t)
                else:
                    t = [post(dst[:, kt, tok(i)], ps[:, kt * 128:kt * 128 + 128], kt, t) for kt in range(2)]
                    ts.append(t)
                    PB.give(k, t)
            return ts

        def rsqrt(dst, src, scale, eps, *deps):
            t = DV(lambda: V.tensor_scalar(dst, src, scale, eps, ALU.mult, ALU.add), *deps)
            t = DV(lambda: V.reciprocal(dst, dst), t)
            return AC(lambda: A.activation(dst, dst, ACT.Sqrt), t)

        xst, xmv = view(SM, 1150, 4, 6), view(SM, 1174, 4, 2)
        x_stats = {}

        def x_done(i, t):
            t = DV(lambda: V.bn_stats(xst[:, i, :], X[:, i, :]), t)
            x_stats[i] = DV(lambda: V.bn_aggr(xmv[:, i, :], xst[:, i, :]), t)

        def norm_rows(src, dst, deps, eps=1e-5):
            rs = sm(4)
            if src is X and x_stats:
                mv, ts = xmv, [x_stats.pop(i) for i in range(4)]
            else:
                st, mv = sm(4, 6), sm(4, 2)
                ts = []
                for i in range(4):
                    t = DV(lambda i=i: V.bn_stats(st[:, i, :], src[:, i, :]), deps)
                    ts.append(DV(lambda i=i: V.bn_aggr(mv[:, i, :], st[:, i, :]), t))
            t = rsqrt(rs, mv[:, :, 1], 1.0, eps, ts)
            return [DV(lambda i=i: V.tensor_scalar(dst[:, i, :], src[:, i, :], mv[:, i, 0:1], rs[:, i:i + 1],
                                                   ALU.subtract, ALU.mult), t) for i in range(4)]

        def rms_rows(src, dst, junk, deps):
            ss, rs = sm(4), sm(4)
            ts = [AC(lambda i=i: A.activation(junk[:, i, :], src[:, i, :], ACT.Square, accum_out=ss[:, i:i + 1]), deps)
                  for i in range(4)]
            t = rsqrt(rs, ss, 1.0, 0.0, ts)
            return [DV(lambda i=i: V.tensor_scalar(dst[:, i, :], src[:, i, :], rs[:, i:i + 1], None, ALU.mult),
                       t, ts[i]) for i in range(4)]

        def add_to_x(ps, i, n, t):
            v = X[:, i:i + n, :].rearrange("p a b -> p (a b)")
            return DV(lambda: V.tensor_tensor(v, ps, v, ALU.add), t)

        def add_row_x(row, *deps):
            return [PL(lambda i=i: G.tensor_tensor(X[:, i, :], X[:, i, :], row, ALU.add), *deps) for i in range(4)]

        def xattn(W, t_w, scale, places, bound, then):
            hs = norm_rows(X, H, t_x_now[0])
            warm(ACT.Exp)
            t_ht = to_T(H, HT, hs)
            Wq, Wk, Wv = (mat(W[k], 2) for k in ("Wq", "Wk", "Wv"))
            S = [view(AR, places[k], KEYS) for k in range(2)]
            PTR = Ring([view(AR, places[2] + 512 * k, 512) for k in range(4)])
            QT = view(AR, places[2], 2, 512)
            OT, CX = HT, H[:].rearrange("p a b -> p (a b)").rearrange("p (k t) -> p k t", k=2)
            t_q = []
            for m in range(2):
                k, ps, free = bank()
                t = PE(mms(*sum_jobs(ps, [(Wq[:, kt, tok(m)], HT[:, kt, :]) for kt in range(2)])), free, t_ht, t_w)
                t = DV(lambda m=m, ps=ps: V.tensor_scalar(QT[:, m, :], ps, W["bq"][:, m:m + 1], scale,
                                                          ALU.add, ALU.mult), t)
                PB.give(k, t)
                t_q.append(t)
            cadd = sm(4)
            k, ps, free = bank()
            jobs = []
            for i in range(4):
                jobs += sum_jobs(ps[:, i:i + 1], [(QT[:, m, tok(i)], W["bk"][:, m:m + 1]) for m in range(2)])
            t = PE(mms(*jobs), free, t_q)
            t_c = DV(lambda ps=ps: V.tensor_copy(cadd, ps[:, 0:4]), t)
            PB.give(k, t_c)
            t_q2 = []
            for m in range(2):
                k, ps, free = bank()
                t = PE(mms(*sum_jobs(ps, [(Wk[:, h, tok(m)], QT[:, h, :]) for h in range(2)])), free, t_q)
                t = AC(lambda m=m, ps=ps: A.copy(QN[:, m, :], ps), t, t_q)
                PB.give(k, t)
                t_q2.append(t)
            q_done = PE.now()

            mxc, mx, nb, rs, rt, ri = sm(4, 8), sm(4), sm(4), sm(4, 4), sm(4), sm(4)
            t_s, t_o, o_free, part = {}, [], [None, None], {}
            s_free = [None, None]

            def chunk(i, c):
                b = i // 2
                k, ps, free = bank()
                rhs = [CT[:, kt, b * KEYS + c * 512:b * KEYS + c * 512 + 512] for kt in range(2)]
                t = PE(mms(*sum_jobs(ps, [(QN[:, kt, tok(i)], rhs[kt]) for kt in range(2)])),
                       free, t_q2, t_ct[b * 4 + c // 2])
                o = S[i % 2][:, c * 512:c * 512 + 512]
                if bound:
                    m = MB[:, c * 512:c * 512 + 512]
                    if i % 2 == 0:
                        part["bound", c] = bound(b, c, part.get((1, c)))
                    if i == 0:
                        s_free[1] = part["bound", c]
                    t = DV(lambda: V.scalar_tensor_tensor(out=o, in0=ps, scalar=cadd[:, i:i + 1], in1=m, op0=ALU.add,
                                                          op1=ALU.min),
                           t, t_c, part["bound", c], s_free[i % 2])
                elif c % 4 == 3:
                    t = DV(lambda: V.tensor_scalar(o, ps, cadd[:, i:i + 1], None, ALU.add), t, t_c, s_free[i % 2])
                else:
                    t = AC(lambda: A.activation(o, ps, ACT.Identity, bias=cadd[:, i:i + 1]), t, t_c, s_free[i % 2])
                PB.give(k, t)
                part[i, c] = t
                part[i, c, "max"] = DV(lambda: V.tensor_reduce(mxc[:, i, c:c + 1], o, AX, ALU.max), t)

            def largest(i):
                t = DV(lambda: V.tensor_reduce(mx[:, i:i + 1], mxc[:, i, :], AX, ALU.max),
                       [part[i, c, "max"] for c in range(8)])
                part[i, "nb"] = DV(lambda: V.tensor_scalar(nb[:, i:i + 1], mx[:, i:i + 1], -1.0, None, ALU.mult), t)

            def exps(i, q):
                o = S[i % 2][:, q * 1024:q * 1024 + 1024]
                t_s[i, q] = AC(lambda: A.activation(o, o, ACT.Exp, bias=nb[:, i:i + 1], accum_out=rs[:, i, q:q + 1]),
                               part[i, "nb"])

            def turn(i, c):
                k, ps, free = bank()
                def go():
                    for y in range(4):
                        u = c * 4 + y
                        l = TE.transpose(ps[:, y * 128:y * 128 + 128], S[i % 2][:, u * 128:u * 128 + 128], ident)
                    return l
                t = PE(go, free, t_s[i, c // 2])
                s_free[i % 2] = t
                kk, pt, pfree = PTR.take()
                t = copy(pt, ps, t, pfree, q_done)
                PB.give(k, t)
                return i, c, kk, pt, t

            def mix(i, c, kk, pt, t):
                b = i // 2
                O = PS[:, 6 + i % 2, 0:256]
                jobs = [(O, pt[:, y * 128:y * 128 + 128], CN[:, b * 32 + c * 4 + y, :],
                         c == 0 and y == 0, c == 7 and y == 3) for y in range(4)]
                t = PE(mms(*jobs), t, t_cn[b * 2 + c // 4], o_free[i % 2])
                PTR.give(kk, t)
                if c == 7:
                    t = DV(lambda: V.tensor_scalar(OB[:, i, :], O, ri[:, i:i + 1], None, ALU.mult), t, part[i, "ri"])
                    o_free[i % 2] = t
                    t_o.append(t)

            for c in range(8):
                chunk(0, c)
            largest(0)
            for q in range(4):
                exps(0, q)
            chunk(1, 0)
            chunk(1, 1)
            pend = []
            for i in range(4):
                for c in range(8):
                    pend.append(turn(i, c))
                    if i < 3 and c < 6:
                        chunk(i + 1, c + 2)
                    if i < 2 and c >= 6:
                        chunk(i + 2, c - 6)
                    if i < 3 and c == 5:
                        largest(i + 1)
                    if i < 3 and c >= 5:
                        exps(i + 1, c - 5)
                    if i > 0 and c == 0:
                        exps(i, 3)
                    if c == 1:
                        t = DV(lambda i=i: V.tensor_reduce(rt[:, i:i + 1], rs[:, i, :], AX, ALU.add),
                               [t_s[i, q] for q in range(4)])
                        part[i, "ri"] = DV(lambda i=i: V.reciprocal(ri[:, i:i + 1], rt[:, i:i + 1]), t)
                    if len(pend) > 2:
                        mix(*pend.pop(0))
                if i == 2:
                    then(s_free[0], part.get(("bound", 7)))
            while pend:
                mix(*pend.pop(0))
            t_ot = to_T(OB, OT, t_o)
            if "Wo" in W:
                Wo = mat(W["Wo"], 2)
                t_row = add_row_x(W["bo"], hs, t_w)
                tc = []
                for m in range(2):
                    k, ps, free = bank()
                    t = PE(mms(*sum_jobs(ps, [(Wv[:, kt, tok(m)], OT[:, kt, :]) for kt in range(2)])), free, t_ot)
                    t = DV(lambda m=m, ps=ps: V.tensor_scalar(CX[:, m, :], ps, W["bv"][:, m:m + 1], None, ALU.add),
                           t, t_ot)
                    PB.give(k, t)
                    tc.append(t)
                src, Wf = CX, Wo
            else:
                t_row = add_row_x(W["bv"], hs, t_w)
                src, Wf, tc = OT, Wv, t_ot
            for i in range(4):
                k, ps, free = bank()
                t = PE(mms(*sum_jobs(ps[:, 0:256], [(src[:, kt, tok(i)], Wf[:, kt, :]) for kt in range(2)])), free, tc)
                t = add_to_x(ps[:, 0:256], i, 1, [t, t_row[i]])
                PB.give(k, t)
                x_done(i, t)

        QN = HT
        OB = H
        t_x_now = [t_x]

        W0, t_w0 = weights("s0", AR, 12288)
        MB = view(AR, 10240, 2048).bitcast(BF16)
        MW = [view(AR, 4096, 1024).bitcast(I32), view(AR, 14600, 1024).bitcast(I32)]
        MU = [w.bitcast(U8) for w in MW]
        t_ct, t_cn = [], []

        def load_ct(*qs):
            for q in qs:
                t_ct.append(load(CT[:, :, q * 1024:q * 1024 + 1024], ctx_t[:, :, q * 1024:q * 1024 + 1024]))

        def load_cn(*qs):
            for q in qs:
                t_cn.append(load(CN[:, q * 16:q * 16 + 16, :], ctx_n[:, q * 16:q * 16 + 16, :]))
        t_mu = [load(MW[0], mask0[0:1, :].partition_broadcast(128))]
        load_ct(0, 1, 2, 3)
        load_cn(0, 1)
        t_mu.append(load(MW[1], mask0[1:2, :].partition_broadcast(128)))
        load_ct(4, 5, 6, 7)
        load_cn(2, 3)

        def bound(b, c, *deps):
            lo = c * 512
            return DV(lambda: V.tensor_scalar(MB[:, lo:lo + 512], MU[b][:, lo:lo + 512], 2 * BIG, -BIG, ALU.mult,
                                              ALU.add), t_mu[b], *deps)

        def ahead_1(s_token, bound_token):
            ahead["s1"] = weights_in("s1", ("qkv", AR, 0, s_token), ("s1", AR, 14600, bound_token))

        if only[0] <= 0 <= only[1]:
            xattn(W0, t_w0, 1.0 / 16, (0, 4096, 8192), bound, ahead_1)
        f = fence()

        def stage_1(f):
            W, t_w = ahead["s1"]
            o = 4096
            hs = norm_rows(X, H, None)
            Y, Z = view(AR, o, 4, 256), view(AR, o + 1024, 4, 256)
            HB = view(AR, o + 8192, 4, 256)
            ZT = HT
            OT = view(AR, o + 2048, 2, 512)
            QF = view(AR, o + 3072, 2, 512)
            KV = view(AR, o + 4096, 4, 512)
            HD = view(AR, o + 6144, 4, 512)
            KM = view(AR, o + 6144, 2, 2, 128)
            KS = view(AR, o + 6656, 2, 2, 128)
            tmp = view(AR, o + 7168, 2, 512)
            qkv, proj, conv1, conv2 = mat(W["qkv"], 2), mat(W["proj"], 2), mat(W["conv1"], 2), mat(W["conv2"], 4)

            def scaled(col):
                def post(dst, ps, kt, t):
                    return DV(lambda: V.tensor_scalar(dst, ps, col[:, kt:kt + 1], 16.0 + 1e-6, ALU.mult, ALU.mult),
                              t, t_w)
                return post
            rs = rms_rows(H, Z, Y, hs)
            warm(ACT.Exp)
            t_zt = to_T(Z, ZT, rs, scaled(W["s1"]))
            t_row = [PL(lambda: G.tensor_tensor(W["pb"], W["pb"], W["gamma"], ALU.mult), t_w, PL.now())]
            t_row.append(PL(lambda: G.tensor_tensor(W["c2b"], W["c2b"], W["gamma"], ALU.mult), t_w, PL.now()))
            t_hb = [PL(lambda i=i: G.tensor_tensor(HB[:, i, :], H[:, i, :], W["pb"], ALU.add), hs, t_row, PL.now())
                    for i in range(4)]
            t_qf = []
            for m in range(2):
                k, ps, free = bank()
                t = PE(mms(*sum_jobs(ps, [(qkv[:, kt, tok(m)], ZT[:, kt, :]) for kt in range(2)])), free, t_zt, t_w)
                t = AC(lambda m=m, ps=ps: A.activation(QF[:, m, :], ps, ACT.Square), t)
                PB.give(k, t)
                t_qf.append(AC(lambda m=m: A.activation(QF[:, m, :], QF[:, m, :], ACT.Exp, scale=-0.5), t))
            t_kv = []
            for i in range(4):
                k, ps, free = bank()
                t = PE(mms(*sum_jobs(ps, [(ZT[:, kt, tok(i)], qkv[:, kt, 256:768]) for kt in range(2)])), free, t_zt)
                t1 = AC(lambda i=i, ps=ps: A.activation(KV[:, i, 0:256], ps[:, 0:256], ACT.Square), t)
                t2 = DV(lambda i=i, ps=ps: V.tensor_copy(KV[:, i, 256:512], ps[:, 256:512]), t1)
                PB.give(k, [t1, t2])
                t_kv.append([t2, AC(lambda i=i: A.activation(KV[:, i, 0:256], KV[:, i, 0:256], ACT.Exp, scale=-0.5),
                                    t1)])
            ksum = sm(4)
            t_at, t_km = [], {}
            ones = cst["ones"]
            warm(ACT.Sqrt)
            for b in range(2):
                for m in range(2):
                    k, ps, free = bank()
                    jobs = sum_jobs(ps[:, 0:128], [(KV[:, 2 * b + i, tok(m)], KV[:, 2 * b + i, 256 + m * 128:384 + m * 128])
                                                   for i in range(2)])
                    jobs += sum_jobs(ps[:, 128:129], [(KV[:, 2 * b + i, tok(m)], ones[:, 0:1]) for i in range(2)])
                    t = PE(mms(*jobs), free, t_kv[2 * b], t_kv[2 * b + 1])
                    t1 = DV(lambda b=b, m=m, ps=ps: V.tensor_tensor(KM[:, b, m, :], ps[:, 0:128], W["bd16"], ALU.mult), t)
                    c = ksum[:, 2 * b + m:2 * b + m + 1]
                    t2 = DV(lambda c=c, ps=ps: V.tensor_copy(c, ps[:, 128:129]), t)
                    PB.give(k, [t1, t2])
                    t_km[b, m] = [t1, DV(lambda b=b, m=m, c=c: V.tensor_scalar(KS[:, b, m, :], W["bd16"], c, None,
                                                                               ALU.mult), t2)]
            for b in range(2):
                for m in range(2):
                    q = QF[:, m, b * 256:b * 256 + 256]
                    k, ps, free = bank()
                    t = PE(mms((ps[:, 0:256], KM[:, b, m, :], q, True, True),
                               (ps[:, 256:512], KS[:, b, m, :], q, True, True)), free, t_km[b, m], t_qf)
                    w = tmp[:, b, m * 256:m * 256 + 256]
                    t = DV(lambda w=w, ps=ps: V.tensor_scalar(w, ps[:, 256:512], 1e-6, None, ALU.add), t)
                    t = DV(lambda w=w: V.reciprocal(w, w), t)
                    t = DV(lambda b=b, m=m, ps=ps, w=w: V.tensor_tensor(OT[:, m, b * 256:b * 256 + 256], ps[:, 0:256],
                                                                        w, ALU.mult), t)
                    PB.give(k, t)
                    t_at.append(t)
            ty = []
            for i in range(4):
                k, ps, free = bank()
                t = PE(mms(*sum_jobs(ps[:, 0:256], [(OT[:, m, tok(i)], proj[:, m, :]) for m in range(2)])), free,
                       t_at[2 * (i // 2):2 * (i // 2) + 2])
                y = Y[:, i, :]
                t = DV(lambda y=y, ps=ps: V.tensor_tensor(y, ps[:, 0:256], W["gamma"], ALU.mult), t)
                PB.give(k, t)
                ty.append(DV(lambda y=y, i=i: V.tensor_tensor(y, y, HB[:, i, :], ALU.add), t, t_hb[i]))
            rs = rms_rows(Y, Z, H, ty)
            warm(ACT.Gelu)
            t_xy = [PL(lambda i=i: G.tensor_tensor(Y[:, i, :], Y[:, i, :], X[:, i, :], ALU.add), ty[i], rs, PL.now())
                    for i in range(4)]
            t_xy = [PL(lambda i=i: G.tensor_tensor(Y[:, i, :], Y[:, i, :], W["c2b"], ALU.add), t_xy[i], PL.now())
                    for i in range(4)]
            t_zt = to_T(Z, ZT, rs, scaled(W["s2"]))
            th = []
            for m in range(4):
                k, ps, free = bank()
                t = PE(mms(*sum_jobs(ps, [(conv1[:, kt, tok(m)], ZT[:, kt, :]) for kt in range(2)])), free, t_zt)
                t = AC(lambda m=m, ps=ps: A.activation(HD[:, m, :], ps, ACT.Gelu, bias=W["c1b"][:, m:m + 1]), t, t_at)
                PB.give(k, t)
                th.append(t)
            for i in range(4):
                k, ps, free = bank()
                t = PE(mms(*sum_jobs(ps[:, 0:256], [(HD[:, m, tok(i)], conv2[:, m, :]) for m in range(4)])), free, th)
                z = Z[:, i, :]
                t = DV(lambda z=z, ps=ps: V.tensor_tensor(z, ps[:, 0:256], W["gamma"], ALU.mult), t)
                PB.give(k, t)
                x_done(i, DV(lambda z=z, i=i: V.tensor_tensor(X[:, i, :], Y[:, i, :], z, ALU.add), t, t_xy[i]))
            return fence()

        if only[0] <= 1 <= only[1]:
            f = stage_1(f)

        def stage_2(f):
            W, t_w = {}, []
            for name, cols in PACK["s2"]:
                at = WHERE["s2", name][0]
                W[name] = AR[:, 8192 + at:8192 + at + cols]
            s0 = SPAN["s2"][0]
            both_w = lambda a, q: a[:, :, 256 * q:256 * q + 256]
            for q in range(4):
                t_w.append(load(both_w(view(AR, 8192, 4, 1024), q),
                                both_w(pack[:, s0:s0 + 4096].rearrange("p (a b) -> p a b", a=4), q), f))
                if q == 0:
                    t_small = load(AR[:, 8192 + 6144:8192 + SPAN["s2"][1]], pack[:, s0 + 6144:s0 + SPAN["s2"][1]], f)
            t_w3 = load(AR[:, 12288:14336], pack[:, s0 + 4096:s0 + 6144], f)
            hA, hB = view(AR, 0, 8, 512), view(AR, 4096, 8, 512)
            w1, w2, w3 = mat(W["w1"], 2), mat(W["w2"], 2), mat(W["w3"], 8)
            hs = norm_rows(X, H, None)
            warm(ACT.Silu)
            t_ht = to_T(H, HT, hs)
            ring = Ring([H[:].rearrange("p a b -> p (a b)").rearrange("p (a b) -> p a b", b=128)]
                        + [view(AR, 8192 + 1024 * k, 8, 128) for k in range(4)])

            def hidden_w(n, *deps):
                kk, w, wf = ring.take()
                s0 = SPAN["s2h"][0] + n * 1024
                return kk, w, load(w.rearrange("p a b -> p (a b)"), pack[:, s0:s0 + 1024], wf, *deps)
            hw = [hidden_w(0, PE.now())]
            ts = []
            for m in range(8):
                k1, p1, f1 = bank()
                ta = PE(mms(*sum_jobs(p1, [(w1[:, kt, tok(m)], HT[:, kt, :]) for kt in range(2)])), f1, t_ht,
                        t_w[m // 2])
                k2, p2, f2 = bank()
                tb = PE(mms(*sum_jobs(p2, [(w2[:, kt, tok(m)], HT[:, kt, :]) for kt in range(2)])), f2)
                ta = AC(lambda m=m, p=p1: A.activation(hB[:, m, :], p, ACT.Silu, scale=W["w1s"][:, m:m + 1]), ta,
                        t_small)
                PB.give(k1, ta)
                tb = DV(lambda m=m, p=p2: V.scalar_tensor_tensor(out=hA[:, m, :], in0=p, scalar=W["w2s"][:, m:m + 1],
                                                                 in1=hB[:, m, :], op0=ALU.mult, op1=ALU.mult),
                        ta, tb, t_small)
                PB.give(k2, tb)
                ts.append(tb)
            over = PE.now()
            hw += [hidden_w(n, over) for n in range(1, 5)]
            src, dst = hA, hB
            for layer in range(2):
                nts = []
                for m in range(8):
                    kk, w, t_l = hw[layer * 8 + m]
                    k, ps, free = bank()
                    t = PE(mms(*sum_jobs(ps, [(w[:, kt, :], src[:, kt, :]) for kt in range(8)])), free, t_l, ts)
                    ring.give(kk, t)
                    if len(hw) < 16:
                        hw.append(hidden_w(len(hw)))
                    t = AC(lambda m=m, ps=ps, dst=dst, s=W["h1s" if layer == 0 else "h2s"]: A.activation(
                        dst[:, m, :], ps, ACT.Gelu, scale=s[:, m:m + 1]), t, ts)
                    PB.give(k, t)
                    nts.append(t)
                src, dst, ts = dst, src, nts
            ahead["s3"] = weights("s3", AR, 4096, PE.now())
            for i in range(4):
                k, ps, free = bank()
                t = PE(mms(*sum_jobs(ps[:, 0:256], [(src[:, m, tok(i)], w3[:, m, :]) for m in range(8)])), free, ts,
                       t_w3)
                o = H[:, i, :]
                t = DV(lambda o=o, ps=ps: V.tensor_tensor(o, ps[:, 0:256], W["w3s"], ALU.mult), t)
                PB.give(k, t)
                x_done(i, DV(lambda o=o, i=i: V.tensor_tensor(X[:, i, :], X[:, i, :], o, ALU.add), t))
            return fence()

        if only[0] <= 2 <= only[1]:
            f = stage_2(f)

        def stage_3(f):
            W, t_w = ahead["s3"]

            def then(t, _):
                ahead["s4"] = weights("s4", AR, 5906, t)
            t_x_now[0] = None
            xattn(W, t_w, 1.0, (5906, 10002, 0), None, then)
            return fence()

        if only[0] <= 3 <= only[1]:
            f = stage_3(f)

        def stage_4(f):
            W, t_w = ahead["s4"]
            ahead["s5"] = weights("s5", AR, 7443, f)
            hs = norm_rows(X, H, None)
            warm(ACT.Exp)
            t_ht = to_T(H, HT, hs)
            FT, GT = view(AR, 0, 2, 512), view(AR, 1024, 2, 512)
            HV = view(AR, 2048, 4, 256)
            P, PT = view(AR, 3072, 4, 256), view(AR, 4096, 4, 256)
            Wq, Wk, Wv = (mat(W[k], 2) for k in ("Wq", "Wk", "Wv"))
            ts = []
            for w, o in ((Wq, FT), (Wk, GT)):
                for m in range(2):
                    k, ps, free = bank()
                    t = PE(mms(*sum_jobs(ps, [(w[:, kt, tok(m)], HT[:, kt, :]) for kt in range(2)])), free, t_ht, t_w)
                    t = copy(o[:, m, :], ps, t)
                    PB.give(k, t)
                    ts.append(t)
            tv = []
            for i in range(4):
                k, ps, free = bank()
                t = PE(mms(*sum_jobs(ps[:, 0:256], [(HT[:, kt, tok(i)], Wv[:, kt, :]) for kt in range(2)])), free)
                t = copy(HV[:, i, :], ps[:, 0:256], t)
                PB.give(k, t)
                tv.append(t)
            mx, nb, rs, ri = sm(4), sm(4), sm(4), sm(4)
            t_e, t_pt = [], []
            t_xh = [PL(lambda i=i: G.tensor_tensor(X[:, i, :], X[:, i, :], H[:, i, :], ALU.add), hs, PL.now())
                    for i in range(4)]
            for i in range(4):
                b = i // 2
                k, ps, free = bank()
                t = PE(mms(*sum_jobs(ps[:, 0:256], [(GT[:, m, tok(i)], FT[:, m, b * 256:b * 256 + 256])
                                                    for m in range(2)])), free, ts)
                t1 = DV(lambda i=i, ps=ps: V.tensor_reduce(mx[:, i:i + 1], ps[:, 0:256], AX, ALU.max), t)
                t1 = DV(lambda i=i: V.tensor_scalar(nb[:, i:i + 1], mx[:, i:i + 1], -1.0, None, ALU.mult), t1)
                t1 = AC(lambda i=i, ps=ps: A.activation(P[:, i, :], ps[:, 0:256], ACT.Exp, bias=nb[:, i:i + 1],
                                                        accum_out=rs[:, i:i + 1]), t1)
                PB.give(k, t1)
                t_e.append(t1)
            for i in range(4):
                k, ps, free = bank()
                def go(i=i, ps=ps):
                    TE.transpose(ps[:, 0:128], P[:, i, 0:128], ident)
                    return TE.transpose(ps[:, 128:256], P[:, i, 128:256], ident)
                t = PE(go, free, t_e[i])
                t = copy(PT[:, i, :], ps[:, 0:256], t)
                PB.give(k, t)
                t_pt.append(t)
            t2 = DV(lambda: V.reciprocal(ri, rs), t_e)
            t2 = DV(lambda: V.tensor_scalar(ri, ri, W["gamma"], None, ALU.mult), t2)
            for i in range(4):
                b = i // 2
                k, ps, free = bank()
                t = PE(mms(*sum_jobs(ps[:, 0:256], [(PT[:, i, tok(y)], HV[:, 2 * b + y, :]) for y in range(2)])),
                       free, t_pt[i], tv)
                t = DV(lambda i=i, ps=ps: V.scalar_tensor_tensor(out=X[:, i, :], in0=ps[:, 0:256], scalar=ri[:, i:i + 1],
                                                                 in1=X[:, i, :], op0=ALU.mult, op1=ALU.add),
                       t, t2, t_xh[i])
                PB.give(k, t)
                x_done(i, t)
            return fence()

        if only[0] <= 4 <= only[1]:
            f = stage_4(f)

        def first_of_max(src, *deps):
            top, w, m, oh = sm(4), sm(4, 8), sm(4), sm(4, 8)
            up = lambda a: a.unsqueeze(2).to_broadcast([128, 4, 8])
            t = DV(lambda: V.tensor_reduce(top, src, AX, ALU.max), *deps)
            t = DV(lambda: V.tensor_tensor(w, src, up(top), ALU.is_equal), t)
            t = DV(lambda: V.tensor_tensor(w, w, cst["iota8"].rearrange("p (a b) -> p a b", b=8), ALU.mult), t)
            t = DV(lambda: V.tensor_reduce(m, w, AX, ALU.max), t)
            t = DV(lambda: V.tensor_tensor(oh, w, up(m), ALU.is_equal), t)
            return oh, top, t

        def logits8(w, row, *deps):
            lg = sm(4, 8)
            k, ps, free = bank()
            jobs = []
            for i in range(4):
                jobs += sum_jobs(ps[:, i * 8:i * 8 + 8], [(HT[:, kt, tok(i)], w[:, kt, :]) for kt in range(2)])
            t = PE(mms(*jobs), free, *deps)
            p = ps[:, 0:32].rearrange("p (a b) -> p a b", b=8)
            if row is None:
                t = DV(lambda: V.tensor_copy(lg, p), t)
            else:
                t = DV(lambda: V.tensor_tensor(lg, p, row.rearrange("p (a b) -> p a b", b=8), ALU.add), t)
            PB.give(k, t)
            return lg, t

        def rows8(R, dst, *deps):
            k, ps, free = bank()
            def go():
                for i in range(4):
                    l = TE.transpose(ps[0:8, tok(i)], R[:, i, :], ident)
                return l
            t = PE(go, free, *deps)
            t = DV(lambda: V.tensor_copy(dst, ps[0:8, :]), t)
            PB.give(k, t)
            return t

        def up8(a):
            return a.unsqueeze(2).to_broadcast([128, 4, 8])

        def experts(W, n, n_gated, RT, route, t_ht, work, gate_first, t_late):
            acc = [PS[:, 6 + i // 2, (i % 2) * 256:(i % 2) * 256 + 256] for i in range(4)]
            esel = W["esel"]
            rb_r = Ring([view(AR, work + 512 * k, 512) for k in range(2)])
            g_r = Ring([view(AR, work + 1024 + 512 * k, 512) for k in range(2)])
            h_r = Ring([view(AR, work + 2048 + 512 * k, 512) for k in range(3)])
            pend = []

            def down(e, hk, h, t):
                wd = W[f"d{e}"]
                jobs = [(acc[i], h[:, tok(i)], wd, e == 0 and i % 2 == 0, e == n - 1) for i in range(4)]
                t = PE(mms(*jobs), t)
                h_r.give(hk, t)
                return t

            def up(e):
                wg, wu = mat(W[f"g{e}"], 2), mat(W[f"u{e}"], 2)
                k1, p1, f1 = bank()
                ta = PE(mms(*sum_jobs(p1, [(wg[:, kt, :], HT[:, kt, :]) for kt in range(2)])), f1, t_ht,
                        t_late if e >= 5 else None)
                k2, p2, f2 = bank()
                tb = PE(mms(*sum_jobs(p2, [(wu[:, kt, :], HT[:, kt, :]) for kt in range(2)])), f2)
                return k1, p1, ta, k2, p2, tb
            nxt = up(0)
            t_rt = route()
            for e in range(n):
                k1, p1, ta, k2, p2, tb = nxt
                gated = e < n_gated
                tr = None
                if gated:
                    k, ps, free = bank()
                    t = PE(mms((ps, esel[0:8, e * 128:e * 128 + 128], RT, True, True)), free, t_rt)
                    rk, rb, rf = rb_r.take()
                    tr = AC(lambda rb=rb, ps=ps: A.copy(rb, ps), t, rf)
                    PB.give(k, tr)
                if e + 1 < n:
                    nxt = up(e + 1)
                gk, g, gf = g_r.take()
                hk, h, hf = h_r.take()
                if gate_first:
                    ta = DV(lambda p1=p1, g=g, rb=rb: V.tensor_tensor(g, p1, rb, ALU.mult), ta, tr, gf)
                    PB.give(k1, ta)
                    ta = AC(lambda g=g: A.activation(g, g, ACT.Silu), ta)
                    tb = DV(lambda p2=p2, h=h, rb=rb: V.tensor_tensor(h, p2, rb, ALU.mult), tb, tr, hf)
                    PB.give(k2, tb)
                    rb_r.give(rk, tb)
                    tb = DV(lambda g=g, h=h: V.tensor_tensor(h, h, g, ALU.mult), ta, tb)
                    g_r.give(gk, tb)
                else:
                    ta = AC(lambda p1=p1, g=g: A.activation(g, p1, ACT.Silu), ta, gf)
                    PB.give(k1, ta)
                    tb = DV(lambda p2=p2, h=h, g=g: V.tensor_tensor(h, p2, g, ALU.mult), tb, ta, hf)
                    PB.give(k2, tb)
                    g_r.give(gk, tb)
                    if gated:
                        tb = DV(lambda h=h, rb=rb: V.tensor_tensor(h, h, rb, ALU.mult), tb, tr)
                        rb_r.give(rk, tb)
                pend.append((e, hk, h, tb))
                if len(pend) > 1:
                    down(*pend.pop(0))
            t = down(*pend.pop(0))
            for q in range(2):
                z = add_to_x(PS[:, 6 + q, :], 2 * q, 2, t)
                x_done(2 * q, z)
                x_done(2 * q + 1, z)

        def stage_5(f):
            W, t_w = ahead["s5"]
            ahead["s6"] = weights("s6", AR, 0, f)
            hs = norm_rows(X, H, None)
            warm(ACT.Sigmoid)
            t_ht = to_T(H, HT, hs)
            lg, t = logits8(mat(W["gate"], 2), None, t_ht, t_w)
            oh, top, t = first_of_max(lg, t)
            rw, R = sm(4), sm(4, 8)
            t = AC(lambda: A.activation(rw, top, ACT.Sigmoid), t)
            warm(ACT.Silu)
            t = DV(lambda: V.tensor_tensor(R, oh, up8(rw), ALU.mult), t)
            RT = AR[0:8, 1810:2322]
            experts(W, 8, 8, RT, lambda t=t: rows8(R, RT, t), t_ht, 2322, True, None)
            return fence()

        if only[0] <= 5 <= only[1]:
            f = stage_5(f)

        def stage_6(f):
            W, t_w = ahead["s6"]

            def then(t, _):
                ahead["s7"] = weights("s7", AR, 1810, t)
            t_x_now[0] = None
            xattn(W, t_w, 4.0, (1810, 5906, 10002), None, then)
            return fence()

        if only[0] <= 6 <= only[1]:
            f = stage_6(f)

        ROWS = (0, 0, 0, 1, 1, 2)
        COLS = (0, 1, 2, 0, 1, 0)

        def split_steps(RT, x, parts, bias, scale, t, *deps):
            rk, r, rf = RT.take()
            r = r[0:x.shape[0]]
            ta = DV(lambda: V.tensor_scalar(r, x, bias, scale, ALU.add, ALU.mult), t, rf)
            t1 = AC(lambda: A.copy(parts[0], r), ta, *deps)
            yield ta
            t2 = DV(lambda: V.tensor_tensor(r, r, parts[0], ALU.subtract), t1)
            t3 = AC(lambda: A.copy(parts[1], r), t2, *deps)
            t4 = PL(lambda: G.tensor_tensor(parts[2], r, parts[1], ALU.subtract), t3, PL.now(), *deps)
            RT.give(rk, t4)
            yield [t1, t3, t4]

        def split(*args):
            return tuple(split_steps(*args))

        def loads(pairs, *deps):
            s = ctx.enter_context(nc.semaphore(f"g{len(SP)}"))
            for dst, src in pairs:
                SP.append((flat(deps), dst, src, s))
            return (s, 16 * len(pairs))

        def spread(scratch, Z, rows, m, *deps):
            return loads([(Z[16 * r:16 * r + 16, 8 * m:8 * m + 8, :],
                           scratch[s, 128 * m:128 * m + 128, :].rearrange("(h d) t -> d h t", d=16))
                          for r, s in enumerate(rows)], *deps)

        def attention(QS, KS, nr, scale, vrow, CTX, PTR, MM, IDB, t_idb, t_m, tv, norm, then):
            P1 = Ring([0, 1])
            P1.free = [PB.free[0], PB.free[1]]
            ST = Ring([2, 4])
            ST.free = [[PB.free[2], PB.free[3]], [PB.free[4], PB.free[5]]]
            order = [(b, g, jj) for b in range(2) for g in range(4) for jj in range(2)]
            mxs = sm(2, 4) if MM is not None else None
            t_hi, mm_free, t_row, c_done, t_c, half = {}, [None, None], {}, {}, [], []

            def best(n):
                b, g, jj = order[n]
                a, ts = n % 2, []
                for y in range(2):
                    h = 4 * g + 2 * jj + y
                    k, bk, free = P1.take()
                    t = PE(mms(*[(PS[:, bk, i * 256:i * 256 + 256], QS[0:96, h, tok(2 * b + i)],
                                  KS[0:96, h, b * 256:b * 256 + 256], True, True) for i in range(2)]),
                           free, t_m[h // 8])
                    t = DV(lambda y=y, bk=bk: V.tensor_reduce(
                        mxs[:, a, 2 * y:2 * y + 2], PS[:, bk, :].rearrange("p (i k) -> p i k", i=2), AX, ALU.max),
                        t, t_hi.get(n - 2))
                    P1.give(k, t)
                    ts.append(t)
                t = DV(lambda: V.tensor_copy(MM[:, a, :, 96], mxs[:, a, :]), ts, mm_free[a])
                t_hi[n] = DV(lambda: V.tensor_tensor(MM[:, a, :, 97], mxs[:, a, :], MM[:, a, :, 96], ALU.subtract), t)

            def best_rows(n):
                b, g, jj = order[n]
                h, a = 4 * g + 2 * jj, n % 2
                k, bk, free = P1.take()
                pb = PS[:, bk, 0:256].bitcast(BF16)
                def go():
                    for y in range(4):
                        l = TE.transpose(pb[:, y * 128:y * 128 + 128], MM[:, a, y, :], IDB)
                    return l
                t = PE(go, free, t_hi[n], t_idb)
                mm_free[a] = t
                t = AC(lambda: A.copy(QS[96:98, h:h + 2, b * 256:b * 256 + 256],
                                      pb[96:98, :].rearrange("p (y t) -> p y t", y=2)), t)
                P1.give(k, t)
                t_row[n] = t

            def mix(first, second):
                b, g, _ = order[first[0]]
                u = first[0] // 2
                cb = 6 + u % 2
                jobs = []
                for kt in range(2):
                    for j in range(4):
                        h, pt = 4 * g + j, (first, second)[j // 2][2]
                        jobs.append((PS[32 * j:32 * j + 32, cb, 0:256], vrow(2 * b + kt)[:, 17 * h:17 * h + 32],
                                     pt[:, 2 * (j % 2) + kt, :], kt == 0, kt == 1))
                t = PE(mms(*jobs), first[3], second[3], tv, c_done.get(u - 2))
                PTR.give(first[1], t)
                PTR.give(second[1], t)
                t = DV(lambda: V.tensor_copy(CTX[:, g, b * 256:b * 256 + 256], PS[:, cb, 0:256]), t)
                c_done[u] = t
                t_c.append((u, b, g, norm(cb, b, g, t)))

            def go_on():
                for item in list(t_c):
                    u, b, g, steps = item
                    c_done[u] = next(steps)
                    if item in half:
                        t_c.remove(item)
                        then(P1, b, g, c_done[u])
                    half.append(item)

            if MM is not None:
                best(0)
                best(1)
                best_rows(0)
            pend = []
            for n in range(16):
                b, g, jj = order[n]
                h = 4 * g + 2 * jj
                k, bk, free = ST.take()
                jobs = [(PS[:, bk + y, kt * 256:kt * 256 + 256], KS[0:nr, h + y, tok(2 * b + kt)],
                         QS[0:nr, h + y, b * 256:b * 256 + 256], True, True) for y in range(2) for kt in range(2)]
                t = PE(mms(*jobs), free, t_m[h // 8], t_row.get(n))
                kk, pt, pf = PTR.take()
                t = AC(lambda bk=bk, pt=pt: A.activation(
                    pt, PS[:, bk:bk + 2, :].rearrange("p a (c q) -> p (a c) q", c=2), ACT.Exp, scale=scale), t, pf)
                ST.give(k, t)
                pend.append((n, kk, pt, t))
                if MM is not None and n + 2 < 16:
                    best(n + 2)
                if MM is not None and n + 1 < 16:
                    best_rows(n + 1)
                go_on()
                if len(pend) > 2:
                    mix(pend.pop(0), pend.pop(0))
            mix(pend.pop(0), pend.pop(0))
            go_on()
            go_on()
            PB.free = P1.free + [ST.free[0]] * 2 + [ST.free[1]] * 2

        def heads_norm(CTX, RC, dsel, cb, b, g, t):
            c, r = CTX[:, g, b * 256:b * 256 + 256], RC[:, g % 2, b * 256:b * 256 + 256]
            ps = PS[:, cb, 256:512]
            t = PE(mms((ps, dsel, c, True, True)), t)
            t = DV(lambda: V.reciprocal(r, ps), t)
            yield t
            yield DV(lambda: V.tensor_tensor(c, c, r, ALU.mult), t)

        def values(W_, HTs, n, vrow, row, t_dep, t_ones):
            k, ps, free = bank()
            t = PE(mms(*sum_jobs(ps[:, 0:256], [(HTs[kt], W_[:, kt, :]) for kt in range(2)])), free, t_dep)
            o = vrow(n)[:, 0:272].rearrange("p (h r) -> p h r", r=17)[:, :, 0:16]
            p = ps[:, 0:256].rearrange("p (h r) -> p h r", r=16)
            if row is None:
                t = DV(lambda: V.tensor_copy(o, p), t, t_ones)
            else:
                t = DV(lambda: V.tensor_tensor(o, p, row.rearrange("p (h r) -> p h r", r=16), ALU.add), t, t_ones)
            PB.give(k, t)
            return t

        def s8_first(f):
            s0, n = SPAN["s8"][0], WHERE["s8", "g5"][0]
            return load(AR[:, 10460:10460 + n], pack[:, s0:s0 + n], f)

        def stage_7(f):
            W, t_w = ahead["s7"]
            ahead["s8"] = s8_first(f)
            B0 = CNf
            QS, KS = (view(B0, 4096 * k, 4096).bitcast(BF16).rearrange("p (h t) -> p h t", h=16) for k in range(2))
            CTX = view(B0, 8192, 4, 512)
            VP = view(B0, 10240, 4, 288)
            PTR = Ring([view(B0, 11392 + 1024 * k, 4, 256) for k in range(3)] + [view(AR, 0, 4, 256)])
            RC = view(B0, 14976, 2, 512)
            BD = view(B0, 14464, 4, 128)
            o = 6100
            AO = view(AR, o, 4, 512)
            ST3 = [view(AR, o + 768 * m, 768).bitcast(BF16).rearrange("p (s t) -> p s t", s=3) for m in range(3)]
            SQ = [view(AR, o + 2304 + 512 * m, 512) for m in range(2)]
            RT = Ring([view(AR, o + 3328 + 512 * k, 512) for k in range(2)])
            Wkp, Wk, Wvp, Wo = mat(W["Wkp"], 2), mat(W["Wk"], 2), mat(W["Wvp"], 2), mat(W["Wo"], 4)
            rd = nc.dram_tensor("r_parts", (3, 256, 512), BF16, kind="Internal").ap()
            nd = nc.dram_tensor("r_norms", (3, 16, 512), BF16, kind="Internal").ap()
            t_ones = [PL(lambda: G.memset(VP, 1.0), PL.now())]
            t_rows = [PL(lambda k=k: G.memset(view(B0, 4096 * k, 4096)[96:102], ONES2), PL.now()) for k in range(2)]
            hs = norm_rows(X, H, None)
            warm(ACT.Exp)
            t_ht = to_T(H, HT, hs)
            begun, t_sq = [], []
            for m in range(2):
                k, ps, free = bank()
                t = PE(mms(*sum_jobs(ps, [(Wk[:, kt, tok(m)], HT[:, kt, :]) for kt in range(2)])), free, t_ht, t_w)
                t1 = AC(lambda m=m, ps=ps: A.activation(SQ[m], ps, ACT.Square), t)
                t_sq.append(t1)
                steps = split_steps(RT, ps, [ST3[m][:, s, :] for s in range(3)], 0.0, 1.0, t1)
                PB.give(k, next(steps))
                begun.append(steps)
            t_p = [next(steps) for steps in begun]
            k, ps, free = bank()
            t = PE(mms(*sum_jobs(ps[0:16], [(W["hsel"][:, 16 * m:16 * m + 16], SQ[m]) for m in range(2)])), free, t_sq)
            ta, tt = split(RT, ps[0:16], [ST3[2][0:16, s, :] for s in range(3)], 0.0, -0.5, t)
            PB.give(k, ta)
            t_w1 = [load(rd[:, 128 * m:128 * m + 128, :].rearrange("s p t -> p s t"), ST3[m], t_p[m]) for m in range(2)]
            t_w2 = load(nd.rearrange("s p t -> p s t"), ST3[2][0:16], tt)
            t_n = loads([(KS[96:99], nd), (QS[99:102], nd)], t_w2, t_rows)
            t_m = [[t_n, spread(rd, QS, COLS, m, t_w1[m]), spread(rd, KS, ROWS, m, t_w1[m])] for m in range(2)]
            for g in range(4):
                k, ps, free = bank()
                t = PE(mms(*sum_jobs(ps[:, 0:128], [(Wkp[:, kt, tok(g)], Wvp[:, kt, tok(g)]) for kt in range(2)])), free)
                t = DV(lambda g=g, ps=ps: V.tensor_tensor(BD[:, g, :], ps[:, 0:128], W["bd32"], ALU.mult), t)
                PB.give(k, t)
            t_bd = t
            tv = [values(Wk, [HT[:, kt, tok(n)] for kt in range(2)], n, lambda n: VP[:, n, :], None, None, t_ones)
                  for n in range(4)]
            ts, last = [], []

            def merged(b, g, t, P1):
                k, bk, free = P1.take()
                ps = PS[:, bk, 0:256]
                cols = slice(b * 256, b * 256 + 256)
                t = PE(mms((ps, BD[:, g, :], CTX[:, g, cols], True, True)), free, t, t_bd)
                t = AC(lambda: A.mul(AO[:, g, cols], ps, 0.25), t, tt, t_p)
                P1.give(k, t)
                ts.append(t)

            def norm(*args):
                return heads_norm(CTX, RC, W["dsel"], *args)

            def then(P1, b, g, t):
                if last:
                    merged(*last.pop(), P1)
                last.append((b, g, t))
                if (b, g) == (1, 3):
                    merged(*last.pop(), P1)
            attention(QS, KS, 102, 0.5, lambda n: VP[:, n, :], CTX, PTR, None, None, None, t_m, tv, norm, then)
            for i in range(4):
                k, ps, free = bank()
                t = PE(mms(*sum_jobs(ps[:, 0:256], [(AO[:, g, tok(i)], Wo[:, g, :]) for g in range(4)])), free,
                       ts[4 * (i // 2):4 * (i // 2) + 4])
                t = add_to_x(ps[:, 0:256], i, 1, t)
                PB.give(k, t)
                x_done(i, t)
            return fence()

        if only[0] <= 7 <= only[1]:
            f = stage_7(f)

        def stage_8(f):
            n = WHERE["s8", "g5"][0]
            W = {name: AR[:, (10460 + at if at < n else at - n):][:, 0:cols]
                 for name, cols in PACK["s8"] for at in [WHERE["s8", name][0]]}
            t_w = ahead["s8"]
            s0 = SPAN["s8"][0]
            t_late = load(AR[:, 0:SPAN["s8"][1] - n], pack[:, s0 + n:s0 + SPAN["s8"][1]], f)
            ahead["s9"] = weights("s9", AR, 8000, f)
            hs = norm_rows(X, H, None)
            warm(ACT.Exp)
            t_ht = to_T(H, HT, hs)
            lg, t = logits8(mat(W["rw"], 2), W["rb"], t_ht, t_w)
            oh1, top, t1 = first_of_max(lg, t)
            l2, ex, R, den = sm(4, 8), sm(4, 8), sm(4, 8), sm(4)
            t = DV(lambda: V.tensor_scalar(l2, oh1, -3e38, None, ALU.mult), t1)
            t = DV(lambda: V.tensor_tensor(l2, l2, lg, ALU.add), t)
            oh2, _, t = first_of_max(l2, t)
            t = DV(lambda: V.tensor_tensor(oh2, oh2, oh1, ALU.add), t)
            t2 = DV(lambda: V.tensor_tensor(ex, lg, up8(top), ALU.subtract), t)
            t2 = AC(lambda: A.activation(ex, ex, ACT.Exp), t2)
            warm(ACT.Silu)
            t = DV(lambda: V.tensor_tensor(R, ex, oh2, ALU.mult), t2, t)
            t = DV(lambda: V.tensor_reduce(den, R, AX, ALU.add), t)
            t = DV(lambda: V.reciprocal(den, den), t)
            t = DV(lambda: V.tensor_tensor(R, R, up8(den), ALU.mult), t)
            RT = AR[0:8, 3840:4352]
            experts(W, 10, 8, RT, lambda t=t: rows8(R, RT, t), t_ht, 4352, False, t_late)
            return fence()

        def prepare_9():
            one = [PL(lambda: G.memset(VP0, 1.0))]
            rows = [PL(lambda: G.memset(view(CNf, 9216, 4096)[96:99], 0.0), PL.now())]
            rows.append(PL(lambda: G.memset(view(CNf, 9216, 4096)[96:97], ONES2), rows[0]))
            rows.append(PL(lambda: G.memset(view(CNf, 13312, 2048)[96:99], MINUS2), PL.now()))
            return {"VP0": one, "rows": rows}

        VP0 = view(CNf, 0, 32, 288)
        QS9 = view(CNf, 9216, 4096).bitcast(BF16).rearrange("p (h t) -> p h t", h=16)
        KSL0 = view(CNf, 13312, 2048).bitcast(BF16)
        t_set = prepare_9()
        if only[0] <= 8 <= only[1]:
            f = stage_8(f)

        def stage_9(f):
            W, t_w = ahead["s9"]
            KSL = [KSL0] + [view(AR, 2048 * k, 2048).bitcast(BF16) for k in range(3)]
            QS = QS9
            QP = view(AR, 6144, 1536).bitcast(BF16).rearrange("p (s m t) -> p s m t", s=3, m=2)
            parts3 = lambda at: view(AR, at, 768).bitcast(BF16).rearrange("p (s t) -> p s t", s=3)
            KS1 = Ring([parts3(6144 + 768 * k) for k in range(2)])
            o = 9813
            VX = view(AR, o, 560)
            VP1 = [CTf[:, 8192 * (n // 15) + 272 * (n % 15):8192 * (n // 15) + 272 * (n % 15) + 288] for n in range(30)]
            VP1 += [VX[:, 272 * n:272 * n + 288] for n in range(2)]
            o += 560
            PTR = Ring([view(AR, o + 1024 * k, 4, 256) for k in range(3)])
            KS0 = Ring([parts3(o + 768 * k) for k in range(4)])
            o += 3072
            RT = Ring([view(AR, o + 512 * k, 512) for k in range(2)])
            CXR = Ring([view(AR, o + 1024 + 256 * k, 256) for k in range(2)])
            o += 1536
            MM = view(AR, o, 256).bitcast(BF16).rearrange("p (a i r) -> p a i r", a=2, i=2)
            MI = view(AR, o + 256, 64).bitcast(I32)
            MB = view(AR, o + 320, 32).bitcast(BF16)
            IDB = view(AR, o + 352, 64).bitcast(BF16)
            assert o + 416 <= 15640
            Wq, Wk, Wv = mat(W["Wq"], 2), mat(W["Wk"], 2), mat(W["Wv"], 2)
            kd = nc.dram_tensor("k_parts", (3, 2, 256, KEYS), BF16, kind="Internal").ap()
            qd = nc.dram_tensor("q_parts", (3, 256, 512), BF16, kind="Internal").ap()
            md = nc.dram_tensor("mask_row", (2, KEYS), BF16, kind="Internal").ap()
            t_mi = load(MI.rearrange("p (b t) -> p b t", b=2), mask1.rearrange("b (p t) -> p b t", p=128), f)
            t_mb = DV(lambda: V.tensor_scalar(MB, MI, 0.0, -1e30, ALU.is_gt, ALU.mult), t_mi)
            t_md = load(md.rearrange("b (p t) -> p b t", p=128), MB.rearrange("p (b t) -> p b t", b=2), t_mb)
            t_idb = DV(lambda: V.tensor_copy(IDB, ident))
            t_init = [DV(lambda: V.memset(MM, 0.0))]
            t_init.append(DV(lambda: V.memset(MM[:, :, :, 96], 1.0), t_init[0]))
            t_init.append(t_set["VP0"])
            t_rows = list(t_set["rows"])

            t_kd, t_v = {}, {0: [], 1: []}

            def keys_steps(b, m, c, banks, slots, *deps):
                s0 = b * KEYS + c * 512
                sk, st, sf = slots.take()
                k, bk, free = banks.take()
                ps = PS[:, bk, :]
                t = PE(mms(*sum_jobs(ps, [(Wk[:, kt, tok(m)], CT[:, kt, s0:s0 + 512]) for kt in range(2)])), free, t_w)
                steps = split_steps(RT, ps, [st[:, s, :] for s in range(3)], W["bk"][:, m:m + 1], 1.0, t, sf, list(deps))
                banks.give(k, next(steps))
                yield
                tt = next(steps)
                t = load(kd[:, b, m * 128:m * 128 + 128, c * 512:c * 512 + 512].rearrange("s p t -> p s t"), st, tt)
                slots.give(sk, t)
                t_kd.setdefault((b, m), []).append(t)
                yield

            under_way = []

            def keys(*args):
                under_way.append(keys_steps(*args))
                next(under_way[-1])
                if len(under_way) > 1:
                    next(under_way.pop(0))

            def keys_end():
                while under_way:
                    next(under_way.pop(0))

            def vrow(b, n):
                return VP1[n] if b else VP0[:, n, :]

            def values_of(b, n, banks, *deps):
                s0 = b * KEYS + n * 128
                k, bk, free = banks.take()
                ps = PS[:, bk, 0:256]
                t = PE(mms(*sum_jobs(ps, [(CT[:, kt, s0:s0 + 128], Wv[:, kt, :]) for kt in range(2)])), free, t_w)
                ov = vrow(b, n)[:, 0:272].rearrange("p (h r) -> p h r", r=17)[:, :, 0:16]
                t = DV(lambda: V.tensor_tensor(ov, ps.rearrange("p (h r) -> p h r", r=16),
                                               W["bv"].rearrange("p (h r) -> p h r", r=16), ALU.add), t, list(deps))
                banks.give(k, t)
                t_v[b].append(t)

            hs = norm_rows(X, H, None)
            warm(ACT.Exp)
            keys(0, 0, 0, PB, KS0)
            keys(0, 0, 1, PB, KS0)
            keys_end()
            t_ht = to_T(H, HT, hs)
            tq = []
            for m in range(2):
                k, ps, free = bank()
                t = PE(mms(*sum_jobs(ps, [(Wq[:, kt, tok(m)], HT[:, kt, :]) for kt in range(2)])), free, t_ht)
                ta, tt = split(RT, ps, [QP[:, s, m, :] for s in range(3)], W["bq"][:, m:m + 1], 0.25, t)
                PB.give(k, ta)
                tq += tt
            t = [load(qd[s].rearrange("(m p) t -> p m t", p=128), QP[:, s], tq) for s in range(3)]
            t_qd = t
            t_qs = [load(QS[16 * r:16 * r + 16], qd[s].rearrange("(h d) t -> d h t", d=16), t)
                    for r, s in enumerate(COLS)]

            ksem = [ctx.enter_context(nc.semaphore(f"ks{k}")) for k in range(4)]
            kuse = [0, 0, 0, 0]
            t_ks = {}
            heads = [(b, h) for b in range(2) for h in range(16)]

            def fetch(n, *deps):
                b, h = heads[n]
                k = n % 4
                for s, lo, times in ((0, 0, 3), (1, 48, 2), (2, 80, 1)):
                    src = kd[s, b, 16 * h:16 * h + 16, :]
                    dst = KSL[k][lo:lo + 16 * times]
                    if times > 1:
                        src = src.unsqueeze(0).to_broadcast([times, 16, KEYS])
                    SP.append((flat([t_kd[b, h // 8], t_rows, list(deps)]), dst, src, ksem[k]))
                SP.append((flat([t_md, t_rows]), KSL[k][96:97], md[b:b + 1, :], ksem[k]))
                kuse[k] += 1
                t_ks[n] = (ksem[k], 16 * 4 * kuse[k])

            for c in range(8):
                if c > 1:
                    keys(0, 0, c, PB, KS0)
                if c in (2, 4, 6):
                    t_rows.append(PL(lambda k=c // 2 - 1: G.memset(view(AR, 2048 * k, 2048)[96:99], MINUS2), PL.now()))
                if c > 2:
                    values_of(0, 2 * c - 6, PB, t_init)
                    values_of(0, 2 * c - 5, PB, t_init)
            keys_end()
            fetch(0)
            fetch(1)

            MX, mxs = sm(2, 2, 8), sm(2, 2)
            P1 = Ring([0, 1])
            P1.free = [PB.free[0], PB.free[1]]
            PR = Ring([2, 3, 4, 5])
            PR.free = PB.free[2:6]
            ST = Ring([2, 4])
            CB = Ring([6, 7])
            t_red, t_aux, t_fin = {}, {}, {}
            mm_free, t_mm = [None, None], [None, None]

            def best(n, u):
                b, h = heads[n]
                i, c = u // 8, u % 8
                k, bk, free = P1.take()
                ps = PS[:, bk, :]
                t = PE(mms((ps, QS[0:97, h, tok(2 * b + i)], KSL[n % 4][0:97, c * 512:c * 512 + 512], True, True)),
                       free, t_ks[n], t_qs, t_rows)
                t = DV(lambda: V.tensor_reduce(MX[:, n % 2, i, c:c + 1], ps, AX, ALU.max), t, t_red.get((n - 2, "all")))
                P1.give(k, t)
                t_red.setdefault(n, []).append(t)

            def best_rows(n):
                a = n % 2
                m = mxs[:, a, :]
                t = DV(lambda: V.tensor_reduce(m, MX[:, a], AX, ALU.max), t_red[n])
                t_red[n, "all"] = t
                t = DV(lambda: V.tensor_copy(MM[:, a, :, 97], m), t, t_init, mm_free[a])
                t_mm[a] = DV(lambda: V.tensor_tensor(MM[:, a, :, 98], m, MM[:, a, :, 97], ALU.subtract), t)

            def turn_rows(n, ck):
                b, h = heads[n]
                a = n % 2
                t = t_mm[a]
                pb = PS[:, 6 + ck, 256:384].bitcast(BF16)
                def go():
                    TE.transpose(pb[:, 0:128], MM[:, a, 0, :], IDB)
                    return TE.transpose(pb[:, 128:256], MM[:, a, 1, :], IDB)
                t = PE(go, t, t_idb, t_fin.get(n - 2))
                mm_free[a] = t
                t = DV(lambda: V.tensor_copy(QS[96:99, h, b * 256:b * 256 + 256], pb[96:99, :]), t)
                t_aux[n] = t

            def close_head(n, cb, ck, t):
                C = PS[:, cb, 0:256]
                xk, cx, xf = CXR.take()
                t_fin[n] = AC(lambda: A.copy(cx, C), t, xf)
                return n, xk, cx, ck

            def finish_head(n, xk, cx, ck):
                b, h = heads[n]
                ps = PS[:, 6 + ck, 384:418].rearrange("p (i r) -> p i r", i=2)
                t = PE(mms(*[(ps[:, i, :], cx[:, tok(i)], W["sum17"], True, True) for i in range(2)]), t_fin[n],
                       t_aux.get(n + 2))
                CXR.give(xk, t)
                ri = sm(2)
                t = DV(lambda: V.reciprocal(ri, ps[:, :, 16]), t)
                for i in range(2):
                    x = X[:, 2 * b + i, 16 * h:16 * h + 16]
                    t = DV(lambda i=i, x=x: V.scalar_tensor_tensor(out=x, in0=ps[:, i, 0:16], scalar=ri[:, i:i + 1],
                                                                   in1=x, op0=ALU.mult, op1=ALU.add), t, hs)
                CB.give(ck, t)
                if h == 15:
                    x_done(2 * b, t)
                    x_done(2 * b + 1, t)

            def two_values(b, n, ck):
                jobs, ps = [], PS[:, 6 + ck, :]
                for y in range(2):
                    s0 = b * KEYS + (n + y) * 128
                    jobs += sum_jobs(ps[:, y * 256:y * 256 + 256],
                                     [(CT[:, kt, s0:s0 + 128], Wv[:, kt, :]) for kt in range(2)])
                t = PE(mms(*jobs), CB.free[ck])
                for y in range(2):
                    ov = vrow(b, n + y)[:, 0:272].rearrange("p (h r) -> p h r", r=17)[:, :, 0:16]
                    z = DV(lambda y=y, ov=ov: V.tensor_tensor(
                        ov, ps[:, y * 256:y * 256 + 256].rearrange("p (h r) -> p h r", r=16),
                        W["bv"].rearrange("p (h r) -> p h r", r=16), ALU.add), t, t_one)
                    t_v[b].append(z)
                CB.give(ck, z)

            def mix(n, s, kk, pt, t, cb, ck, cf):
                b, h = heads[n]
                jobs = [(PS[32 * y:32 * y + 32, cb, 0:256], vrow(b, 4 * s + y)[:, 17 * h:17 * h + 32], pt[:, y, :],
                         s == 0, s == 7) for y in range(4)]
                t = PE(mms(*jobs), t, cf, t_v[b])
                PTR.give(kk, t)
                return t

            u0 = 0
            for c in range(8):
                keys(0, 1, c, PR, KS0)
                for n in range(3):
                    if len(t_v[0]) < 32:
                        values_of(0, len(t_v[0]), PR, t_init)
                if c in (3, 5):
                    fetch(c // 2 + 1)
                if c > 2:
                    for _ in range(8 if c == 7 else 6):
                        best(u0 // 16, u0 % 16)
                        u0 += 1
            keys_end()
            assert u0 == 32 and len(t_v[0]) == 32
            over = PE.now()
            t_stage = KS0.free
            ST.free = [PR.free[0:2], PR.free[2:4]]
            t_one = [PL(lambda a=a: G.memset(a, 1.0), over, PL.now()) for a in (CTf[:, 0:4096], CTf[:, 8192:12288], VX)]
            best_rows(0)
            turn_rows(0, 0)
            CB.free = [t_aux[0], None]
            more_keys = [(1, m, c) for m in range(2) for c in range(8)]
            pend = []
            late = steps = None

            for n in range(32):
                b, h = heads[n]
                ck, cb, cf = CB.take()
                for s in range(8):
                    k, bk, free = ST.take()
                    jobs = [(PS[:, bk + y // 2, (y % 2) * 256:(y % 2) * 256 + 256],
                             KSL[n % 4][0:99, (4 * s + y) * 128:(4 * s + y) * 128 + 128],
                             QS[0:99, h, b * 256:b * 256 + 256], True, True) for y in range(4)]
                    t = PE(mms(*jobs), free, t_aux[n])
                    st = t
                    kk, pt, pf = PTR.take()
                    t = AC(lambda bk=bk, pt=pt: A.activation(
                        pt, PS[:, bk:bk + 2, :].rearrange("p a (c q) -> p (a c) q", c=2), ACT.Exp), t, pf, t_stage)
                    ST.give(k, t)
                    pend.append((n, s, kk, pt, t, cb, ck, cf))
                    if n + 2 < 32:
                        best(n + 2, 2 * s)
                    if s == 5 and more_keys:
                        side = Ring([7 - ck])
                        side.free = [CB.free[1 - ck]]
                        steps = keys_steps(*more_keys.pop(0), side, KS1, t_qd)
                        next(steps)
                        CB.give(1 - ck, side.free[0])
                    if s == 6 and n < 16:
                        two_values(1, 2 * n, 1 - ck)
                    if s == 6 and steps:
                        next(steps)
                        steps = None
                    if s == 0 and n + 1 < 32:
                        best_rows(n + 1)
                    if s == 3 and n + 1 < 32:
                        turn_rows(n + 1, 1 - ck)
                        if n == 0:
                            CB.give(1, t_aux[1])
                    if late and s == 4:
                        finish_head(*late)
                        late = None
                    if len(pend) > 2:
                        args = pend.pop(0)
                        t = mix(*args)
                        if args[1] == 7:
                            late = close_head(args[0], args[5], args[6], t)
                            if args[0] == 15:
                                ahead["s10"] = weights("s10", CNf, 0, t)
                    if n + 2 < 32:
                        best(n + 2, 2 * s + 1)
                if n + 4 < 32:
                    fetch(n + 4, st)
            while pend:
                args = pend.pop(0)
                t = mix(*args)
                if args[1] == 7:
                    if late:
                        finish_head(*late)
                    late = close_head(args[0], args[5], args[6], t)
            finish_head(*late)
            return fence()

        if only[0] <= 9 <= only[1]:
            f = stage_9(f)

        ER = Ring([view(CNf, 7808, 4096), view(CNf, 11904, 4096), view(AR, 11100, 4096), view(CNf, 0, 4096)])

        def load_expert(e, *deps):
            s0 = SPAN["s11e"][0] + e * 4096
            kk, w, wf = ER.take()
            return kk, w, load(w, pack[:, s0:s0 + 4096], wf, *deps)

        def stage_10(f):
            W, t_w = ahead["s10"]
            ahead["s11"] = weights("s11", AR, 0, f)
            ahead["experts"] = [load_expert(e, f) for e in range(3)]
            B0 = CTf
            RQ, RK = view(B0, 0, 2, 512), view(B0, 1024, 2, 512)
            VV, GG, OO = view(B0, 2048, 4, 512), view(B0, 4096, 4, 512), view(B0, 6144, 4, 512)
            AT = view(B0, 8192, 8, 512)
            OT = view(B0, 12288, 4, 512)
            tA, tB = view(B0, 14336, 512), view(B0, 14848, 512)
            hs = norm_rows(X, H, None)
            warm(ACT.Silu)
            t_ht = to_T(H, HT, hs)
            cos = W["cos"].unsqueeze(1).to_broadcast([128, 2, 256])
            sin = W["sin"].unsqueeze(1).to_broadcast([128, 2, 256])
            ts, td = [], None
            for (a, s, dst, sc) in (("Wq", "Wqs", RQ, 0.125), ("Wk", "Wks", RK, 1.0)):
                wa, ws = mat(W[a], 2), mat(W[s], 2)
                for m in range(2):
                    k1, p1, f1 = bank()
                    k2, p2, f2 = bank()
                    t1 = PE(mms(*sum_jobs(p1, [(wa[:, kt, tok(m)], HT[:, kt, :]) for kt in range(2)])), f1, t_ht, t_w)
                    t2 = PE(mms(*sum_jobs(p2, [(ws[:, kt, tok(m)], HT[:, kt, :]) for kt in range(2)])), f2)
                    v2 = lambda p: p.rearrange("p (b t) -> p b t", b=2)
                    t1 = DV(lambda p=p1: V.tensor_tensor(v2(tA), v2(p), cos, ALU.mult), t1, td)
                    PB.give(k1, t1)
                    t2 = DV(lambda p=p2: V.tensor_tensor(v2(tB), v2(p), sin, ALU.mult), t2, td)
                    PB.give(k2, t2)
                    t = DV(lambda: V.tensor_tensor(tA, tA, tB, ALU.add), t1, t2)
                    td = DV(lambda m=m, dst=dst, sc=sc: V.tensor_scalar(dst[:, m, :], tA, sc, None, ALU.mult), t)
                    ts.append(td)
            tv, tg = [], []
            wv, wg = mat(W["Wv"], 2), mat(W["Wg"], 2)
            for i in range(4):
                k, ps, free = bank()
                t = PE(mms(*sum_jobs(ps, [(HT[:, kt, tok(i)], wv[:, kt, :]) for kt in range(2)])), free)
                t = AC(lambda i=i, ps=ps: A.copy(VV[:, i, :], ps), t)
                PB.give(k, t)
                tv.append(t)
                k, ps, free = bank()
                t = PE(mms(*sum_jobs(ps, [(HT[:, kt, tok(i)], wg[:, kt, :]) for kt in range(2)])), free)
                t = AC(lambda i=i, ps=ps: A.activation(GG[:, i, :], ps, ACT.Silu), t)
                PB.give(k, t)
                tg.append(t)
            dec = W["decay"].rearrange("p (j h t) -> p j h t", j=2, h=4)
            ss, rr = sm(4, 4), sm(4, 4)
            t_at = {}
            for b in range(2):
                for h in range(4):
                    r = slice(64 * (h % 2), 64 * (h % 2) + 64)
                    k, ps, free = bank()
                    q = RQ[r, h // 2, b * 256:b * 256 + 256]
                    jobs = [(ps[:, j * 256:j * 256 + 256], RK[r, h // 2, tok(2 * b + j)], q, True, True)
                            for j in range(2)]
                    t = PE(mms(*jobs), free, ts)
                    t = DV(lambda b=b, h=h, ps=ps: V.tensor_tensor(
                        AT[:, 4 * b + h, :].rearrange("p (j t) -> p j t", j=2), ps.rearrange("p (j t) -> p j t", j=2),
                        dec[:, :, h, :], ALU.mult), t, t_w)
                    PB.give(k, t)
                    t_at[b, h] = t
            tn, t_oo, t_on = [], [], []
            warm(ACT.Sqrt)
            for i in range(4):
                b, l = i // 2, i % 2
                k, ps, free = bank()
                jobs = []
                for h in range(4):
                    pairs = [(AT[:, 4 * b + h, j * 256 + l * 128:j * 256 + l * 128 + 128],
                              VV[:, 2 * b + j, tok(h)]) for j in range(l + 1)]
                    jobs += sum_jobs(ps[:, tok(h)], pairs)
                t = PE(mms(*jobs), free, tv, [t_at[b, h] for h in range(4)])
                t = DV(lambda i=i, ps=ps: V.tensor_copy(OO[:, i, :], ps), t)
                PB.give(k, t)
                t_oo.append(t)
            t_gn = [DV(lambda i=i: V.tensor_tensor(
                GG[:, i, :].rearrange("p (h d) -> p h d", h=4), GG[:, i, :].rearrange("p (h d) -> p h d", h=4),
                W["gn"].unsqueeze(1).to_broadcast([128, 4, 128]), ALU.mult), tg[i]) for i in range(4)]
            for i in range(4):
                tq_before = AC.now()
                tq = []
                for h in range(4):
                    tq.append(AC(lambda i=i, h=h: A.activation((tA, tB)[i % 2][:, tok(h)], OO[:, i, tok(h)],
                                                               ACT.Square, accum_out=ss[:, i, h:h + 1]), t_oo[i],
                                 ts, tq_before))
                t2 = rsqrt(rr[:, i, :], ss[:, i, :], 1.0 / 128, 1e-5, tq)
                for h in range(4):
                    t = DV(lambda i=i, h=h: V.scalar_tensor_tensor(
                        out=OO[:, i, tok(h)], in0=OO[:, i, tok(h)], scalar=rr[:, i, h:h + 1], in1=GG[:, i, tok(h)],
                        op0=ALU.mult, op1=ALU.mult), t2, t_gn[i], tq)
                t_on.append(t)
            for i in range(4):
                k, ps, free = bank()
                def go(i=i, ps=ps):
                    for h in range(4):
                        z = TE.transpose(ps[:, tok(h)], OO[:, i, tok(h)], ident)
                    return z
                t = PE(go, free, t_on[i])
                t = DV(lambda i=i, ps=ps: V.tensor_copy(OT[:, :, tok(i)], ps.rearrange("p (h t) -> p h t", h=4)), t)
                PB.give(k, t)
                tn.append(t)
            wo = mat(W["Wo"], 4)
            for i in range(4):
                k, ps, free = bank()
                t = PE(mms(*sum_jobs(ps[:, 0:256], [(OT[:, h, tok(i)], wo[:, h, :]) for h in range(4)])), free, tn[i])
                t = add_to_x(ps[:, 0:256], i, 1, t)
                PB.give(k, t)
                x_done(i, t)
            return fence()

        if only[0] <= 10 <= only[1]:
            f = stage_10(f)

        def stage_11(f):
            W, t_w = ahead["s11"]
            expert_w = ahead["experts"] + [load_expert(3, f)]
            B0 = CTf
            X1, X2 = view(B0, 0, 4, 256), view(B0, 1024, 4, 256)
            QS, KS = (view(B0, 2048 + 4096 * k, 4096).bitcast(BF16).rearrange("p (h t) -> p h t", h=16)
                      for k in range(2))
            CTX = view(B0, 10240, 4, 512)
            PTR = Ring([view(B0, 12288 + 1024 * k, 4, 256) for k in range(3)] + [view(CNf, 4096, 4, 256)])
            RC = view(B0, 15360, 2, 512)
            o = SPAN["s11"][1]
            VP = view(AR, o, 4, 288)
            MM = view(AR, o + 1152, 512).bitcast(BF16).rearrange("p (a y r) -> p a y r", a=2, y=4)
            GT = AR[0:8, o + 1664:o + 2176]
            MB12 = view(AR, o + 2176, 8, 8)
            M1, M2 = MB12[:, 0:4, :], MB12[:, 4:8, :]
            ST3 = [view(AR, o + 2240 + 768 * m, 768).bitcast(BF16).rearrange("p (s t) -> p s t", s=3) for m in range(4)]
            RT = Ring([view(AR, o + 5312 + 512 * k, 512) for k in range(2)])
            IDB = view(AR, o + 6336, 64).bitcast(BF16)
            t_idb = DV(lambda: V.tensor_copy(IDB, ident))
            t_ones = [PL(lambda: G.memset(VP, 1.0))]
            t_rows = PL(lambda: G.memset(view(B0, 6144, 4096)[96:98], MINUS2), PL.now())
            t_mm = PL(lambda: G.memset(MM, 0.0), PL.now())
            pd = nc.dram_tensor("s_parts", (2, 3, 256, 512), BF16, kind="Internal").ap()
            x1 = norm_rows(X, X1, None)

            def affine(g_, b_):
                def post(dst, ps, kt, t):
                    return DV(lambda: V.tensor_scalar(dst, ps, W[g_][:, kt:kt + 1], W[b_][:, kt:kt + 1],
                                                      ALU.mult, ALU.add), t, t_w)
                return post
            hs = norm_rows(X1, H, x1)
            warm(ACT.Exp)
            t_ht = to_T(H, HT, hs, affine("g1", "b1n"))
            wq, wk, wv = mat(W["Wq"], 2), mat(W["Wk"], 2), mat(W["Wv"], 2)
            t_wr, begun, t_m = {}, [], []

            def end_split():
                m, z, st, steps = begun.pop(0)
                t_wr[m, z] = load(pd[z, :, 128 * m:128 * m + 128, :].rearrange("s p t -> p s t"), st, next(steps))
                if z == 1:
                    t_m.append([spread(pd[y], (QS, KS)[y], (COLS, ROWS)[y], m, t_wr[m, y]) for y in range(2)]
                               + [t_rows, t_mm])
            for m in range(2):
                for z, (w, bias, sc) in enumerate(((wq, "bq", 0.25), (wk, "bk", 1.0))):
                    k, ps, free = bank()
                    t = PE(mms(*sum_jobs(ps, [(w[:, kt, tok(m)], HT[:, kt, :]) for kt in range(2)])), free, t_ht, t_w)
                    st = ST3[2 * m + z]
                    steps = split_steps(RT, ps, [st[:, s, :] for s in range(3)], W[bias][:, m:m + 1], sc, t)
                    PB.give(k, next(steps))
                    begun.append((m, z, st, steps))
                    if len(begun) > 1:
                        end_split()
            end_split()
            tv = [values(wv, [HT[:, kt, tok(m)] for kt in range(2)], m, lambda m: VP[:, m, :], W["bv"], None, t_ones)
                  for m in range(4)]
            t_n = []

            def norm(*args):
                return heads_norm(CTX, RC, W["dsel"], *args)

            def then(P1, b, g, t):
                t_n.append(t)
            attention(QS, KS, 98, 1.0, lambda n: VP[:, n, :], CTX, PTR, MM, IDB, t_idb, t_m, tv, norm, then)
            warm(ACT.Sqrt)
            wo = mat(W["Wo"], 4)
            x2 = []
            for i in range(4):
                t0 = PL(lambda i=i: G.tensor_tensor(X1[:, i, :], X1[:, i, :], W["bo"], ALU.add), x1, t_ht)
                k, ps, free = bank()
                t = PE(mms(*sum_jobs(ps[:, 0:256], [(CTX[:, g, tok(i)], wo[:, g, :]) for g in range(4)])), free,
                       t_n[4 * (i // 2):4 * (i // 2) + 4])
                t = DV(lambda i=i, ps=ps: V.tensor_tensor(X2[:, i, :], ps[:, 0:256], X1[:, i, :], ALU.add), t, t0)
                PB.give(k, t)
                x2.append(t)
            hs = norm_rows(X2, H, x2)
            warm(ACT.Exp)
            for i in range(4):
                t = DV(lambda i=i: V.tensor_tensor(H[:, i, :], H[:, i, :], W["g2"], ALU.mult), hs[i])
                hs[i] = DV(lambda i=i: V.tensor_tensor(H[:, i, :], H[:, i, :], W["b2n"], ALU.add), t)
            t_ht = to_T(H, HT, hs)
            lg, t = logits8(mat(W["wr"], 2), None, t_ht)
            pr, mxl, den, l2 = sm(4, 8), sm(4), sm(4), sm(4, 8)
            t1 = DV(lambda: V.tensor_reduce(mxl, lg, AX, ALU.max), t)
            t1 = DV(lambda: V.tensor_tensor(pr, lg, up8(mxl), ALU.subtract), t1)
            t1 = AC(lambda: A.activation(pr, pr, ACT.Exp), t1)
            t1 = DV(lambda: V.tensor_reduce(den, pr, AX, ALU.add), t1)
            t1 = DV(lambda: V.reciprocal(den, den), t1)
            t_p = DV(lambda: V.tensor_tensor(pr, pr, up8(den), ALU.mult), t1)
            oh1, _, t1 = first_of_max(pr, t_p)
            t = DV(lambda: V.tensor_scalar(l2, oh1, -3e38, None, ALU.mult), t1)
            t = DV(lambda: V.tensor_tensor(l2, l2, lg, ALU.add), t)
            oh2, _, t = first_of_max(l2, t)
            t1 = DV(lambda: V.tensor_copy(M1, oh1), t1)
            t2 = DV(lambda: V.tensor_copy(M2, oh2), t)
            k, ps, free = bank()
            jobs = []
            blocks = ps[:, 0:64].rearrange("p (a b) -> p a b", b=8)
            jobs.append((blocks, cst["triu"], MB12, True, False))
            for n in range(7):
                first = n + 1 if n < 3 else 4 if n == 3 else n + 1
                row = MB12[:, n:n + 1, :].to_broadcast([128, 8 - first, 8])
                jobs.append((blocks[:, first:8, :], cst["ones"], row, False, n == 6))
            t = PE(mms(*jobs), free, t1, t2)
            k1_, k2_ = sm(4, 8), sm(4, 8)
            v8 = lambda p: p.rearrange("p (a b) -> p a b", b=8)
            ta = DV(lambda ps=ps: V.scalar_tensor_tensor(out=k1_, in0=v8(ps[:, 0:32]), scalar=128.5, in1=oh1,
                                                         op0=ALU.is_lt, op1=ALU.mult), t)
            tb = DV(lambda ps=ps: V.scalar_tensor_tensor(out=k2_, in0=v8(ps[:, 32:64]), scalar=128.5, in1=oh2,
                                                         op0=ALU.is_lt, op1=ALU.mult), t)
            LO, l2_ = sm(4, 8), sm(4, 8)
            tc = DV(lambda ps=ps: V.tensor_tensor(LO, v8(ps[:, 0:32]), k1_, ALU.mult), ta)
            td = DV(lambda ps=ps: V.tensor_tensor(l2_, v8(ps[:, 32:64]), k2_, ALU.mult), tb)
            PB.give(k, [tc, td])
            tc = DV(lambda: V.tensor_tensor(LO, LO, l2_, ALU.add), tc, td)
            t_lo = DV(lambda: V.tensor_scalar(LO, LO, -1.0, None, ALU.add), tc)
            t = DV(lambda: V.tensor_tensor(k1_, k1_, k2_, ALU.add), ta, tb, t_lo)
            t = DV(lambda: V.tensor_tensor(k1_, k1_, pr, ALU.mult), t)
            dn = sm(4)
            t = DV(lambda: V.tensor_reduce(dn, k1_, AX, ALU.add), t)
            t = DV(lambda: V.tensor_scalar(dn, dn, float(np.finfo(np.float32).eps), None, ALU.max), t)
            t = DV(lambda: V.reciprocal(dn, dn), t)
            GG = sm(4, 8)
            t_g = DV(lambda: V.tensor_tensor(GG, k1_, up8(dn), ALU.mult), t)
            t = rows8(GG, GT, t_g)
            acc = [PS[:, 6 + i // 2, (i % 2) * 256:(i % 2) * 256 + 256] for i in range(4)]
            PE(mms(*[(acc[i], GT[:, tok(i)], W["b2"][0:8, :], i % 2 == 0, False) for i in range(4)]), t)
            DS = [view(B0, 2048 + 512 * k, 4, 128) for k in range(4)]
            BT = [view(B0, 4096 + 256 * k, 2, 128) for k in range(2)]
            GDT = [view(B0, 4608 + 512 * k, 512) for k in range(2)]
            HH = [view(B0, 5632 + 1024 * k, 8, 128) for k in range(2)]
            YY = [view(B0, 7680 + 256 * k, 256) for k in range(2)]
            ds_free, bt_free, gd_free, hh_free, yy_free = ([None, None] for _ in range(5))
            att_done = PE.now()
            t_bt, t_gd, t_h, t_y = {}, {}, {}, {}

            def dispatch(e):
                p = e % 2
                D, GD = DS[p], DS[2 + p]
                td, tg = [], []
                for i in range(4):
                    td.append(DV(lambda i=i: V.tensor_scalar(D[:, i, :], W["iota"], LO[:, i, e:e + 1], None,
                                                             ALU.is_equal), t_lo, ds_free[p], att_done))
                    tg.append(DV(lambda i=i: V.tensor_scalar(GD[:, i, :], W["iota"], LO[:, i, e:e + 1],
                                                             GG[:, i, e:e + 1], ALU.is_equal, ALU.mult), t_g))
                k, ps, free = bank()
                jobs = []
                for kt in range(2):
                    jobs += sum_jobs(ps[:, tok(kt)], [(H[:, i, tok(kt)], D[:, i, :]) for i in range(4)])
                t = PE(mms(*jobs), free, td, hs)
                t = AC(lambda ps=ps: A.copy(BT[p], ps[:, 0:256].rearrange("p (k s) -> p k s", k=2)), t, bt_free[p],
                       att_done)
                PB.give(k, t)
                t_bt[e] = t
                k, ps, free = bank()
                def go(ps=ps):
                    for i in range(4):
                        l = TE.transpose(ps[:, tok(i)], GD[:, i, :], ident)
                    return l
                t = PE(go, free, tg)
                ds_free[p] = t
                t = DV(lambda ps=ps: V.tensor_copy(GDT[p], ps), t, gd_free[p])
                PB.give(k, t)
                t_gd[e] = t

            def hidden(e):
                p = e % 2
                w1 = mat(expert_w[e][1][:, 0:2048], 2)
                ts = []
                for q in range(2):
                    k, ps, free = bank()
                    jobs = []
                    for m in range(4):
                        jobs += sum_jobs(ps[:, tok(m)], [(w1[:, kt, tok(4 * q + m)], BT[p][:, kt, :]) for kt in range(2)])
                    t = PE(mms(*jobs), free, t_bt[e], expert_w[e][2])
                    for m in range(4):
                        f_ = 4 * q + m
                        c = W["b1"][:, e * 8 + f_:e * 8 + f_ + 1]
                        if q:
                            t2 = AC(lambda c=c, ps=ps, m=m, f_=f_: A.activation(HH[p][:, f_, :], ps[:, tok(m)], ACT.Relu,
                                                                                bias=c), t, hh_free[p])
                        else:
                            t2 = DV(lambda c=c, ps=ps, m=m, f_=f_: V.tensor_scalar(HH[p][:, f_, :], ps[:, tok(m)], c, 0.0,
                                                                                   ALU.add, ALU.max), t, hh_free[p])
                        ts.append(t2)
                    PB.give(k, t2)
                bt_free[p] = t
                t_h[e] = ts

            def result(e):
                p = e % 2
                w2 = mat(expert_w[e][1][:, 2048:4096], 8)
                k, ps, free = bank()
                t = PE(mms(*sum_jobs(ps[:, 0:256], [(HH[p][:, m, :], w2[:, m, :]) for m in range(8)])), free, t_h[e])
                hh_free[p] = t
                ER.give(expert_w[e][0], t)
                if e + 4 < 8:
                    expert_w.append(load_expert(e + 4))
                t = AC(lambda ps=ps: A.copy(YY[p], ps[:, 0:256]), t, yy_free[p])
                PB.give(k, t)
                t_y[e] = t

            def combine(e):
                p = e % 2
                t = PE(mms(*[(acc[i], GDT[p][:, tok(i)], YY[p], False, e == 7) for i in range(4)]), t_gd[e], t_y[e])
                gd_free[p] = yy_free[p] = t
                return t

            dispatch(0)
            for e in range(8):
                hidden(e)
                if e:
                    combine(e - 1)
                if e + 1 < 8:
                    dispatch(e + 1)
                result(e)
            t = combine(7)
            for q in range(2):
                xv, x2v = (a[:, 2 * q:2 * q + 2, :].rearrange("p a b -> p (a b)") for a in (X, X2))
                tt = DV(lambda q=q, x2v=x2v: V.scalar_tensor_tensor(out=x2v, in0=PS[:, 6 + q, :], scalar=1.0 - 0.2,
                                                                    in1=x2v, op0=ALU.mult, op1=ALU.add), t)
                DV(lambda xv=xv, x2v=x2v: V.tensor_tensor(xv, xv, x2v, ALU.add), tt)
            return fence()

        if only[0] <= 11 <= only[1]:
            f = stage_11(f)

        s_out = ctx.enter_context(nc.semaphore("s_out"))
        block = ctx.enter_context(nc.Block())

        @block.sync
        def _(eng):
            for deps, dst, src, s in SP:
                for ds, v in deps:
                    eng.wait_ge(ds, v)
                eng.dma_start(dst, src).then_inc(s, 16)
            for ds, v in f:
                eng.wait_ge(ds, v)
            eng.dma_start(out.rearrange("b (i p) d -> p (b i) d", p=128), X[:]).then_inc(s_out, 16)
            eng.wait_ge(s_out, 16)

        @block.tensor
        def _(eng):
            PE.emit(eng)

        @block.vector
        def _(eng):
            DV.emit(eng)

        @block.scalar
        def _(eng):
            AC.emit(eng)

        @block.gpsimd
        def _(eng):
            PL.emit(eng)


def _rows_to_partitions(w):
    w = np.asarray(w)
    k = w.shape[0] // 128
    return np.ascontiguousarray(w.reshape(k, 128, -1).transpose(1, 0, 2)).reshape(128, -1)


def _col(v):
    return np.ascontiguousarray(np.asarray(v).reshape(-1, 128).T)


def _row(v, times=1):
    v = np.tile(np.asarray(v), times)
    return np.broadcast_to(v[None, :], (128, v.size))


def _pad_out(w):
    w = np.asarray(w)
    o = np.zeros((w.shape[0], 16, 32), np.float32)
    o[:, :, :16] = w.reshape(w.shape[0], 16, 16)
    return o.reshape(w.shape[0], 512)


def _pad_in(w):
    w = np.asarray(w)
    o = np.zeros((16, 32, w.shape[1]), np.float32)
    o[:, :16] = w.reshape(16, 16, w.shape[1])
    return _rows_to_partitions(o.reshape(512, w.shape[1]))


def _constants():
    c = {}
    c["ident"] = np.eye(128, dtype=np.float32)
    c["triu"] = np.triu(np.ones((128, 128), np.float32))
    c["iota8"] = _row(np.arange(8, 0, -1).astype(np.float32), 4)
    c["iota"] = _row(np.arange(128).astype(np.float32))
    c["ones"] = np.ones((128, 128), np.float32)
    c["bd16"] = np.kron(np.eye(8), np.ones((16, 16))).astype(np.float32)
    c["bd32"] = np.kron(np.eye(4), np.ones((32, 32))).astype(np.float32)
    ds = np.zeros((128, 128), np.float32)
    for j in range(4):
        ds[32 * j + 16, 32 * j:32 * j + 32] = 1.0
    c["dsel"] = ds
    p = np.arange(128)
    c["hsel"] = np.concatenate([((p // 16)[:, None] + 8 * m == np.arange(16)[None, :]) for m in range(2)],
                               axis=1).astype(np.float32)
    p = p % 32
    c["sum17"] = (p[:, None] == np.arange(17)[None, :]).astype(np.float32)
    esel = np.zeros((128, 8, 128), np.float32)
    for e in range(8):
        esel[e, e, :] = 1.0
    c["esel"] = esel.reshape(128, 1024)
    inv = (1.0 / np.float32(10000.0) ** (np.arange(0, 64, 2, dtype=np.float32) / np.float32(64))).astype(np.float32)
    ang = (np.arange(256, dtype=np.float32)[None, :] * inv[:, None]).astype(np.float32)
    cos, sin = np.cos(ang).astype(np.float32), np.sin(ang).astype(np.float32)
    c["cos"] = np.concatenate([cos, cos, cos, cos])
    c["sin"] = np.concatenate([-sin, sin, -sin, sin])
    gam = (1.0 - np.exp2(-5.0 - np.arange(4, dtype=np.float32))).astype(np.float32)
    d = np.arange(256)[None, :] - np.arange(256)[:, None]
    dec = np.where(d[None] >= 0, gam[:, None, None].astype(np.float64) ** np.maximum(d, 0)[None], 0.0)
    c["decay"] = np.ascontiguousarray(dec.reshape(4, 2, 128, 256).transpose(2, 1, 0, 3)).reshape(128, 2048).astype(np.float32)
    return c


def _pack(a):
    R = _rows_to_partitions
    c = _constants()
    g = {}

    def put(stage, **kw):
        for k, v in kw.items():
            g[stage, k] = v

    L = "L0_xattn_"
    put("s0", Wq=R(a[L + "Wq"]), Wk=R(a[L + "Wk"].T), Wv=R(a[L + "Wv"]), Wo=R(a[L + "Wo"]), bq=_col(a[L + "bq"]),
        bk=_col(a[L + "bk"]), bv=_col(a[L + "bv"]), bo=_row(a[L + "bo"]))
    L = "L0_attn_"
    put("s1", qkv=R(a[L + "qkv_w"].T), proj=R(a[L + "proj_w"].T), conv1=R(a[L + "conv1_w"].T),
        conv2=R(a[L + "conv2_w"].T), s1=_col(a[L + "scale1"]), s2=_col(a[L + "scale2"]), gamma=_row(a[L + "gamma"]),
        pb=_row(a[L + "proj_b"]), c1b=_col(a[L + "conv1_b"]), c2b=_row(a[L + "conv2_b"]))
    L = "L0_ffn_"
    put("s2", w1=R(a[L + "w1_w"].T), w2=R(a[L + "w2_w"].T), w3=R(a[L + "w3_w"].T), w1s=_col(a[L + "w1_s"]),
        w2s=_col(a[L + "w2_s"]), h1s=_col(a[L + "h1_s"]), h2s=_col(a[L + "h2_s"]), w3s=_row(a[L + "w3_s"]))
    for l, n in enumerate(("h1_w", "h2_w")):
        w = a[L + n].T
        for m in range(8):
            g["s2h", f"h{8 * l + m}"] = R(w[:, m * 128:m * 128 + 128])
    for st, L in (("s3", "L1_xattn_"), ("s6", "L2_xattn_")):
        put(st, Wq=R(a[L + "Wq"].T), Wk=R(a[L + "Wk"]), Wv=R(a[L + "Wv"].T), bq=_col(a[L + "bq"]),
            bk=_col(a[L + "bk"]), bv=_row(a[L + "bv"]))
    L = "L1_attn_"
    put("s4", Wq=R(a[L + "Wq"].T), Wk=R(a[L + "Wk"].T), Wv=R(a[L + "Wv"].T),
        gamma=np.broadcast_to(a[L + "gamma"].reshape(1, 1), (128, 1)))
    L = "L1_ffn_"
    put("s5", gate=R(a[L + "gate_w"].T))
    for e in range(8):
        put("s5", **{f"g{e}": R(a[L + "w_gate"][e].T), f"u{e}": R(a[L + "w_up"][e].T), f"d{e}": a[L + "w_down"][e].T})
    L = "L2_attn_"
    put("s7", Wkp=R(_pad_out(a[L + "W_k"].T)), Wk=R(a[L + "W_k"].T), Wvp=R(_pad_out(a[L + "W_v"].T)),
        Wo=_pad_in(a[L + "W_o"].T))
    L = "L2_ffn_"
    put("s8", rw=R(a[L + "router_w"]), rb=_row(a[L + "router_b"], 4))
    for e in range(10):
        k, n = ("routed", e) if e < 8 else ("shared", e - 8)
        put("s8", **{f"g{e}": R(a[f"{L}{k}_w1"][n]), f"u{e}": R(a[f"{L}{k}_w3"][n]), f"d{e}": a[f"{L}{k}_w2"][n]})
    L = "L3_xattn_"
    put("s9", Wq=R(a[L + "q_w"].T), Wk=R(a[L + "k_w"].T), Wv=R(a[L + "v_w"].T), bq=_col(a[L + "q_b"]),
        bk=_col(a[L + "k_b"]), bv=_row(a[L + "v_b"]))
    L = "L3_attn_"

    def swap(w):
        return np.ascontiguousarray(w.reshape(4, 2, 32, 256)[:, ::-1]).reshape(256, 256)
    put("s10", Wq=R(a[L + "Wq"].T), Wqs=R(swap(a[L + "Wq"]).T), Wk=R(a[L + "Wk"].T), Wks=R(swap(a[L + "Wk"]).T),
        Wv=R(a[L + "Wv"].T), Wg=R(a[L + "Wg"].T), Wo=R(a[L + "Wo"].T), gn=_row(a[L + "gnorm_w"]))
    L = "L3_ffn_"
    b2 = np.zeros((128, 256), np.float32)
    b2[:8] = a[L + "b2"]
    put("s11", Wq=R(a[L + "wq"]), Wk=R(a[L + "wk"]), Wv=R(a[L + "wv"]), Wo=_pad_in(a[L + "wo"]),
        bq=_col(a[L + "bq"]), bk=_col(a[L + "bk"]), bv=_row(a[L + "bv"]), bo=_row(a[L + "bo"]),
        g1=_col(a[L + "ln1_g"]), b1n=_col(a[L + "ln1_b"]), g2=_row(a[L + "ln2_g"]), b2n=_row(a[L + "ln2_b"]),
        wr=R(a[L + "wr"]), b1=_col(a[L + "b1"].reshape(-1)), b2=b2)
    for e in range(8):
        put("s11e", **{f"w1_{e}": R(a[L + "w1"][e]), f"w2_{e}": R(a[L + "w2"][e])})
    out = np.empty((128, TOTAL), np.float32)
    for stage, entries in PACK.items():
        for name, cols in entries:
            o, _ = WHERE[stage, name]
            v = g[stage, name] if (stage, name) in g else c[name]
            s = SPAN[stage][0] + o
            assert v.shape == (128, cols), (stage, name, v.shape, cols)
            out[:, s:s + cols] = v
    return out


def build(nc, arrays, only=(0, 99)):
    args = [nc.dram_tensor(n, a.shape, mybir.dt.from_np(a.dtype), kind="ExternalInput").ap()
            for n, a in arrays.items()]
    out = nc.dram_tensor("out_dram", (2, 256, 256), F32, kind="ExternalOutput").ap()
    perceiver(nc, *args, out, only=only)


def lay_out(inputs):
    a = {k: np.asarray(v) for k, v in inputs.items()}
    ctxt = a["ctx_1024"].reshape(8192, 256)
    return {
        "pack": _pack(a),
        "x_in": np.ascontiguousarray(a["x"]),
        "ctx_n": np.ascontiguousarray(ctxt.reshape(64, 128, 256).transpose(1, 0, 2)),
        "ctx_t": np.ascontiguousarray(ctxt.reshape(8192, 2, 128).transpose(2, 1, 0)),
        "mask0": np.ascontiguousarray(a["mask_BxS2_bk0"]).view(np.int32),
        "mask1": np.ascontiguousarray(a["mask_BxS2_ik0"]),
    }


def kernel(**inputs):
    import concourse.bacc as _bacc
    from concourse.bass_utils import run_bass_kernel_spmd as _run

    nc = _bacc.Bacc("TRN2", target_bir_lowering=False, num_devices=1)
    arrays = lay_out(inputs)
    build(nc, arrays)
    r = _run(nc, [arrays], core_ids=[0])
    return r.results[0]["out_dram"]
```
